# Optimizing a Trainium2 kernel written in Bass

```python
import numpy as np
import jax
import jax.numpy as jnp

def _softmax(x, axis=-1):
    return jax.nn.softmax(x, axis=axis)

def _gelu(x):
    return jax.nn.gelu(x, approximate=True)

def _silu(x):
    return jax.nn.silu(x)

def _sigmoid(x):
    return jax.nn.sigmoid(x)

def _layernorm(x, axis=-1, eps=1e-05):
    m = jnp.mean(x, axis=axis, keepdims=True)
    v = jnp.var(x, axis=axis, keepdims=True)
    return (x - m) / jnp.sqrt(v + eps)

def _scatter_add(tgt, idx, src, axis=0):
    return tgt.at[idx].add(src)

def _segment_sum(src, seg, n):
    return jax.ops.segment_sum(src, seg, n)
kernel_name = 'mk_flamingo_gated_d4_seqx_r8_ca946e'

def setup_inputs(seed: int=0):
    np.random.seed(seed)
    _w = jnp.asarray

    def _rec_inputs():
        import jax
        import jax.numpy as jnp
        _rk = jax.random.key(seed)
        x = -0.0002928 + 1 * jax.random.normal(jax.random.fold_in(_rk, 1), (32, 56, 128), jnp.float32)
        _lenS = 56 - jax.random.randint(jax.random.fold_in(_rk, 7), (32,), 0, max(1, 56 // 4) + 1, jnp.int32)
        _lenS2 = 1500 - jax.random.randint(jax.random.fold_in(_rk, 8), (32,), 0, max(1, 1500 // 4) + 1, jnp.int32)
        _ctx_768P = jax.random.normal(jax.random.fold_in(_rk, 11), (32, 16, 96), jnp.float32)
        _ctx_768c = jax.random.dirichlet(jax.random.fold_in(_rk, 511), 0.3 * jnp.ones((16,), jnp.float32), (32, 1500))
        _ctx_768t = jnp.einsum('bsk,bkd->bsd', _ctx_768c, _ctx_768P)
        _ctx_768t = _ctx_768t * jax.lax.rsqrt(jnp.mean(jnp.square(_ctx_768t)) + 1e-12) * 0.953939
        ctx_768 = 2.09791e-05 + 1.00001 * (_ctx_768t + 0.3 * jax.random.normal(jax.random.fold_in(_rk, 611), (32, 1500, 96), jnp.float32))
        _g = jax.random.normal(jax.random.fold_in(_rk, 9001), (2, 4), jnp.float32)
        _g = jnp.sign(_g) * jnp.maximum(jnp.abs(_g), 1.0) + (_g == 0) * 1.0
        g_xattn = _g[0]
        g_ffn = _g[1]
        return (x, ctx_768, g_xattn, g_ffn)
    x, ctx_768, g_xattn, g_ffn = _rec_inputs()

    def _L0_xattn_setup():
        import jax, jax.numpy as jnp
        import numpy as np
        QUERY_DIM, KV_DIM, EMBED_DIM, NUM_HEADS = (128, 96, 128, 16)
        HEAD_DIM = EMBED_DIM // NUM_HEADS
        SCALE = HEAD_DIM ** (-0.5)
        LN_EPS = 1e-05

        def _l2norm(x, eps=1e-12):
            n = jnp.sqrt(jnp.sum(x * x, axis=-1, keepdims=True))
            return x / jnp.maximum(n, eps)
        key = jax.random.key(seed)
        ks = jax.random.split(key, 12)
        B, Nq, Nk = (2, 256, 256)
        s = lambda d: 1.0 / np.sqrt(d)
        return {'query': jax.random.normal(ks[0], (B, Nq, QUERY_DIM), jnp.float32), 'key': jax.random.normal(ks[1], (B, Nk, KV_DIM), jnp.float32), 'value': jax.random.normal(ks[2], (B, Nk, KV_DIM), jnp.float32), 'Wq': jax.random.normal(ks[3], (QUERY_DIM, EMBED_DIM), jnp.float32) * s(QUERY_DIM), 'bq': jnp.zeros((EMBED_DIM,), jnp.float32), 'Wk': jax.random.normal(ks[4], (KV_DIM, EMBED_DIM), jnp.float32) * s(KV_DIM), 'bk': jnp.zeros((EMBED_DIM,), jnp.float32), 'Wv': jax.random.normal(ks[5], (KV_DIM, EMBED_DIM), jnp.float32) * s(KV_DIM), 'bv': jnp.zeros((EMBED_DIM,), jnp.float32), 'Wo': jax.random.normal(ks[6], (EMBED_DIM, EMBED_DIM), jnp.float32) * s(EMBED_DIM), 'bo': jnp.zeros((EMBED_DIM,), jnp.float32), 'ln_gamma': jnp.ones((EMBED_DIM,), jnp.float32), 'ln_beta': jnp.zeros((EMBED_DIM,), jnp.float32)}
    _L0_xattn_all = _L0_xattn_setup()
    _L0_xattn_in = {k: v for k, v in _L0_xattn_all.items() if k in ('Wq', 'bq', 'Wk', 'bk', 'Wv', 'bv', 'Wo', 'bo', 'ln_gamma', 'ln_beta')}
    del _L0_xattn_all

    def _L0_ffn_setup():
        import jax, jax.numpy as jnp
        import numpy as np
        D = 128
        H = 512
        E = 64
        K = 3
        B, S = (2, 256)
        C = 64
        key = jax.random.key(seed)
        ks = jax.random.split(key, 6)
        s = 0.02
        return {'x': jax.random.normal(ks[0], (B, S, D), jnp.float32), 'gate_w': jax.random.normal(ks[1], (D, E), jnp.float32) * s, 'gate_b': jnp.zeros((E,), jnp.float32), 'w1': jax.random.normal(ks[2], (E, D, H), jnp.float32) * s, 'b1': jnp.zeros((E, H), jnp.float32), 'w2': jax.random.normal(ks[3], (E, H, D), jnp.float32) * s, 'b2': jnp.zeros((E, D), jnp.float32)}
    _L0_ffn_all = _L0_ffn_setup()
    _L0_ffn_in = {k: v for k, v in _L0_ffn_all.items() if k in ('gate_w', 'gate_b', 'w1', 'b1', 'w2', 'b2')}
    del _L0_ffn_all

    def _L1_xattn_setup():
        import jax, jax.numpy as jnp
        import numpy as np
        HEADS = 16
        DIM_HEAD = 64
        key = jax.random.key(seed)
        ks = jax.random.split(key, 7)
        B, Nq, Dq = (4, 256, 128)
        Nk, Dc = (128, 96)
        inner = HEADS * DIM_HEAD
        sq = 1.0 / np.sqrt(Dq)
        sc = 1.0 / np.sqrt(Dc)
        si = 1.0 / np.sqrt(inner)
        return {'x': jax.random.normal(ks[0], (B, Nq, Dq), dtype=jnp.float32), 'context': jax.random.normal(ks[1], (B, Nk, Dc), dtype=jnp.float32), 'Wq': jax.random.normal(ks[2], (Dq, inner), dtype=jnp.float32) * sq, 'Wk': jax.random.normal(ks[3], (Dc, inner), dtype=jnp.float32) * sc, 'Wv': jax.random.normal(ks[4], (Dc, inner), dtype=jnp.float32) * sc, 'Wo': jax.random.normal(ks[5], (inner, Dq), dtype=jnp.float32) * si, 'bo': jax.random.normal(ks[6], (Dq,), dtype=jnp.float32) * 0.01}
    _L1_xattn_all = _L1_xattn_setup()
    _L1_xattn_in = {k: v for k, v in _L1_xattn_all.items() if k in ('Wq', 'Wk', 'Wv', 'Wo', 'bo')}
    del _L1_xattn_all

    def _L1_ffn_setup():
        import jax, jax.numpy as jnp
        import numpy as np
        HIDDEN = 128
        N_ROUTED = 16
        N_SHARED = 2
        TOP_K = 2
        MID_R = HIDDEN // 4
        MID_S = HIDDEN // 2
        key = jax.random.key(seed)
        ks = jax.random.split(key, 8)
        s = 0.02
        return {'x': jax.random.normal(ks[0], (2, 128, HIDDEN), dtype=jnp.float32), 'router_w': jax.random.normal(ks[1], (HIDDEN, N_ROUTED), dtype=jnp.float32) * s, 'wg_r': jax.random.normal(ks[2], (N_ROUTED, HIDDEN, MID_R), dtype=jnp.float32) * s, 'wu_r': jax.random.normal(ks[3], (N_ROUTED, HIDDEN, MID_R), dtype=jnp.float32) * s, 'wd_r': jax.random.normal(ks[4], (N_ROUTED, MID_R, HIDDEN), dtype=jnp.float32) * s, 'wg_s': jax.random.normal(ks[5], (N_SHARED, HIDDEN, MID_S), dtype=jnp.float32) * s, 'wu_s': jax.random.normal(ks[6], (N_SHARED, HIDDEN, MID_S), dtype=jnp.float32) * s, 'wd_s': jax.random.normal(ks[7], (N_SHARED, MID_S, HIDDEN), dtype=jnp.float32) * s}
    _L1_ffn_all = _L1_ffn_setup()
    _L1_ffn_in = {k: v for k, v in _L1_ffn_all.items() if k in ('router_w', 'wg_r', 'wu_r', 'wd_r', 'wg_s', 'wu_s', 'wd_s')}
    del _L1_ffn_all

    def _L2_xattn_setup():
        import jax, jax.numpy as jnp
        import numpy as np
        import math
        E = 128
        EV = 128
        FFN = 512
        DINO = 96
        B, S, P = (64, 64, 32)

        def bitnet_linear(x, W, b):
            w_scale = jnp.maximum(jnp.mean(jnp.abs(W)), 1e-05)
            qW = jnp.sign(W) * (jnp.abs(W) > 0.5 * w_scale).astype(W.dtype)
            i_scale = jnp.maximum(jnp.max(jnp.abs(x)), 1e-08) / 127.0
            qx = jnp.clip(jnp.round(x / i_scale), -128.0, 127.0)
            out = jnp.einsum('...i,oi->...o', qx, qW) * (w_scale * i_scale)
            return out + b
        key = jax.random.key(seed)
        ks = iter(jax.random.split(key, 32))

        def lin_w(fin, fout):
            return jax.random.normal(next(ks), (fout, fin), jnp.float32) * math.sqrt(2.0 / fin)
        return {'text_embeddings': jax.random.normal(next(ks), (B, S, E), jnp.float32), 'dinov2_features': jax.random.normal(next(ks), (B, P, DINO), jnp.float32), 'W_d2v': lin_w(DINO, EV), 'b_d2v': jnp.zeros((EV,), jnp.float32), 'W_img': lin_w(EV, E), 'b_img': jnp.zeros((E,), jnp.float32), 'W_txt': lin_w(E, E), 'b_txt': jnp.zeros((E,), jnp.float32), 'W_att0': lin_w(E, E // 2), 'b_att0': jnp.zeros((E // 2,), jnp.float32), 'W_att1': lin_w(E, E // 2), 'b_att1': jnp.zeros((E // 2,), jnp.float32), 'W_f1': lin_w(2 * E, FFN), 'b_f1': jnp.zeros((FFN,), jnp.float32), 'W_f2': lin_w(FFN, E), 'b_f2': jnp.zeros((E,), jnp.float32)}
    _L2_xattn_all = _L2_xattn_setup()
    _L2_xattn_in = {k: v for k, v in _L2_xattn_all.items() if k in ('W_d2v', 'b_d2v', 'W_img', 'b_img', 'W_txt', 'b_txt', 'W_att0', 'b_att0', 'W_att1', 'b_att1', 'W_f1', 'b_f1', 'W_f2', 'b_f2')}
    del _L2_xattn_all

    def _L2_ffn_setup():
        import jax, jax.numpy as jnp
        import numpy as np
        E = 8
        K = 2
        D = 128
        F = 128
        B, S = (2, 256)
        key = jax.random.key(seed)
        ks = jax.random.split(key, 8)
        sc = 1.0 / np.sqrt(D)
        scf = 1.0 / np.sqrt(F)
        return {'x': jax.random.normal(ks[0], (B, S, D), dtype=jnp.float32), 'gate_w': jax.random.normal(ks[1], (D, E), dtype=jnp.float32) * sc, 'sw_gate': jax.random.normal(ks[2], (D, F), dtype=jnp.float32) * sc, 'sw_up': jax.random.normal(ks[3], (D, F), dtype=jnp.float32) * sc, 'sw_down': jax.random.normal(ks[4], (F, D), dtype=jnp.float32) * scf, 'ew_gate': jax.random.normal(ks[5], (E, D, F), dtype=jnp.float32) * sc, 'ew_up': jax.random.normal(ks[6], (E, D, F), dtype=jnp.float32) * sc, 'ew_down': jax.random.normal(ks[7], (E, F, D), dtype=jnp.float32) * scf}
    _L2_ffn_all = _L2_ffn_setup()
    _L2_ffn_in = {k: v for k, v in _L2_ffn_all.items() if k in ('gate_w', 'sw_gate', 'sw_up', 'sw_down', 'ew_gate', 'ew_up', 'ew_down')}
    del _L2_ffn_all

    def _L3_xattn_setup():
        import jax, jax.numpy as jnp
        import numpy as np
        NUM_HEADS = 16
        CLAMP = 10000.0
        key = jax.random.key(seed)
        ks = jax.random.split(key, 8)
        B, Nq, Nkv, Cq, Ckv = (4, 256, 256, 128, 96)
        s_q = 1.0 / np.sqrt(Cq)
        s_kv = 1.0 / np.sqrt(Ckv)
        return {'query': jax.random.normal(ks[0], (B, Nq, Cq), jnp.float32), 'key_value': jax.random.normal(ks[1], (B, Nkv, Ckv), jnp.float32), 'Wq': jax.random.normal(ks[2], (Cq, Cq), jnp.float32) * s_q, 'bq': jnp.zeros((Cq,), jnp.float32), 'Wk': jax.random.normal(ks[3], (Ckv, Cq), jnp.float32) * s_kv, 'bk': jnp.zeros((Cq,), jnp.float32), 'Wv': jax.random.normal(ks[4], (Ckv, Cq), jnp.float32) * s_kv, 'bv': jnp.zeros((Cq,), jnp.float32), 'Wo': jax.random.normal(ks[5], (Cq, Cq), jnp.float32) * s_q, 'bo': jnp.zeros((Cq,), jnp.float32)}
    _L3_xattn_all = _L3_xattn_setup()
    _L3_xattn_in = {k: v for k, v in _L3_xattn_all.items() if k in ('Wq', 'bq', 'Wk', 'bk', 'Wv', 'bv', 'Wo', 'bo')}
    del _L3_xattn_all

    def _L3_ffn_setup():
        import jax, jax.numpy as jnp
        import numpy as np

        def _binarize(w):
            alpha = jax.lax.stop_gradient(jnp.mean(jnp.abs(w), axis=1, keepdims=True))
            bw = alpha * jnp.sign(w)
            return w + jax.lax.stop_gradient(bw - w)
        key = jax.random.key(seed)
        k1, k2, k3, k4, k5 = jax.random.split(key, 5)
        D, H = (128, 512)
        x = jax.random.normal(k1, (64, 196, D), dtype=jnp.float32)
        w1 = jax.random.normal(k2, (H, D), dtype=jnp.float32) * 0.02
        b1 = jax.random.normal(k3, (H,), dtype=jnp.float32) * 0.02
        w2 = jax.random.normal(k4, (D, H), dtype=jnp.float32) * 0.02
        b2 = jax.random.normal(k5, (D,), dtype=jnp.float32) * 0.02
        return {'x': x, 'w1': w1, 'b1': b1, 'w2': w2, 'b2': b2}
    _L3_ffn_all = _L3_ffn_setup()
    _L3_ffn_in = {k: v for k, v in _L3_ffn_all.items() if k in ('w1', 'b1', 'w2', 'b2')}
    del _L3_ffn_all
    return {'x': x, 'ctx_768': ctx_768, 'g_xattn': g_xattn, 'g_ffn': g_ffn, 'L0_xattn_Wq': _L0_xattn_in['Wq'], 'L0_xattn_bq': _L0_xattn_in['bq'], 'L0_xattn_Wk': _L0_xattn_in['Wk'], 'L0_xattn_bk': _L0_xattn_in['bk'], 'L0_xattn_Wv': _L0_xattn_in['Wv'], 'L0_xattn_bv': _L0_xattn_in['bv'], 'L0_xattn_Wo': _L0_xattn_in['Wo'], 'L0_xattn_bo': _L0_xattn_in['bo'], 'L0_xattn_ln_gamma': _L0_xattn_in['ln_gamma'], 'L0_xattn_ln_beta': _L0_xattn_in['ln_beta'], 'L0_ffn_gate_w': _L0_ffn_in['gate_w'], 'L0_ffn_gate_b': _L0_ffn_in['gate_b'], 'L0_ffn_w1': _L0_ffn_in['w1'], 'L0_ffn_b1': _L0_ffn_in['b1'], 'L0_ffn_w2': _L0_ffn_in['w2'], 'L0_ffn_b2': _L0_ffn_in['b2'], 'L1_xattn_Wq': _L1_xattn_in['Wq'], 'L1_xattn_Wk': _L1_xattn_in['Wk'], 'L1_xattn_Wv': _L1_xattn_in['Wv'], 'L1_xattn_Wo': _L1_xattn_in['Wo'], 'L1_xattn_bo': _L1_xattn_in['bo'], 'L1_ffn_router_w': _L1_ffn_in['router_w'], 'L1_ffn_wg_r': _L1_ffn_in['wg_r'], 'L1_ffn_wu_r': _L1_ffn_in['wu_r'], 'L1_ffn_wd_r': _L1_ffn_in['wd_r'], 'L1_ffn_wg_s': _L1_ffn_in['wg_s'], 'L1_ffn_wu_s': _L1_ffn_in['wu_s'], 'L1_ffn_wd_s': _L1_ffn_in['wd_s'], 'L2_xattn_W_d2v': _L2_xattn_in['W_d2v'], 'L2_xattn_b_d2v': _L2_xattn_in['b_d2v'], 'L2_xattn_W_img': _L2_xattn_in['W_img'], 'L2_xattn_b_img': _L2_xattn_in['b_img'], 'L2_xattn_W_txt': _L2_xattn_in['W_txt'], 'L2_xattn_b_txt': _L2_xattn_in['b_txt'], 'L2_xattn_W_att0': _L2_xattn_in['W_att0'], 'L2_xattn_b_att0': _L2_xattn_in['b_att0'], 'L2_xattn_W_att1': _L2_xattn_in['W_att1'], 'L2_xattn_b_att1': _L2_xattn_in['b_att1'], 'L2_xattn_W_f1': _L2_xattn_in['W_f1'], 'L2_xattn_b_f1': _L2_xattn_in['b_f1'], 'L2_xattn_W_f2': _L2_xattn_in['W_f2'], 'L2_xattn_b_f2': _L2_xattn_in['b_f2'], 'L2_ffn_gate_w': _L2_ffn_in['gate_w'], 'L2_ffn_sw_gate': _L2_ffn_in['sw_gate'], 'L2_ffn_sw_up': _L2_ffn_in['sw_up'], 'L2_ffn_sw_down': _L2_ffn_in['sw_down'], 'L2_ffn_ew_gate': _L2_ffn_in['ew_gate'], 'L2_ffn_ew_up': _L2_ffn_in['ew_up'], 'L2_ffn_ew_down': _L2_ffn_in['ew_down'], 'L3_xattn_Wq': _L3_xattn_in['Wq'], 'L3_xattn_bq': _L3_xattn_in['bq'], 'L3_xattn_Wk': _L3_xattn_in['Wk'], 'L3_xattn_bk': _L3_xattn_in['bk'], 'L3_xattn_Wv': _L3_xattn_in['Wv'], 'L3_xattn_bv': _L3_xattn_in['bv'], 'L3_xattn_Wo': _L3_xattn_in['Wo'], 'L3_xattn_bo': _L3_xattn_in['bo'], 'L3_ffn_w1': _L3_ffn_in['w1'], 'L3_ffn_b1': _L3_ffn_in['b1'], 'L3_ffn_w2': _L3_ffn_in['w2'], 'L3_ffn_b2': _L3_ffn_in['b2']}

def reference(x, ctx_768, g_xattn, g_ffn, L0_xattn_Wq, L0_xattn_bq, L0_xattn_Wk, L0_xattn_bk, L0_xattn_Wv, L0_xattn_bv, L0_xattn_Wo, L0_xattn_bo, L0_xattn_ln_gamma, L0_xattn_ln_beta, L0_ffn_gate_w, L0_ffn_gate_b, L0_ffn_w1, L0_ffn_b1, L0_ffn_w2, L0_ffn_b2, L1_xattn_Wq, L1_xattn_Wk, L1_xattn_Wv, L1_xattn_Wo, L1_xattn_bo, L1_ffn_router_w, L1_ffn_wg_r, L1_ffn_wu_r, L1_ffn_wd_r, L1_ffn_wg_s, L1_ffn_wu_s, L1_ffn_wd_s, L2_xattn_W_d2v, L2_xattn_b_d2v, L2_xattn_W_img, L2_xattn_b_img, L2_xattn_W_txt, L2_xattn_b_txt, L2_xattn_W_att0, L2_xattn_b_att0, L2_xattn_W_att1, L2_xattn_b_att1, L2_xattn_W_f1, L2_xattn_b_f1, L2_xattn_W_f2, L2_xattn_b_f2, L2_ffn_gate_w, L2_ffn_sw_gate, L2_ffn_sw_up, L2_ffn_sw_down, L2_ffn_ew_gate, L2_ffn_ew_up, L2_ffn_ew_down, L3_xattn_Wq, L3_xattn_bq, L3_xattn_Wk, L3_xattn_bk, L3_xattn_Wv, L3_xattn_bv, L3_xattn_Wo, L3_xattn_bo, L3_ffn_w1, L3_ffn_b1, L3_ffn_w2, L3_ffn_b2):
    import jax
    import jax.numpy as jnp

    def _L0_xattn_ref(query, key, value, Wq, bq, Wk, bk, Wv, bv, Wo, bo, ln_gamma, ln_beta):
        import jax, jax.numpy as jnp
        import numpy as np
        QUERY_DIM, KV_DIM, EMBED_DIM, NUM_HEADS = (128, 96, 128, 16)
        HEAD_DIM = EMBED_DIM // NUM_HEADS
        SCALE = HEAD_DIM ** (-0.5)
        LN_EPS = 1e-05

        def _l2norm(x, eps=1e-12):
            n = jnp.sqrt(jnp.sum(x * x, axis=-1, keepdims=True))
            return x / jnp.maximum(n, eps)
        B, Nq, _ = query.shape
        Nk = key.shape[1]
        Qp = query @ Wq + bq
        K = _l2norm(key @ Wk + bk)
        V = value @ Wv + bv
        Q = _l2norm(Qp)
        Q = Q.reshape(B, Nq, NUM_HEADS, HEAD_DIM).transpose(0, 2, 1, 3)
        K = K.reshape(B, Nk, NUM_HEADS, HEAD_DIM).transpose(0, 2, 1, 3)
        V = V.reshape(B, Nk, NUM_HEADS, HEAD_DIM).transpose(0, 2, 1, 3)
        scores = jnp.einsum('bhqd,bhkd->bhqk', Q, K) * SCALE
        attn = jax.nn.softmax(scores, axis=-1)
        out = jnp.einsum('bhqk,bhkd->bhqd', attn, V)
        out = out.transpose(0, 2, 1, 3).reshape(B, Nq, EMBED_DIM)
        out = out @ Wo + bo
        x = out + Qp
        mu = jnp.mean(x, axis=-1, keepdims=True)
        var = jnp.mean((x - mu) ** 2, axis=-1, keepdims=True)
        return (x - mu) / jnp.sqrt(var + LN_EPS) * ln_gamma + ln_beta

    def _L0_ffn_ref(x, gate_w, gate_b, w1, b1, w2, b2):
        import jax, jax.numpy as jnp
        import numpy as np
        D = 128
        H = 512
        E = 64
        K = 3
        B, S = (2, 256)
        C = 64
        xf = x.reshape(-1, D)
        T = xf.shape[0]
        logits = xf @ gate_w + gate_b
        top_l, top_i = jax.lax.top_k(logits, K)
        gates = jax.nn.softmax(top_l, axis=-1)
        fe = top_i.reshape(-1)
        fg = gates.reshape(-1)
        tok = jnp.repeat(jnp.arange(T), K)
        oh = jax.nn.one_hot(fe, E, dtype=jnp.int32)
        pos = (jnp.cumsum(oh, axis=0) * oh).sum(-1) - 1
        valid = pos < C
        buf = jnp.zeros((E, C, D), x.dtype).at[fe, pos].set(xf[tok], mode='drop')
        h = jax.nn.gelu(jnp.einsum('ecd,edh->ech', buf, w1) + b1[:, None, :], approximate=False)
        y = jnp.einsum('ech,ehd->ecd', h, w2) + b2[:, None, :]
        rows = y[fe, jnp.minimum(pos, C - 1)] * (fg * valid.astype(x.dtype))[:, None]
        out = jnp.zeros_like(xf).at[tok].add(rows)
        return out.reshape(x.shape)

    def _L1_xattn_ref(x, context, Wq, Wk, Wv, Wo, bo):
        import jax, jax.numpy as jnp
        import numpy as np
        HEADS = 16
        DIM_HEAD = 64
        B, Nq, _ = x.shape
        Nk = context.shape[1]
        h, dh = (HEADS, DIM_HEAD)
        q = (x @ Wq).reshape(B, Nq, h, dh)
        k = (context @ Wk).reshape(B, Nk, h, dh)
        v = (context @ Wv).reshape(B, Nk, h, dh)
        scale = 1.0 / jnp.sqrt(jnp.asarray(dh, dtype=x.dtype))
        scores = jnp.einsum('bqhd,bkhd->bhqk', q, k) * scale
        attn = jax.nn.softmax(scores, axis=-1)
        out = jnp.einsum('bhqk,bkhd->bqhd', attn, v).reshape(B, Nq, h * dh)
        return out @ Wo + bo

    def _L1_ffn_ref(x, router_w, wg_r, wu_r, wd_r, wg_s, wu_s, wd_s):
        import jax, jax.numpy as jnp
        import numpy as np
        HIDDEN = 128
        N_ROUTED = 16
        N_SHARED = 2
        TOP_K = 2
        MID_R = HIDDEN // 4
        MID_S = HIDDEN // 2
        orig_shape = x.shape
        flat = x.reshape(-1, orig_shape[-1])
        gs = jnp.einsum('td,ndm->tnm', flat, wg_s)
        us = jnp.einsum('td,ndm->tnm', flat, wu_s)
        out = jnp.einsum('tnm,nmd->td', jax.nn.silu(gs) * us, wd_s)
        logits = (flat @ router_w).astype(jnp.float32)
        probs = jax.nn.softmax(logits, axis=-1)
        weights, indices = jax.lax.top_k(probs, TOP_K)
        weights = weights / (weights.sum(axis=-1, keepdims=True) + 1e-09)
        weights = weights.astype(x.dtype)
        comb = jnp.sum(jax.nn.one_hot(indices, N_ROUTED, dtype=x.dtype) * weights[..., None], axis=1)
        g = jnp.einsum('td,edm->tem', flat, wg_r)
        u = jnp.einsum('td,edm->tem', flat, wu_r)
        h = jax.nn.silu(g) * u
        h = h * comb[:, :, None]
        out = out + jnp.einsum('tem,emd->td', h, wd_r)
        return out.reshape(orig_shape)

    def _L2_xattn_ref(text_embeddings, dinov2_features, W_d2v, b_d2v, W_img, b_img, W_txt, b_txt, W_att0, b_att0, W_att1, b_att1, W_f1, b_f1, W_f2, b_f2):
        import jax, jax.numpy as jnp
        import numpy as np
        import math
        E = 128
        EV = 128
        FFN = 512
        DINO = 96
        B, S, P = (64, 64, 32)

        def bitnet_linear(x, W, b):
            w_scale = jnp.maximum(jnp.mean(jnp.abs(W)), 1e-05)
            qW = jnp.sign(W) * (jnp.abs(W) > 0.5 * w_scale).astype(W.dtype)
            i_scale = jnp.maximum(jnp.max(jnp.abs(x)), 1e-08) / 127.0
            qx = jnp.clip(jnp.round(x / i_scale), -128.0, 127.0)
            out = jnp.einsum('...i,oi->...o', qx, qW) * (w_scale * i_scale)
            return out + b
        b, s, e = text_embeddings.shape
        vis = bitnet_linear(dinov2_features, W_d2v, b_d2v)
        image_embeds = bitnet_linear(vis, W_img, b_img)
        fused = bitnet_linear(text_embeddings, W_txt, b_txt)
        inv_sqrt_e = 1.0 / math.sqrt(e)
        for Wa, ba in ((W_att0, b_att0), (W_att1, b_att1)):
            kv = bitnet_linear(image_embeds, Wa, ba)
            k = jnp.concatenate([kv, kv], axis=-1)
            scores = jnp.einsum('bse,bpe->bsp', fused, k) * inv_sqrt_e
            attn = jax.nn.softmax(scores, axis=-1)
            fused = fused + 0.1 * jnp.einsum('bsp,bpe->bse', attn, k)
        avg_img = jnp.mean(image_embeds, axis=1, keepdims=True)
        concatenated = jnp.concatenate([fused, jnp.broadcast_to(avg_img, (b, s, e))], axis=-1)
        h = jax.nn.relu(bitnet_linear(concatenated, W_f1, b_f1))
        return bitnet_linear(h, W_f2, b_f2)

    def _L2_ffn_ref(x, gate_w, sw_gate, sw_up, sw_down, ew_gate, ew_up, ew_down):
        import jax, jax.numpy as jnp
        import numpy as np
        E = 8
        K = 2
        D = 128
        F = 128
        B, S = (2, 256)
        b, s, d = x.shape
        xf = x.reshape(-1, d)
        T = xf.shape[0]
        silu = jax.nn.silu
        shared = silu(xf @ sw_gate) * (xf @ sw_up) @ sw_down
        gate = jax.nn.softmax(xf @ gate_w, axis=-1)
        topw, topi = jax.lax.top_k(gate, K)
        topw = topw / (topw.sum(axis=-1, keepdims=True) + 1e-20)
        w = jnp.zeros((T, E), dtype=gate.dtype).at[jnp.arange(T)[:, None], topi].add(topw)
        h = jnp.einsum('td,edf->etf', xf, ew_gate)
        u = jnp.einsum('td,edf->etf', xf, ew_up)
        y = jnp.einsum('etf,efd->etd', silu(h) * u, ew_down)
        routed = jnp.einsum('etd,te->td', y, w)
        return (shared + routed).reshape(b, s, d)

    def _L3_xattn_ref(query, key_value, Wq, bq, Wk, bk, Wv, bv, Wo, bo):
        import jax, jax.numpy as jnp
        import numpy as np
        NUM_HEADS = 16
        CLAMP = 10000.0
        B, Nq, Cq = query.shape
        Nkv = key_value.shape[1]
        H = NUM_HEADS
        D = Cq // H
        scale = D ** (-0.5)
        q = (query @ Wq + bq).reshape(B, Nq, H, D).transpose(0, 2, 1, 3)
        k = (key_value @ Wk + bk).reshape(B, Nkv, H, D).transpose(0, 2, 1, 3)
        v = (key_value @ Wv + bv).reshape(B, Nkv, H, D).transpose(0, 2, 1, 3)
        attn = jnp.einsum('bhqd,bhkd->bhqk', q, k) * scale
        attn = jnp.clip(attn, -CLAMP, CLAMP)
        attn = jax.nn.softmax(attn, axis=-1)
        attn = jnp.where(jnp.any(jnp.isnan(attn)), jnp.asarray(1.0 / Nkv, attn.dtype), attn)
        x = jnp.einsum('bhqk,bhkd->bqhd', attn, v).reshape(B, Nq, Cq)
        return x @ Wo + bo

    def _L3_ffn_ref(x, w1, b1, w2, b2):
        import jax, jax.numpy as jnp
        import numpy as np

        def _binarize(w):
            alpha = jax.lax.stop_gradient(jnp.mean(jnp.abs(w), axis=1, keepdims=True))
            bw = alpha * jnp.sign(w)
            return w + jax.lax.stop_gradient(bw - w)
        bw1 = _binarize(w1)
        h = jnp.einsum('bsd,hd->bsh', x, bw1) + b1
        h = jax.nn.gelu(h, approximate=False)
        bw2 = _binarize(w2)
        out = jnp.einsum('bsh,dh->bsd', h, bw2) + b2
        return out
    x = x + jnp.tanh(g_xattn[0]) * _L0_xattn_ref(_layernorm(x, axis=-1), ctx_768, ctx_768, L0_xattn_Wq, L0_xattn_bq, L0_xattn_Wk, L0_xattn_bk, L0_xattn_Wv, L0_xattn_bv, L0_xattn_Wo, L0_xattn_bo, L0_xattn_ln_gamma, L0_xattn_ln_beta)
    x = x + jnp.tanh(g_ffn[0]) * _L0_ffn_ref(_layernorm(x, axis=-1), L0_ffn_gate_w, L0_ffn_gate_b, L0_ffn_w1, L0_ffn_b1, L0_ffn_w2, L0_ffn_b2)
    x = x + jnp.tanh(g_xattn[1]) * _L1_xattn_ref(_layernorm(x, axis=-1), ctx_768, L1_xattn_Wq, L1_xattn_Wk, L1_xattn_Wv, L1_xattn_Wo, L1_xattn_bo)
    x = x + jnp.tanh(g_ffn[1]) * _L1_ffn_ref(_layernorm(x, axis=-1), L1_ffn_router_w, L1_ffn_wg_r, L1_ffn_wu_r, L1_ffn_wd_r, L1_ffn_wg_s, L1_ffn_wu_s, L1_ffn_wd_s)
    x = x + jnp.tanh(g_xattn[2]) * _L2_xattn_ref(_layernorm(x, axis=-1), ctx_768, L2_xattn_W_d2v, L2_xattn_b_d2v, L2_xattn_W_img, L2_xattn_b_img, L2_xattn_W_txt, L2_xattn_b_txt, L2_xattn_W_att0, L2_xattn_b_att0, L2_xattn_W_att1, L2_xattn_b_att1, L2_xattn_W_f1, L2_xattn_b_f1, L2_xattn_W_f2, L2_xattn_b_f2)
    x = x + jnp.tanh(g_ffn[2]) * _L2_ffn_ref(_layernorm(x, axis=-1), L2_ffn_gate_w, L2_ffn_sw_gate, L2_ffn_sw_up, L2_ffn_sw_down, L2_ffn_ew_gate, L2_ffn_ew_up, L2_ffn_ew_down)
    x = x + jnp.tanh(g_xattn[3]) * _L3_xattn_ref(_layernorm(x, axis=-1), ctx_768, L3_xattn_Wq, L3_xattn_bq, L3_xattn_Wk, L3_xattn_bk, L3_xattn_Wv, L3_xattn_bv, L3_xattn_Wo, L3_xattn_bo)
    x = x + jnp.tanh(g_ffn[3]) * _L3_ffn_ref(_layernorm(x, axis=-1), L3_ffn_w1, L3_ffn_b1, L3_ffn_w2, L3_ffn_b2)
    return x

_drawn_inputs = setup_inputs


def setup_inputs(seed=0):
    import zlib

    import numpy as np

    out = dict(_drawn_inputs(seed))
    spreads = {'L0_xattn_bq': (0.0, 0.1),
     'L0_xattn_bk': (0.0, 2.0),
     'L0_xattn_bv': (0.0, 0.1),
     'L0_xattn_bo': (0.0, 0.1),
     'L0_xattn_ln_gamma': (1.0, 0.2),
     'L0_xattn_ln_beta': (0.0, 0.1),
     'L0_ffn_gate_b': (0.0, 0.1),
     'L0_ffn_b1': (0.0, 0.499),
     'L0_ffn_b2': (0.0, 0.1),
     'L2_xattn_b_d2v': (0.0, 0.1),
     'L2_xattn_b_img': (0.0, 0.1),
     'L2_xattn_b_txt': (0.0, 0.1),
     'L2_xattn_b_att0': (0.0, 1.922),
     'L2_xattn_b_att1': (0.0, 2.0),
     'L2_xattn_b_f1': (0.0, 0.1),
     'L2_xattn_b_f2': (0.0, 0.1),
     'L3_xattn_bq': (0.0, 0.714),
     'L3_xattn_bk': (0.0, 2.0),
     'L3_xattn_bv': (0.0, 0.1),
     'L3_xattn_bo': (0.0, 0.1)}
    factors = {'g_ffn': 8.0,
     'L0_xattn_Wk': 25.559,
     'L0_ffn_w1': 2.815,
     'L1_xattn_bo': 2.913,
     'L1_ffn_router_w': 7.269,
     'L1_ffn_wg_r': 6.715,
     'L1_ffn_wu_r': 6.799,
     'L1_ffn_wd_r': 6.33,
     'L1_ffn_wg_s': 5.079,
     'L1_ffn_wu_s': 4.827,
     'L1_ffn_wd_s': 5.099,
     'L2_xattn_W_att0': 2.776,
     'L2_xattn_W_att1': 3.05,
     'L3_ffn_w1': 3.091,
     'L3_ffn_b1': 8.0,
     'L3_ffn_w2': 3.046,
     'L3_ffn_b2': 5.154}
    for name, (base, spread) in spreads.items():
        noise = np.random.default_rng([zlib.crc32(name.encode()), seed]).standard_normal(out[name].shape)
        drawn = base * np.exp(spread * noise) if base else spread * noise
        out[name] = jnp.asarray(drawn.astype(out[name].dtype))
    for name, factor in factors.items():
        out[name] = (out[name] * factor).astype(out[name].dtype)
    return out
```

```python
from contextlib import ExitStack

import numpy as np
import concourse.bass as bass
from concourse import mybir

F32 = mybir.dt.float32
F32R = mybir.dt.float32r
BF16 = mybir.dt.bfloat16
I16 = mybir.dt.int16
I32 = mybir.dt.int32
U32 = mybir.dt.uint32
ALU = mybir.AluOpType
ACT = mybir.ActivationFunctionType
AX = mybir.AxisListType

B, NQ, D = 32, 56, 128
NK, DC = 1500, 96
T = B * NQ
CH = 448
NCH = T // CH
TT = 112
NT = T // TT
H = 16
HQ = H * NQ
HALF = HQ // 2
DH = 8
VW = 2 * (DH + 1)
KT, KP = 12, 125
KA = DC + 1
KM = DC + 2
LN_EPS = 1e-5
MAGIC = 1.5 * 2.0 ** 23
E0, CAP, TOPK0, HID0 = 64, 64, 3, 512


class Signal:

    def __init__(self, nc, name):
        self.sem = nc.alloc_semaphore(name)
        self.base = 0

    def at(self, n):
        return self.base + n


class Core:

    def __init__(self, nc, ctx, d, out):
        self.nc, self.ctx, self.d, self.out = nc, ctx, d, out
        self.ps = ctx.enter_context(nc.psum_tensor("ps", [128, 8, 512], F32))
        self.xT = self.sb("xT", [D, T])
        self.xn = self.sb("xn", [D, T])
        self.OT = self.sb("OT", [D, T])
        self.J = self.sb("J", [128, 128])
        self.ones = self.sb("ones", [128, 128])
        self.ident = self.sb("ident", [128, 128])
        self.sum_row = self.sb("sum_row", [128, 2, 128])
        self.vec = self.sb("vec", [128, NVEC])
        self.tg = self.sb("tg", [128, 8])
        self.eps = self.sb("eps", [128, 1])
        self.signals, self.part = [], 0
        self.new_signals()

    def sb(self, name, shape, dt=F32, ctx=None):
        return (ctx or self.ctx).enter_context(self.nc.sbuf_tensor(name, shape, dt))

    def sig(self, name):
        s = Signal(self.nc, f"{name}_{self.part}")
        self.signals.append(s)
        return s

    def new_signals(self):
        nc, old = self.nc, self.signals
        if old:
            with nc.Block() as block:
                @block.gpsimd
                def _(pool):
                    nc.clear_and_free_semaphores([s.sem for s in old])
        self.signals = []
        self.part += 1
        self.step = {e: self.sig(f"{e}_step") for e in ("dve", "act", "pe", "pool")}
        self.queries_made, self.queries_act, self.queries_dve = (
            self.sig(f"queries_{n}") for n in ("made", "act", "dve"))
        self.attend = {n: self.sig(f"attend_{n}") for n in ATTEND_ALL}
        self.mean_ready = self.sig("mean_ready")
        self.centred = self.sig("centred")
        self.squared = self.sig("squared")
        self.var_ready = self.sig("var_ready")
        self.std_ready = self.sig("std_ready")

    def linker(self, eng, which):
        s = self.step[which]

        def link(ins):
            ins.then_inc(s.sem, 1)
            s.base += 1
            eng.wait_ge(s.sem, s.base)
        return link


VECS = ["L0_bq", "L0_bo", "L0_g", "L0_b", "L1_bo", "L3_bo", "L3_b2",
        "d2v", "img", "txt", "att0", "att1", "f2"] + [f"f1_{c}" for c in range(4)] \
    + [f"ffb1_{c}" for c in range(4)]
NVEC = len(VECS)


def v(core, name, p=128):
    n = VECS.index(name)
    return core.vec[0:p, n:n + 1]


def start_up(core):
    nc, d = core.nc, core.d
    loaded, g_in = core.sig("loaded"), core.sb("g_in", [128, 8])
    consts, zeroed = core.sig("consts"), core.sig("zeroed")
    with nc.Block() as block:
        @block.sync
        def _(sp):
            sp.dma_start(core.xT[:, :], d["xT"]).then_inc(loaded.sem, 16)
            sp.dma_start(core.vec[:, :], d["vec"]).then_inc(loaded.sem, 16)
            sp.dma_start(g_in[:, :], d["gates"]).then_inc(loaded.sem, 16)
            sp.wait_ge(loaded.sem, 48)

        @block.scalar
        def _(act):
            act.wait_ge(loaded.sem, 48)
            nc.scalar.activation(core.tg[:, :], g_in[:, :], ACT.Tanh).then_inc(consts.sem, 1)

        @block.vector
        def _(dve):
            nc.vector.memset(core.J[:, :], 1.0 / D).then_inc(consts.sem, 1)
            nc.vector.memset(core.ones[:, :], 1.0).then_inc(consts.sem, 1)
            nc.vector.memset(core.eps[:, :], LN_EPS).then_inc(consts.sem, 1)

        @block.gpsimd
        def _(pool):
            nc.gpsimd.memset(core.ident[:, :], 0.0).then_inc(zeroed.sem, 1)
            pool.wait_ge(zeroed.sem, 1)
            nc.gpsimd.affine_select(out=core.ident[:, :], in_=core.ident[:, :], compare_op=ALU.not_equal,
                                    fill=1.0, base=0, pattern=[[-1, 128]],
                                    channel_multiplier=1).then_inc(consts.sem, 1)
            nc.gpsimd.memset(core.sum_row[:, :, :], 0.0).then_inc(zeroed.sem, 1)
            pool.wait_ge(zeroed.sem, 2)
            for j in range(2):
                nc.gpsimd.affine_select(out=core.sum_row[:, j, :].rearrange("p (g c) -> p g c", c=32),
                                        in_=core.sum_row[:, j, :].rearrange("p (g c) -> p g c", c=32),
                                        compare_op=ALU.not_equal, fill=1.0, base=-((DH + 1) * j + DH),
                                        pattern=[[-32, 4], [0, 32]],
                                        channel_multiplier=1).then_inc(consts.sem, 1)


def layer_norm(core, src, dst, tag, finish=None):
    nc = core.nc
    mean, cen, sq, var, std = (core.mean_ready, core.centred, core.squared, core.var_ready,
                               core.std_ready)
    with ExitStack() as ctx:
        xc = core.sb(f"xc{tag}", [D, T], F32, ctx)
        x2 = core.sb(f"x2{tag}", [D, T], F32, ctx)
        sd = core.sb(f"sd{tag}", [D, T], F32, ctx)
        with nc.Block() as block:
            @block.tensor
            def _(pe):
                for c in range(NCH):
                    nc.tensor.matmul(core.ps[:, c, 0:CH], core.J[:, :], src[:, c * CH:(c + 1) * CH],
                                     start=True, stop=True).then_inc(mean.sem, 1)
                for c in range(NCH):
                    pe.wait_ge(sq.sem, sq.at(c + 1))
                    nc.tensor.matmul(core.ps[:, 4 + c, 0:CH], core.J[:, :], x2[:, c * CH:(c + 1) * CH],
                                     start=True, stop=True).then_inc(var.sem, 1)

            @block.scalar
            def _(act):
                for c in range(NCH):
                    act.wait_ge(cen.sem, cen.at(c + 1))
                    s = slice(c * CH, (c + 1) * CH)
                    nc.scalar.activation(x2[:, s], xc[:, s], ACT.Square).then_inc(sq.sem, 1)
                for c in range(NCH):
                    act.wait_ge(var.sem, var.at(c + 1))
                    nc.scalar.activation(sd[:, c * CH:(c + 1) * CH], core.ps[:, 4 + c, 0:CH], ACT.Sqrt,
                                         bias=core.eps[:, :]).then_inc(std.sem, 1)

            @block.vector
            def _(dve):
                link = core.linker(dve, "dve")
                for c in range(NCH):
                    dve.wait_ge(mean.sem, mean.at(c + 1))
                    s = slice(c * CH, (c + 1) * CH)
                    nc.vector.tensor_tensor(xc[:, s], src[:, s], core.ps[:, c, 0:CH],
                                            ALU.subtract).then_inc(cen.sem, 1)
                dve.wait_ge(cen.sem, cen.at(NCH))
                for c in range(NCH):
                    dve.wait_ge(std.sem, std.at(c + 1))
                    s = slice(c * CH, (c + 1) * CH)
                    link(nc.vector.reciprocal(x2[:, s], sd[:, s]))
                    link(nc.vector.tensor_tensor(dst[:, s], xc[:, s], x2[:, s], ALU.mult))
                if finish:
                    finish(link)
        for s in (mean, cen, sq, var, std):
            s.base += NCH


def add_gated(core, src, gate):
    nc = core.nc
    with nc.Block() as block:
        @block.vector
        def _(dve):
            link = core.linker(dve, "dve")
            link(nc.vector.scalar_tensor_tensor(out=core.xT[:, :], in0=src[:, :],
                                                scalar=core.tg[:, gate:gate + 1], in1=core.xT[:, :],
                                                op0=ALU.mult, op1=ALU.add))


def context_statistics(core, rk, amax, csum):
    nc, d = core.nc, core.d
    with ExitStack() as ctx:
        ct = core.sb("cs_ct", [KA, 2, NK], F32, ctx)
        wk = core.sb("cs_wk", [KA, D], F32, ctx)
        sq = core.sb("cs_sq", [KP, 2, KT, D], F32, ctx)
        junk = core.sb("cs_junk", [KA, NK], F32, ctx)
        am = core.sb("cs_am", [DC, B], F32, ctx)
        n2 = core.sb("cs_n2", [KP, B * KT], F32, ctx)
        w_in, normed = core.sig("cs_w_in"), core.sig("cs_normed")
        ct_in = [core.sig(f"cs_ct_in{s}") for s in range(2)]
        projected, squared, reduced, maxed, summed = (core.sig(f"cs_{n}") for n in (
            "projected", "squared", "reduced", "maxed", "summed"))
        with nc.Block() as block:
            @block.sync
            def _(sp):
                sp.dma_start(wk[:, :], d["L0_WkA"]).then_inc(w_in.sem, 16)
                with sp.Fori(0, B // 2) as i:
                    for s in range(2):
                        sp.wait_ge(projected.sem, 2 * i + s + 1)
                        sp.wait_ge(maxed.sem, 2 * i + s + 1)
                        sp.wait_ge(summed.sem, 2 * i + s + 1)
                        sp.dma_start(ct[:, s, :], d["ctxT"][bass.ds(2 * i + s, 1), 0:KA, :]
                                     .rearrange("o p n -> (o p) n")).then_inc(ct_in[s].sem, 16)

            @block.tensor
            def _(pe):
                pe.sem_inc(projected.sem, 2)
                pe.wait_ge(w_in.sem, 16)
                with pe.Fori(0, B // 2) as i:
                    for s in range(2):
                        pe.wait_ge(ct_in[s].sem, 16 * i + 16)
                        pe.wait_ge(squared.sem, 2 * i + s + 1)
                        for j in range(KT):
                            mm = nc.tensor.matmul(core.ps[0:KP, 3 * s + j // 4, (j % 4) * D:(j % 4 + 1) * D],
                                                  ct[:, s, j * KP:(j + 1) * KP], wk[:, :],
                                                  start=True, stop=True)
                        mm.then_inc(projected.sem, 1)

            @block.scalar
            def _(act):
                act.sem_inc(squared.sem, 2)
                act.sem_inc(summed.sem, 2)
                with act.Fori(0, B // 2) as i:
                    for s in range(2):
                        act.wait_ge(ct_in[s].sem, 16 * i + 16)
                        act.wait_ge(summed.sem, 2 * i + s + 2)
                        nc.scalar.activation(junk[:, :], ct[:, s, :], ACT.Copy,
                                             accum_out=csum[:, bass.ds(2 * i + s, 1)]).then_inc(summed.sem, 1)
                        act.wait_ge(projected.sem, 2 * i + s + 3)
                        act.wait_ge(reduced.sem, 2 * i + s + 1)
                        nc.scalar.activation(sq[:, s, :, :].rearrange("p j n -> p (j n)"),
                                             core.ps[0:KP, 3 * s:3 * s + 3, :].rearrange("p b n -> p (b n)"),
                                             ACT.Square).then_inc(squared.sem, 1)
                act.wait_ge(reduced.sem, B + 2)
                nc.scalar.activation(rk[:, :], n2[:, :], ACT.Sqrt).then_inc(normed.sem, 1)

            @block.vector
            def _(dve):
                link = core.linker(dve, "dve")
                dve.sem_inc(reduced.sem, 2)
                dve.sem_inc(maxed.sem, 2)
                with dve.Fori(0, B // 2) as i:
                    for s in range(2):
                        dve.wait_ge(ct_in[s].sem, 16 * i + 16)
                        nc.vector.tensor_reduce(am[:, bass.ds(2 * i + s, 1)], ct[0:DC, s, :], AX.X, ALU.max,
                                                apply_absolute_value=True).then_inc(maxed.sem, 1)
                        dve.wait_ge(squared.sem, 2 * i + s + 3)
                        nc.vector.tensor_reduce(n2[:, bass.ds((2 * i + s) * KT, KT)], sq[:, s, :, :],
                                                AX.X, ALU.add).then_inc(reduced.sem, 1)
                dve.wait_ge(maxed.sem, B + 2)
                link(nc.vector.tensor_reduce(amax[:, :], am[:, :], AX.X, ALU.max))
                dve.wait_ge(normed.sem, 1)
                link(nc.vector.tensor_scalar(n2[:, :], rk[:, :], 1e-12, None, ALU.max))
                link(nc.vector.reciprocal(rk[:, :], n2[:, :]))
                link(nc.vector.tensor_scalar(rk[:, :], rk[:, :], float(8) ** -0.5, None, ALU.mult))


def l2_norm_queries(core, qp, qn):
    nc, d = core.nc, core.d
    w_in = core.sig("l2q_w_in")
    mm1, qpd, sqd, mm2, nrm = (core.sig(f"l2q_{n}") for n in ("mm", "qp", "sq", "sum", "norm"))
    with ExitStack() as ctx:
        wq = core.sb("l2q_w", [D, D], F32, ctx)
        x2 = core.sb("l2q_x2", [D, T], F32, ctx)
        with nc.Block() as block:
            @block.sync
            def _(sp):
                sp.dma_start(wq[:, :], d["L0_Wq"]).then_inc(w_in.sem, 16)

            @block.tensor
            def _(pe):
                pe.wait_ge(w_in.sem, 16)
                for c in range(NCH):
                    nc.tensor.matmul(core.ps[:, c, 0:CH], wq[:, :], core.xn[:, c * CH:(c + 1) * CH],
                                     start=True, stop=True).then_inc(mm1.sem, 1)
                for c in range(NCH):
                    pe.wait_ge(sqd.sem, c + 1)
                    nc.tensor.matmul(core.ps[:, 4 + c, 0:CH], core.ones[:, :], x2[:, c * CH:(c + 1) * CH],
                                     start=True, stop=True).then_inc(mm2.sem, 1)

            @block.scalar
            def _(act):
                for c in range(NCH):
                    s = slice(c * CH, (c + 1) * CH)
                    act.wait_ge(qpd.sem, c + 1)
                    nc.scalar.activation(x2[:, s], qp[:, s], ACT.Square).then_inc(sqd.sem, 1)
                act.wait_ge(sqd.sem, NCH)
                for c in range(NCH):
                    act.wait_ge(mm2.sem, c + 1)
                    nc.scalar.activation(x2[:, c * CH:(c + 1) * CH], core.ps[:, 4 + c, 0:CH],
                                         ACT.Sqrt).then_inc(nrm.sem, 1)

            @block.vector
            def _(dve):
                link = core.linker(dve, "dve")
                for c in range(NCH):
                    dve.wait_ge(mm1.sem, c + 1)
                    nc.vector.tensor_scalar(qp[:, c * CH:(c + 1) * CH], core.ps[:, c, 0:CH],
                                            v(core, "L0_bq"), None, ALU.add).then_inc(qpd.sem, 1)
                dve.wait_ge(qpd.sem, NCH)
                for c in range(NCH):
                    s = slice(c * CH, (c + 1) * CH)
                    dve.wait_ge(nrm.sem, c + 1)
                    link(nc.vector.tensor_scalar(x2[:, s], x2[:, s], 1e-12, None, ALU.max))
                    link(nc.vector.reciprocal(x2[:, s], x2[:, s]))
                    link(nc.vector.tensor_tensor(qn[:, s], qp[:, s], x2[:, s], ALU.mult))


HB = B // 2
NP = HB // 2


def attention(core, L, src, bo, scale=1.0, keep_max=True, clip=None, rk=None, dh=8, csum=None):
    nc, d = core.nc, core.d
    outer = ExitStack()
    few = dh == DH
    N = core.sb(f"{L}_N", [KA, H, D], F32, outer) if not few or clip is not None else None
    M = core.sb(f"{L}_M", [D, H, KA], F32, outer)
    cq = core.sb(f"{L}_cq", [KA, H], F32, outer) if keep_max else None
    ok = core.sb(f"{L}_ok", [128, 2 * QV], F32, outer) if clip is not None else None
    values = None
    if few:
        values = (core.sb(f"{L}_wve", [KA, H // 2 * VW], F32, outer),
                  core.sb(f"{L}_woe", [128, 4, D], F32, outer),
                  [core.sb(f"{L}_values{s}", [KP, KT, H // 2, 32], F32, outer) for s in range(2)])
    with outer:
        fold_weights(core, L, M, N, cq, scale, keep_max, dh, values)
        if few:
            with nc.Block() as block:
                @block.gpsimd
                def _(pool):
                    link = core.linker(pool, "pool")
                    for t in values[2]:
                        link(nc.gpsimd.memset(t[:, :, :, :], 0.0))
                    if ok is not None:
                        link(nc.gpsimd.memset(ok[:, :], 1.0))
        for half in range(2):
            with ExitStack() as ctx:
                qp = core.sb(f"{L}_qp{half}", [KM if keep_max else KA, HB, HQ], F32, ctx)
                make_queries(core, qp, M, cq, src, scale, half)
                attend_half(core, f"{L}{half}", qp, N, bo, half, keep_max, clip, rk, ok, values, ctx)
        if clip is not None:
            uniform_if_nan(core, L, N, ok, csum, bo, outer)


QV = H // 4 * NQ


def fold_weights(core, L, M, N, cq, scale, keep_max, dh, values):
    nc, d, ps = core.nc, core.d, core.ps
    with ExitStack() as c2:
        w_in, m_mm, m_sb = (core.sig(f"{L}_{n}") for n in ("w_in", "fold_mm", "fold_sb"))
        loads = []
        if N is not None:
            wva = core.sb(f"{L}_wva", [dh, H, KA], F32, c2)
            wo = core.sb(f"{L}_wo", [dh, H, D], F32, c2)
            loads += [(wva[:, :, :], "WvA"), (wo[:, :, :], "Wo")]
        if keep_max:
            wqt = core.sb(f"{L}_wqt", [dh, H, D], F32, c2)
            wka = core.sb(f"{L}_wka", [dh, H, KA], F32, c2)
            bqh = core.sb(f"{L}_bqh", [dh, H], F32, c2)
            loads += [(wqt[:, :, :], "WqT"), (wka[:, :, :], "WkAT"), (bqh[:, :], "bqh")]
        else:
            loads += [(M[:, :, :], "WkBD")]
        if values:
            loads += [(values[0][:, :], "WvE"), (values[1][:, :, :], "WoE")]
        nw = 16 * len(loads)
        with nc.Block() as block:
            @block.sync
            def _(sp):
                for dst, name in loads:
                    sp.dma_start(dst, d[f"{L}_{name}"]).then_inc(w_in.sem, 16)
                sp.wait_ge(w_in.sem, nw)

            if N is None and not keep_max:
                return

            @block.tensor
            def _(pe):
                pe.wait_ge(w_in.sem, nw)
                for h in range(H):
                    g, k = h // 4, h % 4
                    mm = nc.tensor.matmul(ps[0:KA, 4 + g, k * D:(k + 1) * D], wva[:, h, :], wo[:, h, :],
                                          start=True, stop=True)
                    if keep_max:
                        mm = nc.tensor.matmul(ps[:, g, k * KA:(k + 1) * KA], wqt[:, h, :], wka[:, h, :],
                                              start=True, stop=True)
                mm.then_inc(m_mm.sem, 1)
                if keep_max:
                    pe.wait_ge(m_sb.sem, 4)
                    for h in range(H):
                        mm = nc.tensor.matmul(ps[0:KA, 0, h:h + 1], wka[:, h, :], bqh[:, h:h + 1],
                                              start=True, stop=True)
                    mm.then_inc(m_mm.sem, 1)

            @block.vector
            def _(dve):
                dve.wait_ge(m_mm.sem, 1)
                if keep_max:
                    for g in range(4):
                        nc.vector.tensor_copy(M[:, 4 * g:4 * g + 4, :].rearrange("p h n -> p (h n)"),
                                              ps[:, g, 0:4 * KA]).then_inc(m_sb.sem, 1)
                for g in range(4):
                    nc.vector.tensor_copy(N[:, 4 * g:4 * g + 4, :].rearrange("p h n -> p (h n)"),
                                          ps[0:KA, 4 + g, :]).then_inc(m_sb.sem, 1)
                if keep_max:
                    dve.wait_ge(m_mm.sem, 2)
                    nc.vector.tensor_scalar(cq[:, :], ps[0:KA, 0, 0:H], scale, None,
                                            ALU.mult).then_inc(m_sb.sem, 1)


def make_queries(core, qp, M, cq, src, scale, half):
    nc, ps = core.nc, core.ps
    qmm, qa, qd_ = core.queries_made, core.queries_act, core.queries_dve
    nch = NCH // 2
    with nc.Block() as block:
        @block.tensor
        def _(pe):
            with pe.Fori(0, nch) as c:
                for h in range(H):
                    w = qa if h % 2 == 0 else qd_
                    pe.wait_ge(w.sem, w.at(8 * c + h // 2 + 1))
                    nc.tensor.matmul(ps[0:KA, h % 8, 0:CH], M[:, h, :],
                                     src[:, bass.ds(c * CH + half * nch * CH, CH)],
                                     start=True, stop=True).then_inc(qmm.sem, 1)

        def bank(h):
            return ps[0:KA, h % 8, 0:CH].rearrange("p (b q) -> p b q", q=NQ)

        def place(h, c):
            return qp[0:KA, bass.ds(c * 8, 8), h * NQ:(h + 1) * NQ]

        @block.scalar
        def _(act):
            act.sem_inc(qa.sem, 4)
            with act.Fori(0, nch) as c:
                for h in range(0, H, 2):
                    act.wait_ge(qmm.sem, qmm.at(H * c + h + 1))
                    if cq is not None:
                        ins = nc.scalar.activation(place(h, c), bank(h), ACT.Identity,
                                                   bias=cq[:, h:h + 1], scale=scale)
                    else:
                        ins = nc.scalar.activation(place(h, c), bank(h), ACT.Copy)
                    ins.then_inc(qa.sem, 1)

        @block.vector
        def _(dve):
            dve.sem_inc(qd_.sem, 4)
            with dve.Fori(0, nch) as c:
                for h in range(1, H, 2):
                    dve.wait_ge(qmm.sem, qmm.at(H * c + h + 1))
                    if cq is not None:
                        ins = nc.vector.tensor_scalar(place(h, c), bank(h), scale, cq[:, h:h + 1],
                                                      ALU.mult, ALU.add)
                    else:
                        ins = nc.vector.tensor_copy(place(h, c), bank(h))
                    ins.then_inc(qd_.sem, 1)
    qmm.base += H * nch
    qa.base += H * nch // 2 + 4
    qd_.base += H * nch // 2 + 4


ATTEND = {"scored": 24 * NP, "exped": 24 * NP + 2, "weighed": 24 * NP + 2, "u_copied": 2 * NP + 1,
          "projected": NP, "out_copied": NP}
ATTEND_WIDE = {"ctx_in0": 32 * NP, "ctx_in1": 32 * NP, "den_out": 32 * NP, "den_in": 32 * NP,
               "den_inverted": 2 * NP, "den_spread": 2 * NP, "u_normed": 2 * NP + 1}
ATTEND_FEW = {"ctx_in0": 16 * NP, "ctx_in1": 16 * NP, "values_made": 8 * NP,
              "values_copied": 8 * NP + 1, "den_spread": NP, "den_inverted": NP, "u_normed": NP + 1}
ATTEND_MAX = {"qb_ready0": NP, "qb_ready1": NP, "ctr_in0": 16 * NP, "ctr_in1": 16 * NP,
              "chunk_scored": 24 * NP, "chunk_maxed": 24 * NP, "max_ready": 2 * NP,
              "max_turned": 2 * NP, "max_negated": 2 * NP, "max_in0": 16 * NP, "max_in1": 16 * NP}
ATTEND_CLIP = {"clip_max": 2 * NP, "low_spread": 2 * NP, "low_ready": 2 * NP, "clipped": 24 * NP + 2,
               "sel_ready": 2, "nan_seen": 2 * NP}
ATTEND_ALL = {**ATTEND, **ATTEND_WIDE, **ATTEND_FEW, **ATTEND_MAX, **ATTEND_CLIP}


def attend_half(core, tag, qp, N, bo, half, keep_max, clip, rk, ok, values, ctx):
    nc, d, ps = core.nc, core.d, core.ps
    S = core.attend

    def at(name, n):
        return S[name].sem, S[name].at(n)

    CT = [core.sb(f"{tag}_ct{s}", [KM, NK], F32, ctx) for s in range(2)]
    P = core.sb(f"{tag}_p", [KP, 2, HQ], F32, ctx)
    if values:
        WVE, WOE, VS = values
        UE, RD, UN = (core.sb(f"{tag}_{n}", [128, 2, QV], F32, ctx) for n in ("ue", "rd", "un"))
        eq = core.sb(f"{tag}_eq", [128, 2, QV], F32, ctx) if clip is not None else None
    else:
        CN = [core.sb(f"{tag}_cn{s}", [KP, KT, KA], F32, ctx) for s in range(2)]
        UE = core.sb(f"{tag}_ue", [KA, HQ], F32, ctx)
        UN = core.sb(f"{tag}_un", [KA, H, 2, NQ], F32, ctx)
        RC = core.sb(f"{tag}_rc", [KA, HQ], F32, ctx)
        dn, dr = (core.sb(f"{tag}_{n}", [8, TT], F32, ctx) for n in ("dn", "dr"))
    if keep_max:
        QB = [core.sb(f"{tag}_qb{s}", [KA, HQ], F32R, ctx) for s in range(2)]
        CR = [core.sb(f"{tag}_cr{s}", [KA, NK], F32R, ctx) for s in range(2)]
        mp = core.sb(f"{tag}_mp", [TT, 24], F32, ctx)
        mu = core.sb(f"{tag}_mu", [TT, 8], F32, ctx)
        mc = [core.sb(f"{tag}_mc{s}", [TT, 8], F32, ctx) for s in range(2)]
        mt = [core.sb(f"{tag}_mt{s}", [8, TT], F32, ctx) for s in range(2)]
    if clip is not None:
        LB = [core.sb(f"{tag}_lb{s}", [KP, HQ], F32, ctx) for s in range(2)]
        sel = core.sb(f"{tag}_sel", [KM, 128], F32, ctx)
    KS = KM if keep_max else KA
    SB = [ps[0:KP, 0:2, 0:HALF], ps[0:KP, 2:4, 0:HALF]]
    U = ps[:, 4, 0:QV] if values else ps[0:KA, 4:6, 0:HALF]
    b0 = half * HB
    NEXT_VALUES, FIRST_VALUES = (7, 9, 11, 13), (16, 18, 20, 22)

    def two(ap):
        return ap.rearrange("p (a n) -> p a n", a=2)

    def heads(ap):
        return ap.rearrange("p (h q) -> p h q", q=NQ)

    def query(i, s, a, rows):
        return qp[0:rows, bass.ds(2 * i + s, 1), a * HALF:(a + 1) * HALF].rearrange("p o n -> p (o n)")

    def pairs(eng, body, last=1):
        body(0, False, True, True)
        with eng.Fori(1, NP - last) as i:
            body(i, True, True, True)
        for i in range(NP - last, NP):
            body(i, True, i + 1 < NP, i + 2 < NP)

    with nc.Block() as block:
        @block.sync
        def _(sp):
            def load(i, s):
                bb = bass.ds(2 * i + s + b0, 1)
                sp.dma_start(CT[s][:, :], d["ctxT"][bb, :, :].rearrange("o p n -> (o p) n")
                             ).then_inc(S[f"ctx_in{s}"].sem, 16)
                if values:
                    return
                sp.dma_start(CN[s][:, :, :].rearrange("p j n -> p (j n)"),
                             d["ctxN"][bb, :, :].rearrange("o p n -> (o p) n")
                             ).then_inc(S[f"ctx_in{s}"].sem, 16)

            def invert(i, s):
                sp.wait_ge(*at("u_copied", 2 * i + s + 2))
                sp.dma_start(dn[:, :], UE[DC:KA, :]).then_inc(S["den_out"].sem, 16)
                sp.wait_ge(*at("den_inverted", 2 * i + s + 1))
                sp.dma_start(RC[DC:KA, :], dr[:, :]).then_inc(S["den_in"].sem, 16)

            def body(i, prev, nxt, after):
                if prev and not values:
                    invert(i - 1, 1)
                for s in range(2):
                    if nxt:
                        if values:
                            sp.wait_ge(*at("scored", 24 * i + 12 * s + 12))
                        else:
                            sp.wait_ge(*at("weighed", 24 * i + 12 * s + 14))
                        load(i + 1, s)
                    if s == 0 and not values:
                        invert(i, 0)

            for s in range(2):
                load(0, s)
            pairs(sp, body)
            if not values:
                invert(NP - 1, 1)

        @block.gpsimd
        def _(pool):
            def first_pass_inputs(i, s):
                nc.gpsimd.tensor_copy(QB[s][:, :], qp[0:KA, bass.ds(2 * i + s, 1), :]
                                      .rearrange("p o n -> p (o n)")).then_inc(S[f"qb_ready{s}"].sem, 1)
                pool.dma_start(CR[s][:, :], d["ctxT"][bass.ds(2 * i + s + b0, 1), 0:KA, :]
                               .rearrange("o p n -> (o p) n")).then_inc(S[f"ctr_in{s}"].sem, 16)

            def max_row(i, s):
                pool.wait_ge(*at("max_negated", 2 * i + s + 1))
                pool.dma_start(qp[KA:KM, bass.ds(2 * i + s, 1), :].rearrange("p o n -> p (o n)"),
                               mt[s][:, :]).then_inc(S[f"max_in{s}"].sem, 16)

            if clip is not None:
                nc.gpsimd.memset(sel[:, :], 1.0).then_inc(S["sel_ready"].sem, 1)
                pool.wait_ge(*at("sel_ready", 1))
                nc.gpsimd.affine_select(out=sel[:, :], in_=sel[:, :], compare_op=ALU.is_ge, fill=0.0,
                                        base=-(KM - 1), pattern=[[0, 128]],
                                        channel_multiplier=1).then_inc(S["sel_ready"].sem, 1)
            if keep_max:
                for s in range(2):
                    first_pass_inputs(0, s)
                for s in range(2):
                    pool.wait_ge(*at("chunk_scored", 12 * s + 12))
                    first_pass_inputs(1, s)
                max_row(0, 0)

            def body(i, prev, nxt, after):
                max_row(i, 1)
                if after:
                    pool.wait_ge(*at("chunk_scored", 24 * i + 36))
                    first_pass_inputs(i + 2, 0)
                if nxt:
                    max_row(i + 1, 0)
                if after:
                    pool.wait_ge(*at("chunk_scored", 24 * i + 48))
                    first_pass_inputs(i + 2, 1)

            if keep_max:
                pairs(pool, body, 2)

        @block.tensor
        def _(pe):
            def chunks(i, s, k):
                if k == 0:
                    pe.wait_ge(*at(f"ctr_in{s}", 16 * i + 16))
                    pe.wait_ge(*at(f"qb_ready{s}", i + 1))
                pe.wait_ge(*at("chunk_maxed", 24 * i + 12 * s + k))
                for a in range(2):
                    t, c = (2 * k + a) // 3, (2 * k + a) % 3
                    mm = nc.tensor.matmul(ps[0:TT, 6 + a, 0:500], QB[s][:, t * TT:(t + 1) * TT],
                                          CR[s][:, c * 500:(c + 1) * 500], start=True, stop=True)
                mm.then_inc(S["chunk_scored"].sem, 1)

            def turn_max(i, s):
                pe.wait_ge(*at("max_ready", 2 * i + s + 1))
                nc.tensor.transpose(ps[0:8, 6, 0:TT], mc[s][:, :], core.ident[0:TT, 0:TT]
                                    ).then_inc(S["max_turned"].sem, 1)

            def spread_low(i, s):
                pe.wait_ge(*at(f"max_in{s}", 16 * i + 16))
                for a in range(2):
                    mm = nc.tensor.matmul(ps[0:KP, 6 + a, 0:HALF], sel[:, 0:KP], query(i, s, a, KM),
                                          start=True, stop=True)
                mm.then_inc(S["low_spread"].sem, 1)

            def spread_den(i, s):
                pe.wait_ge(*at("den_in", 32 * i + 16 * s + 16))
                for a in range(2):
                    mm = nc.tensor.matmul(ps[0:KA, 6 + a, 0:HALF], core.ones[DC:KA, 0:KA],
                                          RC[DC:KA, a * HALF:(a + 1) * HALF], start=True, stop=True)
                mm.then_inc(S["den_spread"].sem, 1)

            def project(i):
                pe.wait_ge(*at("u_normed", 2 * i + 3))
                for h in range(H):
                    mm = nc.tensor.matmul(ps[:, 6, 0:2 * NQ], N[:, h, :],
                                          UN[:, h, :, :].rearrange("p s q -> p (s q)"),
                                          start=(h == 0), stop=(h == H - 1))
                mm.then_inc(S["projected"].sem, 1)

            def columns(t, j):
                return t.rearrange("p (s r j q) -> p (s r) j q", s=2, j=2, q=NQ)[:, :, j, :]

            def spread_sums(i, is_last=False):
                pe.wait_ge(*at("values_copied", 8 * i + 8 + (1 if is_last else 5)))
                pe.wait_ge(*at("u_copied", 2 * i + 3))
                for j in range(2):
                    mm = nc.tensor.matmul(columns(ps[:, 5, 0:2 * QV], j), core.sum_row[:, j, :],
                                          columns(UE[:, :, :].rearrange("p s n -> p (s n)"), j),
                                          start=True, stop=True)
                mm.then_inc(S["den_spread"].sem, 1)

            def project_sums(i):
                pe.wait_ge(*at("u_normed", i + 2))
                n = UN[:, :, :].rearrange("p s (r j q) -> p s r j q", j=2, q=NQ)
                for c in range(4):
                    mm = nc.tensor.matmul(ps[:, 5, 0:2 * NQ].rearrange("p (s q) -> p s q", s=2),
                                          WOE[:, c, :], n[:, :, c // 2, c % 2, :],
                                          start=(c == 0), stop=(c == 3))
                mm.then_inc(S["projected"].sem, 1)

            def make_values(i, s, g):
                if g == 0:
                    pe.wait_ge(*at(f"ctx_in{s}", 16 * i + 16))
                pe.wait_ge(*at("values_copied", 8 * i + 4 * s + g + 1))
                for t in range(3):
                    j = 3 * g + t
                    mm = nc.tensor.matmul(ps[0:KP, 5, t * H // 2 * VW:(t + 1) * H // 2 * VW],
                                          CT[s][0:KA, j * KP:(j + 1) * KP], WVE[:, :],
                                          start=True, stop=True)
                mm.then_inc(S["values_made"].sem, 1)

            def bank5(i, k, prev, nxt):
                if k == 1 and prev:
                    spread_sums(i - 1)
                if k == 4 and prev:
                    project_sums(i - 1)
                if k == 7 and prev:
                    pe.wait_ge(*at("out_copied", i))
                if k in NEXT_VALUES:
                    make_values(i, 1, NEXT_VALUES.index(k))
                if k in FIRST_VALUES and nxt:
                    make_values(i + 1, 0, FIRST_VALUES.index(k))

            def score(i, n):
                s, j = n // KT, n % KT
                if j == 0:
                    n_in = 16 if values else 32
                    pe.wait_ge(*at(f"ctx_in{s}", n_in * i + n_in))
                    if keep_max:
                        pe.wait_ge(*at(f"max_in{s}", 16 * i + 16))
                pe.wait_ge(*at("exped" if clip is None else "clipped", 24 * i + n + 1))
                for a in range(2):
                    mm = nc.tensor.matmul(SB[n % 2][:, a, :], CT[s][0:KS, j * KP:(j + 1) * KP],
                                          query(i, s, a, KS), start=True, stop=True)
                mm.then_inc(S["scored"].sem, 1)

            def weigh(i, n):
                s, j = n // KT, n % KT
                pe.wait_ge(*at("exped", 24 * i + n + 3))
                if j == 0:
                    pe.wait_ge(*at("u_copied", 2 * i + s + 1))
                if values:
                    if j % 3 == 0:
                        pe.wait_ge(*at("values_copied", 8 * i + 4 * s + j // 3 + 2))
                    for m in range(H // 2):
                        g, c = m % 4, m // 4 * 2 * NQ
                        mm = nc.tensor.matmul(U[32 * g:32 * g + 32, c:c + 2 * NQ], VS[s][:, j, m, :],
                                              P[:, n % 2, m * 2 * NQ:(m + 1) * 2 * NQ],
                                              start=(j == 0 and m < 4), stop=(j == KT - 1 and m >= 4))
                    mm.then_inc(S["weighed"].sem, 1)
                    return
                for a in range(2):
                    mm = nc.tensor.matmul(U[:, a, :], CN[s][:, j, :], P[:, n % 2, a * HALF:(a + 1) * HALF],
                                          start=(j == 0), stop=(j == KT - 1))
                mm.then_inc(S["weighed"].sem, 1)

            def settled(i, k, prev, nxt):
                if k == 0 and keep_max:
                    pe.wait_ge(*at("max_negated", 2 * i + 2))
                if k == 4 and prev and not values:
                    pe.wait_ge(*at("u_normed", 2 * i + 1))
                if k == 6 and prev and not values:
                    pe.wait_ge(*at("out_copied", i))
                if k == 8 and clip is not None:
                    pe.wait_ge(*at("low_ready", 2 * i + 2))
                if k == 12 and nxt and keep_max:
                    pe.wait_ge(*at("max_negated", 2 * i + 3))
                if k == 17 and not values:
                    pe.wait_ge(*at("u_normed", 2 * i + 2))
                if k == 19 and nxt and clip is not None:
                    pe.wait_ge(*at("low_ready", 2 * i + 3))

            ASIDE = (0, 4, 6, 8, 12, 17, 19)

            def aside(i, k, prev, nxt):
                if k not in ASIDE:
                    return
                if keep_max and nxt:
                    pe.wait_ge(*at("chunk_maxed", 24 * i + 24 + k + 1))
                elif k != 0:
                    settled(i, ASIDE[ASIDE.index(k) - 1], prev, nxt)
                if k == 0 and keep_max:
                    turn_max(i, 1)
                if k == 4 and prev and not values:
                    spread_den(i - 1, 1)
                if k == 6 and prev and not values:
                    project(i - 1)
                if k == 8 and clip is not None:
                    spread_low(i, 1)
                if k == 12 and nxt and keep_max:
                    turn_max(i + 1, 0)
                if k == 17 and not values:
                    spread_den(i, 0)
                if k == 19 and nxt and clip is not None:
                    spread_low(i + 1, 0)

            def body(i, prev, nxt, after):
                score(i, 0)
                score(i, 1)
                for k in range(24):
                    weigh(i, k)
                    if keep_max and nxt:
                        if k:
                            settled(i, k - 1, prev, nxt)
                        chunks(i + 1, k // 12, k % 12)
                    if k + 2 < 24:
                        score(i, k + 2)
                    aside(i, k, prev, nxt)
                    if values:
                        bank5(i, k, prev, nxt)

            if keep_max:
                for k in range(24):
                    chunks(0, k // 12, k % 12)
                pe.wait_ge(*at("chunk_maxed", 24))
                turn_max(0, 0)
                if clip is not None:
                    pe.wait_ge(*at("sel_ready", 2))
                    pe.wait_ge(*at("max_negated", 1))
                    spread_low(0, 0)
                    pe.wait_ge(*at("low_ready", 1))
                pe.wait_ge(*at("max_negated", 1))
            if values:
                for g in range(4):
                    make_values(0, 0, g)
            pairs(pe, body)
            if values:
                spread_sums(NP - 1, True)
                project_sums(NP - 1)
            else:
                pe.wait_ge(*at("u_normed", 2 * NP))
                spread_den(NP - 1, 1)
                project(NP - 1)

        @block.scalar
        def _(act):
            act.sem_inc(S["exped"].sem, 2)
            act.sem_inc(S["u_copied"].sem, 1)

            def out(i):
                act.wait_ge(*at("projected", i + 1))
                nc.scalar.activation(core.OT[:, bass.ds((2 * i + b0) * NQ, 2 * NQ)],
                                     ps[:, 5 if values else 6, 0:2 * NQ],
                                     ACT.Identity, bias=bo).then_inc(S["out_copied"].sem, 1)

            def copy_sums(i, s):
                act.wait_ge(*at("weighed", 24 * i + 12 * s + 14))
                if values:
                    act.wait_ge(*at("u_normed", i + 1))
                    nc.scalar.activation(UE[:, s, :], U, ACT.Copy).then_inc(S["u_copied"].sem, 1)
                    return
                act.wait_ge(*at("u_normed", 2 * i + s + 1))
                nc.scalar.activation(two(UE[:, :]), U, ACT.Copy).then_inc(S["u_copied"].sem, 1)

            def body(i, prev, nxt, after):
                for n in range(24):
                    if n == 9 and prev:
                        out(i - 1)
                    if n == 13:
                        copy_sums(i, 0)
                    if clip is None:
                        act.wait_ge(*at("scored", 24 * i + n + 1))
                    else:
                        act.wait_ge(*at("clipped", 24 * i + n + 3))
                    act.wait_ge(*at("weighed", 24 * i + n + 1))
                    sc = 1.0 if rk is None else rk[:, bass.ds(24 * i + n + b0 * KT, 1)]
                    src = two(P[:, n % 2, :]) if clip is not None else SB[n % 2]
                    nc.scalar.activation(two(P[:, n % 2, :]), src, ACT.Exp,
                                         scale=sc).then_inc(S["exped"].sem, 1)
                copy_sums(i, 1)

            pairs(act, body)
            out(NP - 1)

        @block.vector
        def _(dve):
            dve.sem_inc(S["weighed"].sem, 2)
            dve.sem_inc(S["u_normed"].sem, 1)

            def chunk_max(i, s, k):
                dve.wait_ge(*at("chunk_scored", 24 * i + 12 * s + k + 1))
                nc.vector.tensor_reduce(mp[:, 2 * k:2 * k + 2], ps[0:TT, 6:8, 0:500],
                                        AX.X, ALU.max).then_inc(S["chunk_maxed"].sem, 1)
                if k < 11:
                    return
                dve.wait_ge(*at("chunk_maxed", 24 * i + 12 * s + 12))
                m3 = mp[:, :].rearrange("p (t c) -> p t c", c=3)
                if clip is None:
                    nc.vector.tensor_reduce(mc[s][:, :], m3, AX.X, ALU.max).then_inc(S["max_ready"].sem, 1)
                else:
                    nc.vector.tensor_reduce(mu[:, :], m3, AX.X, ALU.max).then_inc(S["clip_max"].sem, 1)
                    dve.wait_ge(*at("clip_max", 2 * i + s + 1))
                    nc.vector.tensor_scalar(mc[s][:, :], mu[:, :], clip, -clip, ALU.min,
                                            ALU.max).then_inc(S["max_ready"].sem, 1)
                dve.wait_ge(*at("max_ready", 2 * i + s + 1))

            def turned(i, s):
                dve.wait_ge(*at("max_turned", 2 * i + s + 1))
                nc.vector.tensor_scalar(mt[s][:, :], ps[0:8, 6, 0:TT], -1.0, None,
                                        ALU.mult).then_inc(S["max_negated"].sem, 1)

            def low(i, s):
                dve.wait_ge(*at("low_spread", 2 * i + s + 1))
                nc.vector.tensor_scalar(two(LB[s][:, :]), ps[0:KP, 6:8, 0:HALF], -clip, None,
                                        ALU.add).then_inc(S["low_ready"].sem, 1)

            def clip_tile(i, n):
                dve.wait_ge(*at("scored", 24 * i + n + 1))
                dve.wait_ge(*at("weighed", 24 * i + n + 1))
                if n % KT == 0:
                    dve.wait_ge(*at("low_ready", 2 * i + n // KT + 1))
                nc.vector.scalar_tensor_tensor(out=two(P[:, n % 2, :]), in0=SB[n % 2], scalar=0.0,
                                               in1=two(LB[n // KT][:, :]), op0=ALU.min,
                                               op1=ALU.max).then_inc(S["clipped"].sem, 1)

            def invert(i, s):
                dve.wait_ge(*at("den_out", 32 * i + 16 * s + 16))
                nc.vector.reciprocal(dr[:, :], dn[:, :]).then_inc(S["den_inverted"].sem, 1)

            def norm(i, s):
                dve.wait_ge(*at("den_spread", 2 * i + s + 1))
                for a in range(2):
                    ins = nc.vector.tensor_tensor(UN[:, a * 8:(a + 1) * 8, s, :],
                                                  heads(UE[:, a * HALF:(a + 1) * HALF]),
                                                  heads(ps[0:KA, 6 + a, 0:HALF]), ALU.mult)
                ins.then_inc(S["u_normed"].sem, 1)

            def norm_sums(i):
                dve.wait_ge(*at("den_spread", i + 1))
                nc.vector.reciprocal(RD[:, :, :].rearrange("p s n -> p (s n)"), ps[:, 5, 0:2 * QV]
                                     ).then_inc(S["den_inverted"].sem, 1)
                dve.wait_ge(*at("den_inverted", i + 1))
                nc.vector.tensor_tensor(UN[:, :, :], UE[:, :, :], RD[:, :, :], ALU.mult
                                        ).then_inc(S["u_normed"].sem, 1)
                if clip is not None:
                    nc.vector.tensor_tensor(eq[:, :, :], RD[:, :, :], RD[:, :, :],
                                            ALU.is_equal).then_inc(S["nan_seen"].sem, 1)
                    dve.wait_ge(*at("nan_seen", 2 * i + 1))
                    nc.vector.tensor_tensor(ok[:, :], ok[:, :], eq[:, :, :].rearrange("p s n -> p (s n)"),
                                            ALU.mult).then_inc(S["nan_seen"].sem, 1)
                    dve.wait_ge(*at("nan_seen", 2 * i + 2))

            def copy_values(i, s, g):
                dve.wait_ge(*at("values_made", 8 * i + 4 * s + g + 1))
                w = H // 2 * VW
                nc.vector.tensor_copy(VS[s][:, 3 * g:3 * g + 3, :, 0:VW],
                                      ps[0:KP, 5, 0:3 * w].rearrange("p (t m c) -> p t m c", t=3, c=VW)
                                      ).then_inc(S["values_copied"].sem, 1)

            def body(i, prev, nxt, after):
                if clip is not None:
                    clip_tile(i, 0)
                    clip_tile(i, 1)
                for k in range(24):
                    if keep_max and nxt:
                        chunk_max(i + 1, k // 12, k % 12)
                    if clip is not None and k + 2 < 24:
                        clip_tile(i, k + 2)
                    if k == 0 and keep_max:
                        turned(i, 1)
                    if k == 8 and clip is not None:
                        low(i, 1)
                    if k == 12 and nxt and keep_max:
                        turned(i + 1, 0)
                    if k == 19 and nxt and clip is not None:
                        low(i + 1, 0)
                    if values:
                        if k == 2 and prev:
                            norm_sums(i - 1)
                        if k in NEXT_VALUES:
                            copy_values(i, 1, NEXT_VALUES.index(k))
                        if k in FIRST_VALUES and nxt:
                            copy_values(i + 1, 0, FIRST_VALUES.index(k))
                        continue
                    if k == 2 and prev:
                        invert(i - 1, 1)
                    if k == 4 and prev:
                        norm(i - 1, 1)
                    if k == 14:
                        invert(i, 0)
                    if k == 17:
                        norm(i, 0)

            if clip is not None:
                dve.sem_inc(S["clipped"].sem, 2)
            if keep_max:
                for k in range(24):
                    chunk_max(0, k // 12, k % 12)
                turned(0, 0)
                if clip is not None:
                    low(0, 0)
            if values:
                dve.sem_inc(S["values_copied"].sem, 1)
                for g in range(4):
                    copy_values(0, 0, g)
            pairs(dve, body)
            if values:
                norm_sums(NP - 1)
            else:
                invert(NP - 1, 1)
                norm(NP - 1, 1)

    for counts in (ATTEND, ATTEND_FEW if values else ATTEND_WIDE, ATTEND_MAX if keep_max else {}, ATTEND_CLIP if clip is not None else {}):
        for name, n in counts.items():
            S[name].base += n


def uniform_if_nan(core, L, N, okays, csum, bo, ctx):
    nc, ps = core.nc, core.ps
    ok = core.sb(f"{L}_row_ok", [128, 1], F32, ctx)
    row_bad = core.sb(f"{L}_row_bad", [128, 1], F32, ctx)
    bad = core.sb(f"{L}_bad", [128, 1], F32, ctx)
    badT = core.sb(f"{L}_badT", [D, T], I32, ctx)
    cm = core.sb(f"{L}_cm", [KA, B], F32, ctx)
    uo = core.sb(f"{L}_uo", [D, B], F32, ctx)
    uT = core.sb(f"{L}_uT", [D, T], F32, ctx)
    reduced, spread = core.sig(f"{L}_ok_reduced"), core.sig(f"{L}_ok_spread")
    with nc.Block() as block:
        @block.vector
        def _(dve):
            link = core.linker(dve, "dve")
            link(nc.vector.tensor_reduce(ok[:, :], okays[:, :], AX.X, ALU.min))
            nc.vector.tensor_scalar(row_bad[:, :], ok[:, :], -1.0, 1.0, ALU.mult, ALU.add).then_inc(reduced.sem, 1)
            nc.vector.tensor_scalar(cm[:, :], csum[:, :], 1.0 / NK, None, ALU.mult).then_inc(reduced.sem, 1)
            dve.wait_ge(spread.sem, 2)
            link(nc.vector.tensor_copy(bad[:, :], ps[:, 0, 0:1]))
            link(nc.vector.tensor_scalar(uo[:, :], ps[:, 1, 0:B], bo, None, ALU.add))
            link(nc.vector.tensor_copy(badT[:, :], bad[:, 0:1].to_broadcast([D, T])))
            link(nc.vector.tensor_copy(uT[:, :].rearrange("p (b q) -> p b q", q=NQ),
                                       uo[:, :].unsqueeze(2).to_broadcast([D, B, NQ])))
            link(nc.vector.copy_predicated(core.OT[:, :], badT[:, :], uT[:, :]))

        @block.tensor
        def _(pe):
            pe.wait_ge(reduced.sem, 2)
            nc.tensor.matmul(ps[:, 0, 0:1], core.ones[:, :], row_bad[:, :], start=True,
                             stop=True).then_inc(spread.sem, 1)
            for h in range(H):
                mm = nc.tensor.matmul(ps[:, 1, 0:B], N[:, h, :], cm[:, :], start=(h == 0), stop=(h == H - 1))
            mm.then_inc(spread.sem, 1)


def top_choice(link, nc, V, im, value, index, hot, tmp, shape, last):
    p, n, e = shape
    link(nc.vector.tensor_reduce(value, V, AX.X, ALU.max))
    link(nc.vector.tensor_tensor(tmp, V, value.unsqueeze(2).to_broadcast([p, n, e]), ALU.is_equal))
    link(nc.vector.tensor_tensor(tmp, tmp, im, ALU.mult))
    link(nc.vector.tensor_reduce(index, tmp, AX.X, ALU.min))
    link(nc.vector.tensor_tensor(hot, im, index.unsqueeze(2).to_broadcast([p, n, e]), ALU.is_equal))
    if not last:
        link(nc.vector.scalar_tensor_tensor(out=V, in0=hot, scalar=-1e30, in1=V, op0=ALU.mult, op1=ALU.add))


def experts0(core, gate):
    nc, d, ps = core.nc, core.d, core.ps
    R = E0 * CAP
    buf = nc.dram_tensor("moe_in", (R, D), F32).ap()
    ydr = nc.dram_tensor("moe_out", (R, D), F32).ap()
    C4 = HID0 // 128
    with ExitStack() as ctx:
        def sb(n, shape, dt=F32, c=ctx):
            return core.sb(f"moe_{n}", shape, dt, c)
        gat = [sb(f"gate{k}", [TT, NT]) for k in range(TOPK0)]
        row = [sb(f"row{k}", [TT, NT], I32) for k in range(TOPK0)]
        NS = 4
        w1 = sb("w1", [D, NS, 2, HID0])
        w2 = sb("w2", [D, NS, 2, HID0])
        b2 = sb("b2", [1, NS, 2, D])
        b1 = sb("b1", [D, E0, C4])
        wt_in = [core.sig(f"moe_wt_in{s}") for s in range(NS)]

        def load_weights(eng, e2, s):
            for src, dst in ((d["L0_w1"], w1), (d["L0_w2"], w2), (d["L0_b2"], b2)):
                eng.dma_start(dst[:, s, :, :], src[bass.ds(e2, 1)].rearrange("o p e n -> (o p) e n")
                              ).then_inc(wt_in[s].sem, 16)

        with ExitStack() as c1:
            gw, gb = sb("gw", [D, E0], c=c1), sb("gb", [TT, E0], c=c1)
            xnn = sb("xnn", [TT, NT, D], c=c1)
            V, im, tmp, mask, cum = (sb(n, [TT, NT, E0], c=c1) for n in ("V", "im", "tmp", "mask", "cum"))
            hot = [sb(f"hot{k}", [TT, NT, E0], c=c1) for k in range(TOPK0)]
            imi = sb("imi", [TT, E0], I32, c=c1)
            tri = sb("tri", [TT, TT], c=c1)
            zero = sb("zero", [128, R * D // 128 // 4], c=c1)
            val = [sb(f"val{k}", [TT, NT], c=c1) for k in range(TOPK0)]
            idx = [sb(f"idx{k}", [TT, NT], c=c1) for k in range(TOPK0)]
            slot, ok, rf, den = (sb(n, [TT, NT], c=c1) for n in ("slot", "ok", "rf", "den"))
            put = [sb(f"put{k}", [TT, NT], I32, c=c1) for k in range(TOPK0)]
            names = ["gw_in", "zeroed", "buf_zeroed", "turned", "logits", "iota", "tri_ready",
                     "rows_copied", "routed", "counted", "exp_in", "exp_out", "put_ready", "scattered"]
            S = {n: core.sig(f"moe_{n}").sem for n in names}
            shp = (TT, NT, E0)
            with nc.Block() as block:
                @block.sync
                def _(sp):
                    sp.dma_start(gw[:, :], d["L0_gw"]).then_inc(S["gw_in"], 16)
                    sp.dma_start(gb[:, :], d["L0_gb"]).then_inc(S["gw_in"], 16)
                    sp.dma_start(b1[:, :, :], d["L0_b1"]).then_inc(S["gw_in"], 16)
                    sp.wait_ge(S["zeroed"], 1)
                    for q in range(4):
                        sp.dma_start(buf[q * R // 4:(q + 1) * R // 4, :].rearrange("(p r) n -> p (r n)", p=128),
                                     zero[:, :]).then_inc(S["buf_zeroed"], 16)
                    for s in range(NS):
                        load_weights(sp, s, s)
                    sp.wait_ge(S["gw_in"], 48)

                @block.tensor
                def _(pe):
                    pe.wait_ge(S["gw_in"], 48)
                    for t in range(NT):
                        nc.tensor.matmul(ps[0:TT, t // 8, (t % 8) * E0:(t % 8 + 1) * E0],
                                         core.xn[:, t * TT:(t + 1) * TT], gw[:, :],
                                         start=True, stop=True).then_inc(S["logits"], 1)
                    for t in range(NT):
                        nc.tensor.transpose(ps[0:TT, 2 + t // 4, (t % 4) * D:(t % 4 + 1) * D],
                                            core.xn[:, t * TT:(t + 1) * TT],
                                            core.ident[:, :]).then_inc(S["turned"], 1)
                    pe.wait_ge(S["routed"], 1)
                    pe.wait_ge(S["tri_ready"], 2)
                    for a in range(2):
                        for lhs, rhs in ((tri[:, :], mask), (core.ones[0:TT, 0:TT], cum)):
                            mm = nc.tensor.matmul(ps[0:TT, a, :], lhs, rhs[:, 8 * a:8 * a + 8, :]
                                                  .rearrange("p t e -> p (t e)"),
                                                  start=(rhs is mask), stop=(rhs is cum))
                    mm.then_inc(S["counted"], 1)

                @block.scalar
                def _(act):
                    act.wait_ge(S["turned"], NT)
                    nc.scalar.activation(xnn[:, :, :].rearrange("p t n -> p (t n)"),
                                         ps[0:TT, 2:6, :].rearrange("p b n -> p (b n)"),
                                         ACT.Copy).then_inc(S["rows_copied"], 1)
                    act.wait_ge(S["exp_in"], 1)
                    for k in range(TOPK0):
                        nc.scalar.activation(gat[k][:, :], gat[k][:, :], ACT.Exp).then_inc(S["exp_out"], 1)

                @block.gpsimd
                def _(pool):
                    nc.gpsimd.memset(zero[:, :], 0.0).then_inc(S["zeroed"], 1)
                    nc.gpsimd.iota(imi[:, :], pattern=[[1, E0]], base=-E0,
                                   channel_multiplier=0).then_inc(S["iota"], 1)
                    nc.gpsimd.memset(tri[:, :], 1.0).then_inc(S["tri_ready"], 1)
                    pool.wait_ge(S["tri_ready"], 1)
                    nc.gpsimd.affine_select(out=tri[:, :], in_=tri[:, :], compare_op=ALU.is_gt, fill=0.0,
                                            base=0, pattern=[[1, TT]],
                                            channel_multiplier=-1).then_inc(S["tri_ready"], 1)
                    pool.wait_ge(S["rows_copied"], 1)
                    pool.wait_ge(S["put_ready"], 1)
                    pool.wait_ge(S["buf_zeroed"], 64)
                    for k in range(TOPK0):
                        for t in range(NT):
                            pool.indirect_dma_start(
                                out=buf, out_offset=bass.IndirectOffsetOnAxis(ap=put[k][:, t:t + 1], axis=0),
                                in_=xnn[:, t, :], in_offset=None, bounds_check=R - 1,
                                oob_is_err=False).then_inc(S["scattered"], 16)
                    pool.wait_ge(S["scattered"], 16 * TOPK0 * NT)

                @block.vector
                def _(dve):
                    link = core.linker(dve, "dve")
                    dve.wait_ge(S["iota"], 1)
                    link(nc.vector.tensor_copy(im[:, :, :], imi[:, :].unsqueeze(1).to_broadcast([TT, NT, E0])))
                    dve.wait_ge(S["logits"], NT)
                    link(nc.vector.tensor_tensor(V[:, :, :], ps[0:TT, 0:2, :].rearrange(
                        "p b (t e) -> p (b t) e", e=E0), gb[:, :].unsqueeze(1).to_broadcast([TT, NT, E0]),
                        ALU.add))
                    for k in range(TOPK0):
                        top_choice(link, nc, V[:, :, :], im[:, :, :], val[k][:, :], idx[k][:, :],
                                   hot[k][:, :, :], tmp[:, :, :], shp, k == TOPK0 - 1)
                    link(nc.vector.tensor_tensor(mask[:, :, :], hot[0][:, :, :], hot[1][:, :, :], ALU.add))
                    link(nc.vector.tensor_tensor(mask[:, :, :], mask[:, :, :], hot[2][:, :, :], ALU.add))
                    link(nc.vector.memset(cum[:, 0, :], 0.0))
                    for t in range(1, NT):
                        link(nc.vector.tensor_tensor(cum[:, t, :], cum[:, t - 1, :], mask[:, t - 1, :], ALU.add))
                    nc.vector.tensor_copy(tmp[:, 0, 0:1], cum[:, 0, 0:1]).then_inc(S["routed"], 1)
                    for k in range(TOPK0):
                        link(nc.vector.tensor_tensor(gat[k][:, :], val[k][:, :], val[0][:, :], ALU.subtract))
                    nc.vector.tensor_copy(tmp[:, 0, 1:2], cum[:, 0, 0:1]).then_inc(S["exp_in"], 1)
                    dve.wait_ge(S["exp_out"], TOPK0)
                    link(nc.vector.tensor_tensor(den[:, :], gat[0][:, :], gat[1][:, :], ALU.add))
                    link(nc.vector.tensor_tensor(den[:, :], den[:, :], gat[2][:, :], ALU.add))
                    link(nc.vector.reciprocal(den[:, :], den[:, :]))
                    dve.wait_ge(S["counted"], 1)
                    for k in range(TOPK0):
                        link(nc.vector.tensor_tensor(tmp[:, :, :], hot[k][:, :, :], ps[0:TT, 0:2, :].rearrange(
                            "p b (t e) -> p (b t) e", e=E0), ALU.mult))
                        link(nc.vector.tensor_reduce(slot[:, :], tmp[:, :, :], AX.X, ALU.add))
                        link(nc.vector.tensor_scalar(ok[:, :], slot[:, :], float(CAP), None, ALU.is_lt))
                        link(nc.vector.tensor_tensor(gat[k][:, :], gat[k][:, :], den[:, :], ALU.mult))
                        link(nc.vector.tensor_tensor(gat[k][:, :], gat[k][:, :], ok[:, :], ALU.mult))
                        link(nc.vector.tensor_scalar(rf[:, :], idx[k][:, :], float(E0), float(CAP), ALU.add,
                                                     ALU.mult))
                        link(nc.vector.tensor_tensor(rf[:, :], rf[:, :], slot[:, :], ALU.add))
                        link(nc.vector.tensor_tensor(rf[:, :], rf[:, :], ok[:, :], ALU.mult))
                        link(nc.vector.tensor_copy(row[k][:, :], rf[:, :]))
                        link(nc.vector.tensor_scalar(ok[:, :], ok[:, :], -float(R), float(R), ALU.mult, ALU.add))
                        link(nc.vector.tensor_tensor(rf[:, :], rf[:, :], ok[:, :], ALU.add))
                        link(nc.vector.tensor_copy(put[k][:, :], rf[:, :]))
                    nc.vector.tensor_copy(tmp[:, 0, 2:3], cum[:, 0, 0:1]).then_inc(S["put_ready"], 1)

        with ExitStack() as c2:
            xr = sb("xr", [2 * CAP, NS, D], c=c2)
            xb = sb("xb", [D, 2, 2 * CAP], c=c2)
            hb = sb("hb", [D, 2, 2 * C4, CAP], c=c2)
            hg = sb("hg", [D, 2, 2 * C4, CAP], c=c2)
            ys = sb("ys", [2 * CAP, 2, D], c=c2)
            names = [f"x_in{s}" for s in range(NS)] + ["y_out0", "y_out1",
                     "x_turned", "x_ready", "h_ready", "biased", "gelued", "y_ready", "y_copied"]
            S = {n: core.sig(f"moe_{n}").sem for n in names}
            NP = E0 // 2

            def load_rows(sp, e2, s):
                sp.dma_start(xr[:, s, :], buf[bass.ds(e2 * 2 * CAP, 2 * CAP), :]).then_inc(S[f"x_in{s}"], 16)

            with nc.Block() as block:
                @block.sync
                def _(sp):
                    for s in range(NS):
                        load_rows(sp, s, s)
                    with sp.Fori(0, NP // NS - 1) as i:
                        for s in range(NS):
                            sp.wait_ge(S["y_ready"], NS * i + s + 1)
                            load_rows(sp, NS * (i + 1) + s, s)
                            load_weights(sp, NS * (i + 1) + s, s)

                @block.tensor
                def _(pe):
                    with pe.Fori(0, NP // NS) as i:
                        def turn_and_lift(k):
                            pe.wait_ge(S[f"x_in{k}"], 16 * i + 16)
                            pe.wait_ge(S["x_ready"], NS * i + k + 1)
                            nc.tensor.transpose(ps[:, k % 2, 0:2 * CAP], xr[:, k, :],
                                                core.ident[:, :]).then_inc(S["x_turned"], 1)
                            pe.wait_ge(wt_in[k].sem, 48 * i + 48)
                            pe.wait_ge(S["x_ready"], NS * i + k + 3)
                            pe.wait_ge(S["biased"], NS * i + k + 1)
                            for e in range(2):
                                for c in range(C4):
                                    n = e * C4 + c
                                    mm = nc.tensor.matmul(ps[:, 2 + k % 2, n * CAP:(n + 1) * CAP],
                                                          w1[:, k, e, c:HID0:C4],
                                                          xb[:, k % 2, e * CAP:(e + 1) * CAP],
                                                          start=True, stop=True)
                            mm.then_inc(S["h_ready"], 1)

                        def lower(k):
                            pe.wait_ge(S["gelued"], NS * i + k + 1)
                            pe.wait_ge(S["y_copied"], NS * i + k + 1)
                            for e in range(2):
                                o = ps[e * CAP:(e + 1) * CAP, 4 + k % 2, 0:D]
                                nc.tensor.matmul(o, core.ones[0:1, 0:CAP], b2[:, k, e, :], start=True, stop=False)
                                for c in range(C4):
                                    mm = nc.tensor.matmul(o, hg[:, k % 2, e * C4 + c, :],
                                                          w2[:, k, e, c * D:(c + 1) * D],
                                                          start=False, stop=(c == C4 - 1))
                            mm.then_inc(S["y_ready"], 1)

                        turn_and_lift(0)
                        for k in range(NS):
                            if k + 1 < NS:
                                turn_and_lift(k + 1)
                            lower(k)

                @block.vector
                def _(dve):
                    dve.sem_inc(S["x_ready"], 2)
                    dve.sem_inc(S["biased"], 2)
                    with dve.Fori(0, NP // NS) as i:
                        for k in range(NS):
                            n = NS * i + k
                            dve.wait_ge(S["x_turned"], n + 1)
                            nc.vector.tensor_copy(xb[:, k % 2, :], ps[:, k % 2, 0:2 * CAP]
                                                  ).then_inc(S["x_ready"], 1)
                            dve.wait_ge(S["h_ready"], n + 1)
                            dve.wait_ge(S["y_copied"], n + 1)
                            nc.vector.tensor_tensor(
                                hb[:, k % 2, :, :], ps[:, 2 + k % 2, :].rearrange("p (n c) -> p n c", c=CAP),
                                b1[:, bass.ds(2 * n, 2), :].rearrange("p e c -> p (e c)").unsqueeze(2)
                                .to_broadcast([D, 2 * C4, CAP]), ALU.add).then_inc(S["biased"], 1)

                @block.scalar
                def _(act):
                    act.sem_inc(S["y_copied"], 2)
                    act.sem_inc(S["y_out0"], 16)
                    act.sem_inc(S["y_out1"], 16)
                    with act.Fori(0, NP // NS) as i:
                        for k in range(NS):
                            n = NS * i + k
                            act.wait_ge(S["biased"], n + 3)
                            nc.scalar.activation(hg[:, k % 2, :, :], hb[:, k % 2, :, :],
                                                 ACT.Gelu).then_inc(S["gelued"], 1)
                            act.wait_ge(S["y_ready"], n + 1)
                            act.wait_ge(S[f"y_out{k % 2}"], 32 * i + 16 * (k // 2) + 16)
                            nc.scalar.activation(ys[:, k % 2, :], ps[:, 4 + k % 2, 0:D],
                                                 ACT.Copy).then_inc(S["y_copied"], 1)
                            act.wait_ge(S["y_copied"], n + 3)
                            act.dma_start(ydr[bass.ds(n * 2 * CAP, 2 * CAP), :], ys[:, k % 2, :]
                                          ).then_inc(S[f"y_out{k % 2}"], 16)
                    act.wait_ge(S["y_out0"], 16 * NP // 2 + 16)
                    act.wait_ge(S["y_out1"], 16 * NP // 2 + 16)

        with ExitStack() as c3:
            yr = [sb(f"yr{k}", [TT, NT, D], c=c3) for k in range(TOPK0)]
            S = {n: core.sig(f"moe_{n}").sem for n in ("gathered0", "gathered1", "gathered2", "mixed",
                                                        "mix_turned")}
            with nc.Block() as block:
                @block.gpsimd
                def _(pool):
                    for k in range(TOPK0):
                        for t in range(NT):
                            pool.indirect_dma_start(
                                out=yr[k][:, t, :], out_offset=None, in_=ydr,
                                in_offset=bass.IndirectOffsetOnAxis(ap=row[k][:, t:t + 1], axis=0),
                                bounds_check=R - 1, oob_is_err=False).then_inc(S[f"gathered{k}"], 16)

                @block.vector
                def _(dve):
                    link = core.linker(dve, "dve")
                    for k in range(TOPK0):
                        dve.wait_ge(S[f"gathered{k}"], 16 * NT)
                        link(nc.vector.tensor_tensor(yr[k][:, :, :], yr[k][:, :, :], gat[k][:, :].unsqueeze(2)
                                                     .to_broadcast([TT, NT, D]), ALU.mult))
                        if k:
                            link(nc.vector.tensor_tensor(yr[0][:, :, :], yr[0][:, :, :], yr[k][:, :, :], ALU.add))
                    nc.vector.tensor_copy(yr[1][:, 0, 0:1], yr[0][:, 0, 0:1]).then_inc(S["mixed"], 1)
                    for g in range(4):
                        dve.wait_ge(S["mix_turned"], g + 1)
                        s = slice(g * CH, (g + 1) * CH)
                        link(nc.vector.scalar_tensor_tensor(
                            out=core.xT[:, s], in0=ps[:, g, 0:CH], scalar=core.tg[:, gate:gate + 1],
                            in1=core.xT[:, s], op0=ALU.mult, op1=ALU.add))

                @block.tensor
                def _(pe):
                    pe.wait_ge(S["mixed"], 1)
                    for t in range(NT):
                        mm = nc.tensor.transpose(ps[:, t // 4, (t % 4) * TT:(t % 4 + 1) * TT], yr[0][:, t, :],
                                                 core.ident[0:TT, 0:TT])
                        if t % 4 == 3:
                            mm.then_inc(S["mix_turned"], 1)


def gated_experts(core, L, n_exp, n_chunk, eps, gate):
    nc, d, ps = core.nc, core.d, core.ps
    EA = n_exp + 1
    with ExitStack() as ctx:
        def sb(n, shape, dt=F32):
            return core.sb(f"{L}f_{n}", shape, dt, ctx)
        wr = sb("wr", [D, n_exp])
        wg, wu, wd = (sb(n, [128, n_chunk, 128]) for n in ("wg", "wu", "wd"))
        ex = sb("ex", [EA, n_chunk, 128])
        V, im, tmp, hot0, hot1 = (sb(n, [TT, NT, n_exp]) for n in ("V", "im", "tmp", "hot0", "hot1"))
        imi = sb("imi", [TT, n_exp], I32)
        comb = sb("comb", [TT, NT, EA])
        combT = sb("combT", [EA, T])
        mx, ix, p0, p1, den = (sb(n, [TT, NT]) for n in ("mx", "ix", "p0", "p1", "den"))
        sg, t1, hh = (sb(n, [128, 2, CH]) for n in ("sg", "t1", "hh"))
        names = ["w_in", "iota", "logits", "shifted", "exped", "combined", "comb_turned", "combT_ready",
                 "lifted", "silued", "gated", "hidden", "lowered", "added"]
        S = {n: core.sig(f"{L}f_{n}").sem for n in names}
        shp = (TT, NT, n_exp)

        def bc(ap):
            return ap.unsqueeze(2).to_broadcast([TT, NT, n_exp])

        with nc.Block() as block:
            @block.sync
            def _(sp):
                for dst, n in ((wr[:, :], "wr"), (ex[:, :, :], "ex"), (wg[:, :, :], "wg"),
                               (wu[:, :, :], "wu"), (wd[:, :, :], "wd")):
                    sp.dma_start(dst, d[f"{L}_{n}"]).then_inc(S["w_in"], 16)
                sp.wait_ge(S["w_in"], 80)

            @block.gpsimd
            def _(pool):
                nc.gpsimd.iota(imi[:, :], pattern=[[1, n_exp]], base=-n_exp,
                               channel_multiplier=0).then_inc(S["iota"], 1)

            @block.tensor
            def _(pe):
                pe.wait_ge(S["w_in"], 80)
                for t in range(NT):
                    mm = nc.tensor.matmul(ps[0:TT, 0, t * n_exp:(t + 1) * n_exp],
                                          core.xn[:, t * TT:(t + 1) * TT], wr[:, :], start=True, stop=True)
                mm.then_inc(S["logits"], 1)
                pe.wait_ge(S["combined"], 1)
                for t in range(NT):
                    mm = nc.tensor.transpose(ps[0:EA, 1 + t // 4, (t % 4) * TT:(t % 4 + 1) * TT],
                                             comb[:, t, :], core.ident[0:TT, 0:TT])
                mm.then_inc(S["comb_turned"], 1)

            @block.scalar
            def _(act):
                act.wait_ge(S["shifted"], 1)
                nc.scalar.activation(V[:, :, :], V[:, :, :], ACT.Exp).then_inc(S["exped"], 1)

            @block.vector
            def _(dve):
                link = core.linker(dve, "dve")
                dve.wait_ge(S["iota"], 1)
                link(nc.vector.tensor_copy(im[:, :, :], imi[:, :].unsqueeze(1).to_broadcast([TT, NT, n_exp])))
                dve.wait_ge(S["logits"], 1)
                lg = ps[0:TT, 0, 0:NT * n_exp].rearrange("p (t e) -> p t e", e=n_exp)
                link(nc.vector.tensor_reduce(mx[:, :], lg, AX.X, ALU.max))
                nc.vector.tensor_tensor(V[:, :, :], lg, bc(mx[:, :]), ALU.subtract).then_inc(S["shifted"], 1)
                dve.wait_ge(S["exped"], 1)
                link(nc.vector.tensor_reduce(den[:, :], V[:, :, :], AX.X, ALU.add))
                link(nc.vector.reciprocal(den[:, :], den[:, :]))
                link(nc.vector.tensor_tensor(V[:, :, :], V[:, :, :], bc(den[:, :]), ALU.mult))
                top_choice(link, nc, V[:, :, :], im[:, :, :], p0[:, :], ix[:, :], hot0[:, :, :],
                           tmp[:, :, :], shp, False)
                top_choice(link, nc, V[:, :, :], im[:, :, :], p1[:, :], ix[:, :], hot1[:, :, :],
                           tmp[:, :, :], shp, True)
                link(nc.vector.tensor_tensor(den[:, :], p0[:, :], p1[:, :], ALU.add))
                link(nc.vector.tensor_scalar(den[:, :], den[:, :], eps, None, ALU.add))
                link(nc.vector.reciprocal(den[:, :], den[:, :]))
                for p, hot in ((p0, hot0), (p1, hot1)):
                    link(nc.vector.tensor_tensor(p[:, :], p[:, :], den[:, :], ALU.mult))
                    link(nc.vector.tensor_tensor(hot[:, :, :], hot[:, :, :], bc(p[:, :]), ALU.mult))
                link(nc.vector.memset(comb[:, :, :], 1.0))
                nc.vector.tensor_tensor(comb[:, :, 0:n_exp], hot0[:, :, :], hot1[:, :, :],
                                        ALU.add).then_inc(S["combined"], 1)
                dve.wait_ge(S["comb_turned"], 1)
                nc.vector.tensor_copy(combT[:, :].rearrange("p (b n) -> p b n", b=4),
                                      ps[0:EA, 1:5, 0:CH]).then_inc(S["combT_ready"], 1)

        feed_forward(core, S, n_chunk, (wg, wu, wd), (sg, t1, hh), gate, ex=ex, combT=combT)


def feed_forward(core, S, n_chunk, weights, bufs, gate, ex=None, combT=None, b1=None, b2=None):
    nc, ps = core.nc, core.ps
    wg, wu, wd = weights
    sg, t1, hh = bufs
    with nc.Block() as block:
        def n_of(i, c):
            return n_chunk * i + c

        def free(i, c):
            odd = n_chunk % 2 == 1 and c == 0
            return n_of(i, c) + (2 if odd else 1)

        @block.tensor
        def _(pe):
            def lift(i, c):
                s = c % 2
                x = core.xn[:, bass.ds(i * CH, CH)]
                pe.wait_ge(S["hidden"], free(i, c))
                mm = nc.tensor.matmul(ps[:, 3 * s, 0:CH], wg[:, c, :], x, start=True, stop=True)
                if wu is not None:
                    nc.tensor.matmul(ps[:, 3 * s + 1, 0:CH], wu[:, c, :], x, start=True, stop=True)
                    mm = nc.tensor.matmul(ps[:, 3 * s + 2, 0:CH], ex[:, c, :], combT[:, bass.ds(i * CH, CH)],
                                          start=True, stop=True)
                mm.then_inc(S["lifted"], 1)

            with pe.Fori(0, NCH) as i:
                lift(i, 0)
                pe.wait_ge(S["added"], i + 1)
                for c in range(n_chunk):
                    if c + 1 < n_chunk:
                        lift(i, c + 1)
                    pe.wait_ge(S["hidden"], n_of(i, c) + 3)
                    mm = nc.tensor.matmul(ps[:, 6, 0:CH], wd[:, c, :], hh[:, c % 2, :], start=(c == 0),
                                          stop=(c == n_chunk - 1))
                    mm.then_inc(S["lowered"], 1)

        @block.scalar
        def _(act):
            if wu is None:
                act.sem_inc(S["hidden"], 2)
            with act.Fori(0, NCH) as i:
                for c in range(n_chunk):
                    s = c % 2
                    act.wait_ge(S["lifted"], n_of(i, c) + 1)
                    if wu is None:
                        act.wait_ge(S["lowered"], free(i, c))
                        nc.scalar.activation(hh[:, s, :], ps[:, 3 * s, 0:CH], ACT.Gelu,
                                             bias=b1[c]).then_inc(S["hidden"], 1)
                    else:
                        act.wait_ge(S["hidden"], free(i, c))
                        nc.scalar.activation(sg[:, s, :], ps[:, 3 * s, 0:CH], ACT.Silu).then_inc(S["silued"], 1)

        @block.vector
        def _(dve):
            dve.sem_inc(S["lowered"], 2)
            dve.sem_inc(S["added"], 1)
            if wu is not None:
                dve.sem_inc(S["hidden"], 2)
            with dve.Fori(0, NCH) as i:
                for c in range(n_chunk):
                    s = c % 2
                    if wu is None:
                        continue
                    dve.wait_ge(S["silued"], n_of(i, c) + 1)
                    nc.vector.tensor_tensor(t1[:, s, :], ps[:, 3 * s + 1, 0:CH], sg[:, s, :],
                                            ALU.mult).then_inc(S["gated"], 1)
                    dve.wait_ge(S["gated"], n_of(i, c) + 1)
                    dve.wait_ge(S["lowered"], free(i, c))
                    nc.vector.tensor_tensor(hh[:, s, :], ps[:, 3 * s + 2, 0:CH], t1[:, s, :],
                                            ALU.mult).then_inc(S["hidden"], 1)
                dve.wait_ge(S["lowered"], n_chunk * i + n_chunk + 2)
                x = core.xT[:, bass.ds(i * CH, CH)]
                o = core.OT[:, bass.ds(i * CH, CH)]
                if b2 is not None:
                    nc.vector.tensor_scalar(o, ps[:, 6, 0:CH], b2, None, ALU.add).then_inc(S["biased2"], 1)
                    dve.wait_ge(S["biased2"], i + 1)
                nc.vector.scalar_tensor_tensor(out=x, in0=ps[:, 6, 0:CH] if b2 is None else o,
                                               scalar=core.tg[:, gate:gate + 1], in1=x,
                                               op0=ALU.mult, op1=ALU.add).then_inc(S["added"], 1)


def binarized_mlp(core, gate):
    nc, d, ps = core.nc, core.d, core.ps
    with ExitStack() as ctx:
        def sb(n, shape):
            return core.sb(f"bin_{n}", shape, F32, ctx)
        w = sb("w", [128, 8, 128])
        sgn = sb("sgn", [128, 8, 128])
        al, al2 = sb("al", [128, 8]), sb("al2", [128, 1])
        wT = sb("wT", [128, 8, 128])
        hh = sb("hh", [128, 2, CH])
        S = {n: core.sig(f"bin_{n}").sem for n in ("w_in", "signed", "binarized", "turned", "lifted",
                                                    "hidden", "lowered", "added", "biased2")}
        with nc.Block() as block:
            @block.sync
            def _(sp):
                sp.dma_start(w[:, 0:4, :], d["L3_w1"]).then_inc(S["w_in"], 16)
                sp.dma_start(w[:, 4:8, :], d["L3_w2"]).then_inc(S["w_in"], 16)

            @block.scalar
            def _(act):
                act.wait_ge(S["w_in"], 32)
                nc.scalar.activation(sgn[:, :, :], w[:, :, :], ACT.Sign).then_inc(S["signed"], 1)

            @block.vector
            def _(dve):
                link = core.linker(dve, "dve")
                dve.wait_ge(S["w_in"], 32)
                link(nc.vector.tensor_reduce(al[:, :], w[:, :, :], AX.X, ALU.add, apply_absolute_value=True))
                link(nc.vector.tensor_reduce(al2[:, :], al[:, 4:8], AX.X, ALU.add))
                link(nc.vector.tensor_scalar(al[:, 0:4], al[:, 0:4], 1.0 / D, None, ALU.mult))
                link(nc.vector.tensor_scalar(al2[:, :], al2[:, :], 1.0 / 512, None, ALU.mult))
                dve.wait_ge(S["signed"], 1)
                link(nc.vector.tensor_tensor(sgn[:, 0:4, :], sgn[:, 0:4, :],
                                             al[:, 0:4].unsqueeze(2).to_broadcast([128, 4, 128]), ALU.mult))
                link(nc.vector.tensor_scalar(sgn[:, 4:8, :], sgn[:, 4:8, :], al2[:, 0:1], None, ALU.mult))
                link(nc.vector.tensor_tensor(sgn[:, :, :], sgn[:, :, :], w[:, :, :], ALU.subtract))
                nc.vector.tensor_tensor(w[:, :, :], w[:, :, :], sgn[:, :, :], ALU.add
                                        ).then_inc(S["binarized"], 1)
                dve.wait_ge(S["turned"], 1)
                link(nc.vector.tensor_copy(wT[:, :, :].rearrange("p (a c) n -> p a (c n)", a=2), ps[:, 0:2, :]))

            @block.tensor
            def _(pe):
                pe.wait_ge(S["binarized"], 1)
                for n in range(8):
                    mm = nc.tensor.transpose(ps[:, n // 4, (n % 4) * 128:(n % 4 + 1) * 128], w[:, n, :],
                                             core.ident[:, :])
                mm.then_inc(S["turned"], 1)
        feed_forward(core, S, 4, (wT[:, 0:4, :], None, wT[:, 4:8, :]), (None, None, hh), gate,
                     b1=[v(core, f"ffb1_{c}") for c in range(4)], b2=v(core, "L3_b2"))


BITS = {"d2v": (DC, 1, 128), "img": (128, 1, 128), "txt": (128, 1, 128), "att0": (128, 1, 128),
        "att1": (128, 1, 128), "f1": (128, 2, 512), "f2": (128, 4, 128)}
BIT_COUNT = {"d2v": DC * 128, "img": 128 * 128, "txt": 128 * 128, "att0": 128 * 64, "att1": 128 * 64,
             "f1": 256 * 512, "f2": 512 * 128}
QMAX = 127.0


class Bit:

    def __init__(self, core, ctx):
        self.core, self.ctx = core, ctx
        self.q = {n: core.sb(f"bit_{n}", [p, k, o], BF16, ctx) for n, (p, k, o) in BITS.items()}
        self.ws = core.sb("bit_ws", [128, len(BITS)], F32, ctx)
        self.isc = core.sb("bit_isc", [128, 6], F32, ctx)
        self.inv = core.sb("bit_inv", [128, 6], F32, ctx)
        self.out = core.sb("bit_out", [128, len(BITS)], F32, ctx)
        self.magic = core.sb("bit_magic", [128, 1], F32, ctx)
        self.small = core.sb("bit_small", [128, 2], F32, ctx)
        self.turned, self.one, self.spread = (core.sig(f"bit_{n}") for n in ("turned", "one", "spread"))

    def weight(self, n):
        return list(BITS).index(n)


def quantize_weights(core, bit):
    nc, d, ps = core.nc, core.d, core.ps
    with ExitStack() as ctx:
        w = {n: core.sb(f"bitw_{n}", [p, k, o], F32, ctx) for n, (p, k, o) in BITS.items()}
        tot = core.sb("bitw_tot", [128, len(BITS)], F32, ctx)
        thr = core.sb("bitw_thr", [128, 2 * len(BITS)], F32, ctx)
        hi = core.sb("bitw_hi", [128, 1024], F32, ctx)
        lo = core.sb("bitw_lo", [128, 1024], F32, ctx)
        w_in, summed, spread = (core.sig(f"bitw_{n}") for n in ("in", "summed", "spread"))
        with nc.Block() as block:
            @block.sync
            def _(sp):
                for n in BITS:
                    sp.dma_start(w[n][:, :, :], d[f"bit_{n}"]).then_inc(w_in.sem, 16)

            @block.tensor
            def _(pe):
                pe.wait_ge(summed.sem, 1)
                nc.tensor.matmul(ps[:, 0, 0:len(BITS)], core.ones[:, :], tot[:, :], start=True,
                                 stop=True).then_inc(spread.sem, 1)

            @block.vector
            def _(dve):
                link = core.linker(dve, "dve")
                dve.wait_ge(w_in.sem, 16 * len(BITS))
                link(nc.vector.memset(tot[:, :], 0.0))
                link(nc.vector.memset(bit.magic[:, :], -MAGIC))
                for i, (n, (p, k, o)) in enumerate(BITS.items()):
                    o = 64 if n.startswith("att") else o
                    link(nc.vector.tensor_reduce(tot[0:p, i:i + 1], w[n][:, :, 0:o], AX.XY, ALU.add,
                                                 apply_absolute_value=True))
                nc.vector.tensor_copy(hi[:, 0:1], tot[:, 0:1]).then_inc(summed.sem, 1)
                dve.wait_ge(spread.sem, 1)
                for i, (n, (p, k, o)) in enumerate(BITS.items()):
                    link(nc.vector.tensor_scalar(bit.ws[:, i:i + 1], ps[:, 0, i:i + 1], 1.0 / BIT_COUNT[n],
                                                 1e-5, ALU.mult, ALU.max))
                    link(nc.vector.tensor_scalar(thr[:, i:i + 1], bit.ws[:, i:i + 1], 0.5, None, ALU.mult))
                    j = len(BITS) + i
                    link(nc.vector.tensor_scalar(thr[:, j:j + 1], bit.ws[:, i:i + 1], -0.5, None, ALU.mult))
                    h, l_ = hi[0:p, 0:k * o], lo[0:p, 0:k * o]
                    flat = w[n][:, :, :].rearrange("p k o -> p (k o)")
                    link(nc.vector.tensor_scalar(h, flat, thr[0:p, i:i + 1], None, ALU.is_gt))
                    link(nc.vector.tensor_scalar(l_, flat, thr[0:p, j:j + 1], None, ALU.is_lt))
                    link(nc.vector.tensor_tensor(bit.q[n][:, :, :].rearrange("p k o -> p (k o)"), h, l_,
                                                 ALU.subtract))


def input_scale(core, bit, col, p, k, weights):
    nc, ps = core.nc, core.ps
    with nc.Block() as block:
        @block.tensor
        def _(pe):
            nc.tensor.transpose(ps[0:1, 0, 0:p], col, core.ident[0:p, 0:p]).then_inc(bit.turned.sem, 1)
            pe.wait_ge(bit.one.sem, bit.one.at(1))
            nc.tensor.matmul(ps[:, 1, 0:1], core.ones[0:1, :], bit.small[0:1, 0:1], start=True,
                             stop=True).then_inc(bit.spread.sem, 1)

        @block.vector
        def _(dve):
            link = core.linker(dve, "dve")
            dve.wait_ge(bit.turned.sem, bit.turned.at(1))
            nc.vector.tensor_reduce(bit.small[0:1, 0:1], ps[0:1, 0, 0:p], AX.X,
                                    ALU.max).then_inc(bit.one.sem, 1)
            dve.wait_ge(bit.spread.sem, bit.spread.at(1))
            link(nc.vector.tensor_scalar(bit.isc[:, k:k + 1], ps[:, 1, 0:1], 1e-8, 1.0 / QMAX, ALU.max,
                                         ALU.mult))
            link(nc.vector.reciprocal(bit.inv[:, k:k + 1], bit.isc[:, k:k + 1]))
            for n in weights:
                i = bit.weight(n)
                link(nc.vector.tensor_tensor(bit.out[:, i:i + 1], bit.ws[:, i:i + 1], bit.isc[:, k:k + 1],
                                             ALU.mult))
    for s in (bit.turned, bit.one, bit.spread):
        s.base += 1


def image_pass(core, bit, V, n_in, k, w_in, w_out, amax, isum, last=False):
    nc, d, ps = core.nc, core.d, core.ps
    tag = f"img{k}"
    first = n_in == DC
    with ExitStack() as ctx:
        Y = [core.sb(f"{tag}_y{s}", [n_in, NK], F32, ctx) for s in range(2)]
        R = core.sb(f"{tag}_r", [n_in, NK], F32, ctx)
        Q = [core.sb(f"{tag}_q{s}", [n_in, NK], BF16, ctx) for s in range(2)]
        A = [core.sb(f"{tag}_a{s}", [128, NK], F32, ctx) for s in range(2)]
        mx = core.sb(f"{tag}_mx", [128, B], F32, ctx)
        S = {n: core.sig(f"{tag}_{n}").sem for n in ("y_in0", "y_in1", "valued", "scaled", "rounded",
                                                      "lifted", "kept", "absed", "maxed", "reduced")}
        inv = bit.inv[0:n_in, k:k + 1]

        with nc.Block() as block:
            if first:
                @block.sync
                def _(sp):
                    def load(b, s):
                        sp.dma_start(Y[s][:, :], d["ctxT"][bass.ds(b, 1), 0:DC, :]
                                     .rearrange("o p n -> (o p) n")).then_inc(S[f"y_in{s}"], 16)
                    for s in range(2):
                        load(s, s)
                    with sp.Fori(0, B // 2 - 1) as i:
                        for s in range(2):
                            sp.wait_ge(S["scaled"], 2 * i + s + 3)
                            load(2 * (i + 1) + s, s)

            @block.scalar
            def _(act):
                if not last:
                    act.sem_inc(S["kept"], 2)
                with act.Fori(0, B // 2) as i:
                    for s in range(2):
                        n = 2 * i + s
                        if not first:
                            act.wait_ge(S["scaled"], n + 1)
                            j = bit.weight(w_in)
                            nc.scalar.activation(Y[s][:, :], V[:, bass.ds(n * NK, NK)], ACT.Identity,
                                                 scale=bit.out[:, j:j + 1],
                                                 bias=v(core, w_in)).then_inc(S["valued"], 1)
                    for s in range(2):
                        n = 2 * i + s
                        if not last:
                            act.wait_ge(S["lifted"], n + 3)
                            o = ps[:, 4 * s:4 * s + 3, 0:500]
                            act.wait_ge(S["maxed"], n + 1)
                            j = bit.weight(w_out)
                            nc.scalar.activation(A[s][:, :].rearrange("p (a m) -> p a m", a=3), o, ACT.Abs,
                                                 scale=bit.out[:, j:j + 1], bias=v(core, w_out)
                                                 ).then_inc(S["absed"], 1)
                            nc.scalar.activation(V[:, bass.ds(n * NK, NK)].rearrange("p (a m) -> p a m", a=3),
                                                 o, ACT.Copy).then_inc(S["kept"], 1)

            @block.vector
            def _(dve):
                link = core.linker(dve, "dve")
                dve.sem_inc(S["scaled"], 2)
                dve.sem_inc(S["rounded"], 2)
                dve.sem_inc(S["maxed"], 2)
                with dve.Fori(0, B // 2) as i:
                    for s in range(2):
                        n = 2 * i + s
                        if first:
                            dve.wait_ge(S[f"y_in{s}"], 16 * i + 16)
                        else:
                            dve.wait_ge(S["valued"], n + 1)
                        dve.wait_ge(S["rounded"], n + 2)
                        nc.vector.tensor_scalar(R[:, :], Y[s][:, :], inv, MAGIC, ALU.mult,
                                                ALU.add).then_inc(S["scaled"], 1)
                        dve.wait_ge(S["scaled"], n + 3)
                        if last:
                            q = V[:, bass.ds(n * NK, NK)].bitcast(BF16)
                        else:
                            dve.wait_ge(S["lifted"], n + 1)
                            q = Q[s][:, :]
                        nc.vector.tensor_scalar(q, R[:, :], -MAGIC, None, ALU.add
                                                ).then_inc(S["rounded"], 1)
                    if not last:
                        for s in range(2):
                            n = 2 * i + s
                            dve.wait_ge(S["absed"], n + 1)
                            nc.vector.tensor_reduce(mx[:, bass.ds(n, 1)], A[s][:, :], AX.X,
                                                    ALU.max).then_inc(S["maxed"], 1)
                            if isum is not None:
                                dve.wait_ge(S["kept"], n + 3)
                                nc.vector.tensor_reduce(isum[:, bass.ds(n, 1)], V[:, bass.ds(n * NK, NK)],
                                                        AX.X, ALU.add).then_inc(S["reduced"], 1)
                if not last:
                    dve.wait_ge(S["maxed"], B + 2)
                    if isum is not None:
                        dve.wait_ge(S["reduced"], B)
                    link(nc.vector.tensor_reduce(amax[:, :], mx[:, :], AX.X, ALU.max))

            if not last:
                @block.tensor
                def _(pe):
                    pe.sem_inc(S["lifted"], 2)
                    with pe.Fori(0, B // 2) as i:
                        for s in range(2):
                            n = 2 * i + s
                            pe.wait_ge(S["rounded"], n + 3)
                            pe.wait_ge(S["kept"], n + 1)
                            for a in range(3):
                                mm = nc.tensor.matmul(ps[:, 4 * s + a, 0:500], bit.q[w_out][:, 0, :],
                                                      Q[s][:, a * 500:(a + 1) * 500], start=True, stop=True)
                            mm.then_inc(S["lifted"], 1)


def bit_attend(core, bit, V, FU, which):
    nc, d, ps = core.nc, core.d, core.ps
    tag = f"bat{which}"
    j = bit.weight(which)
    W = bit.q[which][:, 0, :]
    sc = bit.out[:, j:j + 1]
    with ExitStack() as ctx:
        FB = core.sb(f"{tag}_fb", [D, 128], F32, ctx)
        KTs = core.sb(f"{tag}_kt", [D, 2, NK], F32, ctx)
        KV = core.sb(f"{tag}_kv", [KP, 2, KT, D], F32, ctx)
        brow = core.sb(f"{tag}_brow", [KP, D], F32, ctx)
        P = core.sb(f"{tag}_p", [128, NK], F32, ctx)
        PT = core.sb(f"{tag}_pt", [KP, KT, 128], F32, ctx)
        sm = core.sb(f"{tag}_sm", [128, 4], F32, ctx)
        S = {n: core.sig(f"{tag}_{n}").sem for n in
             ("row_in", "fb_ready", "k_made", "kv_made", "kt_copied", "kv_copied", "scored",
              "maxed", "exped", "inverted", "scaled", "turned", "pt_copied", "weighed", "fused")}

        with nc.Block() as block:
            @block.sync
            def _(sp):
                sp.dma_start(brow[:, :], d[f"bit_row_{which}"]).then_inc(S["row_in"], 16)
                sp.wait_ge(S["row_in"], 16)

            @block.gpsimd
            def _(pool):
                nc.gpsimd.memset(FB[:, :], 0.0).then_inc(S["fb_ready"], 1)
                pool.wait_ge(S["fb_ready"], 1)
                with pool.Fori(0, B // 2) as i:
                    pool.wait_ge(S["scored"], i + 1)
                    for s in range(2):
                        nc.gpsimd.tensor_copy(FB[:, 64 * s:64 * s + NQ], FU[:, bass.ds((2 * i + s) * NQ, NQ)]
                                              ).then_inc(S["fb_ready"], 1)

            @block.tensor
            def _(pe):
                with pe.Fori(0, B // 2) as i:
                    for s in range(2):
                        pe.wait_ge(S["kt_copied"], 2 * i + s + 1)
                        if s == 0:
                            pe.wait_ge(S["exped"], i + 1)
                        for a in range(3):
                            mm = nc.tensor.matmul(ps[:, a, 0:500], W,
                                                  V[:, bass.ds((2 * i + s) * NK + a * 500, 500)],
                                                  start=True, stop=True)
                        mm.then_inc(S["k_made"], 1)
                        pe.wait_ge(S["kv_copied"], 2 * i + s + 1)
                        for t in range(KT):
                            mm = nc.tensor.matmul(ps[0:KP, 3 + t // 4, (t % 4) * D:(t % 4 + 1) * D],
                                                  V[:, bass.ds((2 * i + s) * NK + t * KP, KP)], W,
                                                  start=True, stop=True)
                        mm.then_inc(S["kv_made"], 1)
                    pe.wait_ge(S["kt_copied"], 2 * i + 3)
                    pe.wait_ge(S["fb_ready"], 2 * i + 3)
                    for s in range(2):
                        for a in range(3):
                            mm = nc.tensor.matmul(ps[64 * s:64 * s + 64, a, 0:500], FB[:, 64 * s:64 * s + 64],
                                                  KTs[:, s, a * 500:(a + 1) * 500], start=True, stop=True)
                    mm.then_inc(S["scored"], 1)
                    pe.wait_ge(S["scaled"], i + 1)
                    for g in range(3):
                        pe.wait_ge(S["pt_copied"], 3 * i + g + 1)
                        for t in range(4 * g, 4 * g + 4):
                            mm = nc.tensor.transpose(ps[0:KP, 6 + g % 2, (t % 4) * 128:(t % 4 + 1) * 128],
                                                     P[:, t * KP:(t + 1) * KP], core.ident[:, :])
                        mm.then_inc(S["turned"], 1)
                    pe.wait_ge(S["pt_copied"], 3 * i + 5)
                    pe.wait_ge(S["kv_copied"], 2 * i + 3)
                    for s in range(2):
                        for t in range(KT):
                            mm = nc.tensor.matmul(ps[:, 6, 64 * s:64 * s + NQ], KV[:, s, t, :],
                                                  PT[:, t, 64 * s:64 * s + NQ], start=(t == 0),
                                                  stop=(t == KT - 1))
                    mm.then_inc(S["weighed"], 1)

            @block.scalar
            def _(act):
                act.sem_inc(S["kt_copied"], 1)
                act.sem_inc(S["exped"], 1)
                with act.Fori(0, B // 2) as i:
                    for s in range(2):
                        act.wait_ge(S["k_made"], 2 * i + s + 1)
                        nc.scalar.activation(KTs[:, s, :].rearrange("p (a m) -> p a m", a=3),
                                             ps[:, 0:3, 0:500], ACT.Identity, scale=sc,
                                             bias=v(core, which)).then_inc(S["kt_copied"], 1)
                    act.wait_ge(S["maxed"], i + 1)
                    nc.scalar.activation(P[:, :].rearrange("p (a m) -> p a m", a=3), ps[:, 0:3, 0:500],
                                         ACT.Exp, bias=sm[:, 0:1], scale=float(D) ** -0.5,
                                         accum_out=sm[:, 1:2]).then_inc(S["exped"], 1)
                    act.wait_ge(S["exped"], i + 2)

            @block.vector
            def _(dve):
                link = core.linker(dve, "dve")
                dve.sem_inc(S["kv_copied"], 1)
                dve.sem_inc(S["pt_copied"], 2)
                dve.sem_inc(S["scored"], 1)
                dve.wait_ge(S["row_in"], 16)
                with dve.Fori(0, B // 2) as i:
                    for s in range(2):
                        dve.wait_ge(S["kv_made"], 2 * i + s + 1)
                        nc.vector.scalar_tensor_tensor(
                            out=KV[:, s, :, :], in0=ps[0:KP, 3:6, :].rearrange("p b (t n) -> p (b t) n", n=D),
                            scalar=sc[0:KP, :], in1=brow[:, :].unsqueeze(1).to_broadcast([KP, KT, D]),
                            op0=ALU.mult, op1=ALU.add).then_inc(S["kv_copied"], 1)
                    dve.wait_ge(S["scored"], i + 2)
                    nc.vector.tensor_reduce(sm[:, 2:3], ps[:, 0:3, 0:500], AX.XY, ALU.max
                                            ).then_inc(S["inverted"], 1)
                    dve.wait_ge(S["inverted"], 3 * i + 1)
                    nc.vector.tensor_scalar(sm[:, 0:1], sm[:, 2:3], -float(D) ** -0.5, None,
                                            ALU.mult).then_inc(S["maxed"], 1)
                    dve.wait_ge(S["exped"], i + 2)
                    nc.vector.reciprocal(sm[:, 3:4], sm[:, 1:2]).then_inc(S["inverted"], 1)
                    dve.wait_ge(S["inverted"], 3 * i + 2)
                    nc.vector.tensor_scalar(P[:, :], P[:, :], sm[:, 3:4], None, ALU.mult
                                            ).then_inc(S["scaled"], 1)
                    for g in range(3):
                        dve.wait_ge(S["turned"], 3 * i + g + 1)
                        nc.vector.tensor_copy(PT[:, 4 * g:4 * g + 4, :].rearrange("p t n -> p (t n)"),
                                              ps[0:KP, 6 + g % 2, :]).then_inc(S["pt_copied"], 1)
                    dve.wait_ge(S["weighed"], i + 1)
                    f = FU[:, bass.ds(2 * i * NQ, 2 * NQ)].rearrange("p (s q) -> p s q", s=2)
                    nc.vector.scalar_tensor_tensor(
                        out=f, in0=ps[:, 6, 0:128].rearrange("p (s q) -> p s q", s=2)[:, :, 0:NQ],
                        scalar=0.1, in1=f, op0=ALU.mult, op1=ALU.add).then_inc(S["inverted"], 1)
                    dve.wait_ge(S["inverted"], 3 * i + 3)


def quantized(core, bit, link, dst, src, k, tmp, p=128):
    nc = core.nc
    link(nc.vector.tensor_scalar(tmp, src, bit.inv[0:p, k:k + 1], MAGIC, ALU.mult, ALU.add))
    link(nc.vector.tensor_scalar(dst, tmp, -MAGIC, None, ALU.add))


def bit_linear(core, bit, name, q, dst, relu, tag):
    nc, ps = core.nc, core.ps
    p, kt, outs = BITS[name]
    j = bit.weight(name)
    S = {n: core.sig(f"{tag}_{n}").sem for n in ("made", "copied")}
    no = outs // 128
    with nc.Block() as block:
        @block.tensor
        def _(pe):
            for o in range(no):
                for c in range(NCH):
                    n = o * NCH + c
                    if n >= 8:
                        pe.wait_ge(S["copied"], n - 7)
                    for t in range(kt):
                        mm = nc.tensor.matmul(ps[:, n % 8, 0:CH], bit.q[name][:, t, o * 128:(o + 1) * 128],
                                              q[t][:, c * CH:(c + 1) * CH], start=(t == 0), stop=(t == kt - 1))
                    mm.then_inc(S["made"], 1)

        @block.scalar
        def _(act):
            for o in range(no):
                bias = v(core, name if no == 1 else f"{name}_{o}")
                for c in range(NCH):
                    n = o * NCH + c
                    act.wait_ge(S["made"], n + 1)
                    nc.scalar.activation(dst[:, o, c * CH:(c + 1) * CH], ps[:, n % 8, 0:CH],
                                         ACT.Relu if relu else ACT.Identity, scale=bit.out[:, j:j + 1],
                                         bias=bias).then_inc(S["copied"], 1)


def bit_attention(core, amax):
    nc, ps = core.nc, core.ps
    with ExitStack() as ctx:
        bit = Bit(core, ctx)
        FU = core.sb("bit_fused", [D, 1, T], F32, ctx)
        isum = core.sb("bit_isum", [128, B], F32, ctx)
        avg = core.sb("bit_avg", [128, B], F32, ctx)
        vmax = core.sb("bit_vmax", [128, 3], F32, ctx)
        quantize_weights(core, bit)
        with ExitStack() as c1:
            V = core.sb("bit_V", [128, B * NK], I16, c1)
            input_scale(core, bit, amax[:, :], DC, 0, ["d2v"])
            image_pass(core, bit, V, DC, 0, None, "d2v", vmax[:, 0:1], None)
            input_scale(core, bit, vmax[:, 0:1], 128, 1, ["img"])
            image_pass(core, bit, V, 128, 1, "d2v", "img", vmax[:, 1:2], isum)
            input_scale(core, bit, vmax[:, 1:2], 128, 2, ["att0", "att1"])
            image_pass(core, bit, V, 128, 2, "img", None, None, None, last=True)

            def with_block(f):
                with nc.Block() as block:
                    @block.vector
                    def _(dve):
                        f(core.linker(dve, "dve"))

            with ExitStack() as c2:
                tmp = core.sb("bit_tmp", [D, T], F32, c2)
                q = core.sb("bit_qx", [D, T], BF16, c2)
                tm = core.sb("bit_tm", [128, 1], F32, c2)
                with_block(lambda link: link(nc.vector.tensor_reduce(
                    tm[:, :], core.xn[:, :], AX.X, ALU.max, apply_absolute_value=True)))
                input_scale(core, bit, tm[:, :], 128, 3, ["txt"])
                with_block(lambda link: quantized(core, bit, link, q[:, :], core.xn[:, :], 3, tmp[:, :]))
                bit_linear(core, bit, "txt", [q], FU, False, "btxt")
            Vb = V[:, :].bitcast(BF16)
            for which in ("att0", "att1"):
                bit_attend(core, bit, Vb, FU[:, 0, :], which)

        with ExitStack() as c2:
            tmp = core.sb("bit_tmp2", [D, 4, T], F32, c2)
            qf = core.sb("bit_qf", [D, 4, T], BF16, c2)
            hh = core.sb("bit_hh", [D, 4, T], F32, c2)
            tm = core.sb("bit_tm2", [128, 4], F32, c2)
            j = bit.weight("img")

            def inputs(link):
                link(nc.vector.tensor_scalar(avg[:, :], isum[:, :], bit.out[:, j:j + 1], None, ALU.mult))
                link(nc.vector.tensor_scalar(avg[:, :], avg[:, :], 1.0 / NK, v(core, "img"), ALU.mult, ALU.add))
                link(nc.vector.tensor_reduce(tm[:, 0:1], FU[:, 0, :], AX.X, ALU.max, apply_absolute_value=True))
                link(nc.vector.tensor_reduce(tm[:, 1:2], avg[:, :], AX.X, ALU.max, apply_absolute_value=True))
                link(nc.vector.tensor_tensor(tm[:, 2:3], tm[:, 0:1], tm[:, 1:2], ALU.max))

            def rounded(link):
                quantized(core, bit, link, qf[:, 0, :], FU[:, 0, :], 4, tmp[:, 0, :])
                quantized(core, bit, link, avg[:, :], avg[:, :], 4, tmp[:, 1, 0:B])
                link(nc.vector.tensor_copy(qf[:, 1, :].rearrange("p (b q) -> p b q", q=NQ),
                                           avg[:, :].unsqueeze(2).to_broadcast([128, B, NQ])))

            with_block(inputs)
            input_scale(core, bit, tm[:, 2:3], 128, 4, ["f1"])
            with_block(rounded)
            bit_linear(core, bit, "f1", [qf[:, 0, :], qf[:, 1, :]], hh, True, "bf1")
            with_block(lambda link: link(nc.vector.tensor_reduce(
                tm[:, 3:4], hh[:, :, :], AX.XY, ALU.max)))
            input_scale(core, bit, tm[:, 3:4], 128, 5, ["f2"])
            with_block(lambda link: quantized(core, bit, link, qf[:, :, :], hh[:, :, :], 5, tmp[:, :, :]))
            bit_linear(core, bit, "f2", [qf[:, t, :] for t in range(4)],
                       core.OT[:, :].rearrange("p (o t) -> p o t", o=1), False, "bf2")


def build(nc, d, out):
    with ExitStack() as ctx:
        core = Core(nc, ctx, d, out)
        rk = core.sb("rk", [KP, B * KT])
        amax = core.sb("amax", [DC, 1])
        csum = core.sb("csum", [KA, B])
        start_up(core)
        context_statistics(core, rk, amax, csum)
        layer_norm(core, core.xT, core.xn, "a0")
        with ExitStack() as c0:
            qp = core.sb("L0_Qp", [D, T], F32, c0)
            l2_norm_queries(core, qp, core.xn)
            attention(core, "L0", core.xn, v(core, "L0_bo"), keep_max=False, rk=rk, dh=8)
            with nc.Block() as block:
                @block.vector
                def _(dve):
                    link = core.linker(dve, "dve")
                    link(nc.vector.tensor_tensor(core.OT[:, :], core.OT[:, :], qp[:, :], ALU.add))

            def gamma_beta(link):
                link(nc.vector.tensor_scalar(core.xn[:, :], core.xn[:, :], v(core, "L0_g"), v(core, "L0_b"),
                                             ALU.mult, ALU.add))
            layer_norm(core, core.OT, core.xn, "o0", gamma_beta)
            add_gated(core, core.xn, 0)
        core.new_signals()
        layer_norm(core, core.xT, core.xn, "f0")
        experts0(core, 1)
        core.new_signals()
        layer_norm(core, core.xT, core.xn, "a1")
        attention(core, "L1", core.xn, v(core, "L1_bo"), scale=0.125, dh=64)
        add_gated(core, core.OT, 2)
        core.new_signals()
        layer_norm(core, core.xT, core.xn, "f1")
        gated_experts(core, "L1", 16, 5, 1e-9, 3)
        core.new_signals()
        layer_norm(core, core.xT, core.xn, "a2")
        bit_attention(core, amax)
        add_gated(core, core.OT, 4)
        core.new_signals()
        layer_norm(core, core.xT, core.xn, "f2")
        gated_experts(core, "L2", 8, 9, 1e-20, 5)
        core.new_signals()
        layer_norm(core, core.xT, core.xn, "a3")
        attention(core, "L3", core.xn, v(core, "L3_bo"), scale=float(8) ** -0.5, dh=8, clip=10000.0,
                  csum=csum)
        add_gated(core, core.OT, 6)
        core.new_signals()
        layer_norm(core, core.xT, core.xn, "f3")
        binarized_mlp(core, 7)
        store(core)


def store(core):
    nc = core.nc
    stored = core.sig("stored")
    with nc.Block() as block:
        @block.sync
        def _(sp):
            sp.dma_start(core.out, core.xT[:, :]).then_inc(stored.sem, 16)
            sp.wait_ge(stored.sem, 16)


def arrange(a):
    z = np.float32
    r = {}
    f = {k: np.asarray(w) for k, w in a.items()}
    r["xT"] = f["x"].reshape(T, D).T
    ctx = f["ctx_768"]
    keys = ctx.reshape(B, KP, KT, DC)
    r["ctxT"] = np.concatenate([keys.transpose(0, 3, 2, 1).reshape(B, DC, NK), np.ones((B, 2, NK), z)], 1)
    r["ctxN"] = np.concatenate([keys, np.ones((B, KP, KT, 1), z)], 3).reshape(B, KP, KT * KA)
    r["gates"] = np.broadcast_to(np.stack([f["g_xattn"], f["g_ffn"]], 1).reshape(1, 8), (128, 8))
    cols = {"L0_bq": f["L0_xattn_bq"], "L0_bo": f["L0_xattn_bo"], "L0_g": f["L0_xattn_ln_gamma"],
            "L0_b": f["L0_xattn_ln_beta"], "L1_bo": f["L1_xattn_bo"], "L3_bo": f["L3_xattn_bo"],
            "L3_b2": f["L3_ffn_b2"], "d2v": f["L2_xattn_b_d2v"], "img": f["L2_xattn_b_img"],
            "txt": f["L2_xattn_b_txt"], "f2": f["L2_xattn_b_f2"]}
    for n in ("att0", "att1"):
        cols[n] = np.concatenate([f[f"L2_xattn_b_{n}"]] * 2)
    for c in range(4):
        cols[f"f1_{c}"] = f["L2_xattn_b_f1"][c * 128:(c + 1) * 128]
        cols[f"ffb1_{c}"] = f["L3_ffn_b1"][c * 128:(c + 1) * 128]
    r["vec"] = np.stack([cols[n] for n in VECS], 1)

    def heads(w, dh):
        return w.reshape(w.shape[0], H, dh).transpose(2, 1, 0)

    for L, dh in (("L0", 8), ("L1", 64), ("L3", 8)):
        p = L + "_xattn_"
        zero = np.zeros(H * dh, z)
        bk, bv, bq = (f.get(p + n, zero) for n in ("bk", "bv", "bq"))
        wk = np.concatenate([f[p + "Wk"], bk[None]], 0)
        wv = np.concatenate([f[p + "Wv"], bv[None]], 0)
        r[f"{L}_WvA"] = heads(wv, dh)
        r[f"{L}_Wo"] = f[p + "Wo"].reshape(H, dh, D).transpose(1, 0, 2)
        if dh == DH:
            e = np.zeros((KA, H, DH + 1), z)
            e[:, :, 0:DH] = wv.reshape(KA, H, DH)
            e[DC, :, DH] = 1
            r[f"{L}_WvE"] = e.reshape(KA, H // 2 * VW)
            e = np.zeros((4, 32, 2, 2, D), z)
            for h in range(H):
                rr, g, j = h // 8, h // 2 % 4, h % 2
                e[g, (DH + 1) * j:(DH + 1) * j + DH, rr, j] = f[p + "Wo"][h * DH:(h + 1) * DH]
            r[f"{L}_WoE"] = e.reshape(128, 4, D)
        if L == "L0":
            r["L0_Wq"] = f[p + "Wq"]
            r["L0_WkA"] = wk
            bd = np.zeros((H, dh, H, KA), z)
            for h in range(H):
                bd[h, :, h, :] = wk[:, h * dh:(h + 1) * dh].T
            r["L0_WkBD"] = bd.reshape(D, H, KA)
        else:
            r[f"{L}_WqT"] = heads(f[p + "Wq"], dh)
            r[f"{L}_WkAT"] = heads(wk, dh)
            r[f"{L}_bqh"] = bq.reshape(H, dh).T

    p = "L0_ffn_"
    r["L0_gw"] = f[p + "gate_w"]
    r["L0_gb"] = np.broadcast_to(f[p + "gate_b"], (TT, E0))
    r["L0_w1"] = f[p + "w1"].reshape(E0 // 2, 2, D, HID0).transpose(0, 2, 1, 3)
    r["L0_w2"] = f[p + "w2"].reshape(E0 // 2, 2, 128, HID0).transpose(0, 2, 1, 3)
    r["L0_b1"] = f[p + "b1"].reshape(E0, 128, HID0 // 128).transpose(1, 0, 2)
    r["L0_b2"] = f[p + "b2"].reshape(E0 // 2, 1, 2, D)

    def spread(n_exp, n_chunk, mid):
        ex = np.zeros((n_exp + 1, n_chunk * 128), z)
        for e in range(n_exp):
            ex[e, e * mid:(e + 1) * mid] = 1
        ex[n_exp, n_exp * mid:] = 1
        return ex.reshape(n_exp + 1, n_chunk, 128)

    def up(w):
        return w.transpose(1, 0, 2).reshape(D, -1)

    def rows(w):
        return w.reshape(-1, 128, D).transpose(1, 0, 2)

    p = "L1_ffn_"
    r["L1_wr"] = f[p + "router_w"]
    r["L1_ex"] = spread(16, 5, 32)
    r["L1_wg"] = np.concatenate([up(f[p + "wg_r"]), up(f[p + "wg_s"])], 1).reshape(D, 5, 128)
    r["L1_wu"] = np.concatenate([up(f[p + "wu_r"]), up(f[p + "wu_s"])], 1).reshape(D, 5, 128)
    r["L1_wd"] = rows(np.concatenate([f[p + "wd_r"].reshape(-1, D), f[p + "wd_s"].reshape(-1, D)], 0))
    p = "L2_ffn_"
    r["L2_wr"] = f[p + "gate_w"]
    r["L2_ex"] = spread(8, 9, 128)
    r["L2_wg"] = np.concatenate([up(f[p + "ew_gate"]), f[p + "sw_gate"]], 1).reshape(D, 9, 128)
    r["L2_wu"] = np.concatenate([up(f[p + "ew_up"]), f[p + "sw_up"]], 1).reshape(D, 9, 128)
    r["L2_wd"] = rows(np.concatenate([f[p + "ew_down"].reshape(-1, D), f[p + "sw_down"]], 0))
    p = "L2_xattn_"
    for n, (rows_, kt, o) in BITS.items():
        w = f[f"{p}W_{n}"].T
        if n.startswith("att"):
            w = np.concatenate([w, w], 1)
            r[f"bit_row_{n}"] = np.broadcast_to(cols[n], (KP, D))
        r[f"bit_{n}"] = w.reshape(kt, rows_, o).transpose(1, 0, 2)
    r["L3_w1"] = f["L3_ffn_w1"].reshape(4, 128, D).transpose(1, 0, 2)
    r["L3_w2"] = f["L3_ffn_w2"].reshape(D, 4, 128)
    return r


def kernel(**inputs):
    import concourse.bacc as _bacc
    from concourse.bass_utils import run_bass_kernel_spmd as _run

    nc = _bacc.Bacc("TRN2", target_bir_lowering=False, num_devices=1)
    arrays, d = {}, {}
    for name, a in arrange(inputs).items():
        a = np.ascontiguousarray(a)
        arrays[f"in_{name}"] = a
        d[name] = nc.dram_tensor(f"in_{name}", a.shape, mybir.dt.from_np(a.dtype), kind="ExternalInput").ap()
    out = nc.dram_tensor("out_x", (D, T), F32, kind="ExternalOutput").ap()
    build(nc, d, out)
    got = _run(nc, [arrays], core_ids=[0]).results[0]["out_x"]
    return np.ascontiguousarray(got.T).reshape(B, NQ, D)
```

```python
from contextlib import ExitStack

import numpy as np
import concourse.bass as bass
from concourse import mybir

F32 = mybir.dt.float32
F32R = mybir.dt.float32r
BF16 = mybir.dt.bfloat16
I16 = mybir.dt.int16
I32 = mybir.dt.int32
U32 = mybir.dt.uint32
ALU = mybir.AluOpType
ACT = mybir.ActivationFunctionType
AX = mybir.AxisListType

B, NQ, D = 32, 56, 128
NK, DC = 1500, 96
T = B * NQ
CH = 448
NCH = T // CH
TT = 112
NT = T // TT
H = 16
HQ = H * NQ
HALF = HQ // 2
DH = 8
VW = 2 * (DH + 1)
KT, KP = 12, 125
KA = DC + 1
KM = DC + 2
LN_EPS = 1e-5
MAGIC = 1.5 * 2.0 ** 23
E0, CAP, TOPK0, HID0 = 64, 64, 3, 512


class Signal:

    def __init__(self, nc, name):
        self.sem = nc.alloc_semaphore(name)
        self.base = 0

    def at(self, n):
        return self.base + n


class Core:

    def __init__(self, nc, ctx, d, out):
        self.nc, self.ctx, self.d, self.out = nc, ctx, d, out
        self.ps = ctx.enter_context(nc.psum_tensor("ps", [128, 8, 512], F32))
        self.xT = self.sb("xT", [D, T])
        self.xn = self.sb("xn", [D, T])
        self.OT = self.sb("OT", [D, T])
        self.J = self.sb("J", [128, 128])
        self.ones = self.sb("ones", [128, 128])
        self.ident = self.sb("ident", [128, 128])
        self.sum_row = self.sb("sum_row", [128, 2, 128])
        self.vec = self.sb("vec", [128, NVEC])
        self.tg = self.sb("tg", [128, 8])
        self.eps = self.sb("eps", [128, 1])
        self.signals, self.part = [], 0
        self.new_signals()

    def sb(self, name, shape, dt=F32, ctx=None):
        return (ctx or self.ctx).enter_context(self.nc.sbuf_tensor(name, shape, dt))

    def sig(self, name):
        s = Signal(self.nc, f"{name}_{self.part}")
        self.signals.append(s)
        return s

    def new_signals(self):
        nc, old = self.nc, self.signals
        if old:
            with nc.Block() as block:
                @block.gpsimd
                def _(pool):
                    nc.clear_and_free_semaphores([s.sem for s in old])
        self.signals = []
        self.part += 1
        self.step = {e: self.sig(f"{e}_step") for e in ("dve", "act", "pe", "pool")}
        self.queries_made, self.queries_act, self.queries_dve = (
            self.sig(f"queries_{n}") for n in ("made", "act", "dve"))
        self.attend = {n: self.sig(f"attend_{n}") for n in ATTEND_ALL}
        self.mean_ready = self.sig("mean_ready")
        self.centred = self.sig("centred")
        self.squared = self.sig("squared")
        self.var_ready = self.sig("var_ready")
        self.std_ready = self.sig("std_ready")

    def linker(self, eng, which):
        s = self.step[which]

        def link(ins):
            ins.then_inc(s.sem, 1)
            s.base += 1
            eng.wait_ge(s.sem, s.base)
        return link


VECS = ["L0_bq", "L0_bo", "L0_g", "L0_b", "L1_bo", "L3_bo", "L3_b2",
        "d2v", "img", "txt", "att0", "att1", "f2"] + [f"f1_{c}" for c in range(4)] \
    + [f"ffb1_{c}" for c in range(4)]
NVEC = len(VECS)


def v(core, name, p=128):
    n = VECS.index(name)
    return core.vec[0:p, n:n + 1]


def start_up(core):
    nc, d = core.nc, core.d
    loaded, g_in = core.sig("loaded"), core.sb("g_in", [128, 8])
    consts, zeroed = core.sig("consts"), core.sig("zeroed")
    with nc.Block() as block:
        @block.sync
        def _(sp):
            sp.dma_start(core.xT[:, :], d["xT"]).then_inc(loaded.sem, 16)
            sp.dma_start(core.vec[:, :], d["vec"]).then_inc(loaded.sem, 16)
            sp.dma_start(g_in[:, :], d["gates"]).then_inc(loaded.sem, 16)
            sp.wait_ge(loaded.sem, 48)

        @block.scalar
        def _(act):
            act.wait_ge(loaded.sem, 48)
            nc.scalar.activation(core.tg[:, :], g_in[:, :], ACT.Tanh).then_inc(consts.sem, 1)

        @block.vector
        def _(dve):
            nc.vector.memset(core.J[:, :], 1.0 / D).then_inc(consts.sem, 1)
            nc.vector.memset(core.ones[:, :], 1.0).then_inc(consts.sem, 1)
            nc.vector.memset(core.eps[:, :], LN_EPS).then_inc(consts.sem, 1)

        @block.gpsimd
        def _(pool):
            nc.gpsimd.memset(core.ident[:, :], 0.0).then_inc(zeroed.sem, 1)
            pool.wait_ge(zeroed.sem, 1)
            nc.gpsimd.affine_select(out=core.ident[:, :], in_=core.ident[:, :], compare_op=ALU.not_equal,
                                    fill=1.0, base=0, pattern=[[-1, 128]],
                                    channel_multiplier=1).then_inc(consts.sem, 1)
            nc.gpsimd.memset(core.sum_row[:, :, :], 0.0).then_inc(zeroed.sem, 1)
            pool.wait_ge(zeroed.sem, 2)
            for j in range(2):
                nc.gpsimd.affine_select(out=core.sum_row[:, j, :].rearrange("p (g c) -> p g c", c=32),
                                        in_=core.sum_row[:, j, :].rearrange("p (g c) -> p g c", c=32),
                                        compare_op=ALU.not_equal, fill=1.0, base=-((DH + 1) * j + DH),
                                        pattern=[[-32, 4], [0, 32]],
                                        channel_multiplier=1).then_inc(consts.sem, 1)


def layer_norm(core, src, dst, tag, finish=None):
    nc = core.nc
    mean, cen, sq, var, std = (core.mean_ready, core.centred, core.squared, core.var_ready,
                               core.std_ready)
    with ExitStack() as ctx:
        xc = core.sb(f"xc{tag}", [D, T], F32, ctx)
        x2 = core.sb(f"x2{tag}", [D, T], F32, ctx)
        sd = core.sb(f"sd{tag}", [D, T], F32, ctx)
        with nc.Block() as block:
            @block.tensor
            def _(pe):
                for c in range(NCH):
                    nc.tensor.matmul(core.ps[:, c, 0:CH], core.J[:, :], src[:, c * CH:(c + 1) * CH],
                                     start=True, stop=True).then_inc(mean.sem, 1)
                for c in range(NCH):
                    pe.wait_ge(sq.sem, sq.at(c + 1))
                    nc.tensor.matmul(core.ps[:, 4 + c, 0:CH], core.J[:, :], x2[:, c * CH:(c + 1) * CH],
                                     start=True, stop=True).then_inc(var.sem, 1)

            @block.scalar
            def _(act):
                for c in range(NCH):
                    act.wait_ge(cen.sem, cen.at(c + 1))
                    s = slice(c * CH, (c + 1) * CH)
                    nc.scalar.activation(x2[:, s], xc[:, s], ACT.Square).then_inc(sq.sem, 1)
                for c in range(NCH):
                    act.wait_ge(var.sem, var.at(c + 1))
                    nc.scalar.activation(sd[:, c * CH:(c + 1) * CH], core.ps[:, 4 + c, 0:CH], ACT.Sqrt,
                                         bias=core.eps[:, :]).then_inc(std.sem, 1)

            @block.vector
            def _(dve):
                link = core.linker(dve, "dve")
                for c in range(NCH):
                    dve.wait_ge(mean.sem, mean.at(c + 1))
                    s = slice(c * CH, (c + 1) * CH)
                    nc.vector.tensor_tensor(xc[:, s], src[:, s], core.ps[:, c, 0:CH],
                                            ALU.subtract).then_inc(cen.sem, 1)
                dve.wait_ge(cen.sem, cen.at(NCH))
                for c in range(NCH):
                    dve.wait_ge(std.sem, std.at(c + 1))
                    s = slice(c * CH, (c + 1) * CH)
                    link(nc.vector.reciprocal(x2[:, s], sd[:, s]))
                    link(nc.vector.tensor_tensor(dst[:, s], xc[:, s], x2[:, s], ALU.mult))
                if finish:
                    finish(link)
        for s in (mean, cen, sq, var, std):
            s.base += NCH


def add_gated(core, src, gate):
    nc = core.nc
    with nc.Block() as block:
        @block.vector
        def _(dve):
            link = core.linker(dve, "dve")
            link(nc.vector.scalar_tensor_tensor(out=core.xT[:, :], in0=src[:, :],
                                                scalar=core.tg[:, gate:gate + 1], in1=core.xT[:, :],
                                                op0=ALU.mult, op1=ALU.add))


def context_statistics(core, rk, amax, csum):
    nc, d = core.nc, core.d
    with ExitStack() as ctx:
        ct = core.sb("cs_ct", [KA, 2, NK], F32, ctx)
        wk = core.sb("cs_wk", [KA, D], F32, ctx)
        sq = core.sb("cs_sq", [KP, 2, KT, D], F32, ctx)
        junk = core.sb("cs_junk", [KA, NK], F32, ctx)
        am = core.sb("cs_am", [DC, B], F32, ctx)
        n2 = core.sb("cs_n2", [KP, B * KT], F32, ctx)
        w_in, normed = core.sig("cs_w_in"), core.sig("cs_normed")
        ct_in = [core.sig(f"cs_ct_in{s}") for s in range(2)]
        projected, squared, reduced, maxed, summed = (core.sig(f"cs_{n}") for n in (
            "projected", "squared", "reduced", "maxed", "summed"))
        with nc.Block() as block:
            @block.sync
            def _(sp):
                sp.dma_start(wk[:, :], d["L0_WkA"]).then_inc(w_in.sem, 16)
                with sp.Fori(0, B // 2) as i:
                    for s in range(2):
                        sp.wait_ge(projected.sem, 2 * i + s + 1)
                        sp.wait_ge(maxed.sem, 2 * i + s + 1)
                        sp.wait_ge(summed.sem, 2 * i + s + 1)
                        sp.dma_start(ct[:, s, :], d["ctxT"][bass.ds(2 * i + s, 1), 0:KA, :]
                                     .rearrange("o p n -> (o p) n")).then_inc(ct_in[s].sem, 16)

            @block.tensor
            def _(pe):
                pe.sem_inc(projected.sem, 2)
                pe.wait_ge(w_in.sem, 16)
                with pe.Fori(0, B // 2) as i:
                    for s in range(2):
                        pe.wait_ge(ct_in[s].sem, 16 * i + 16)
                        pe.wait_ge(squared.sem, 2 * i + s + 1)
                        for j in range(KT):
                            mm = nc.tensor.matmul(core.ps[0:KP, 3 * s + j // 4, (j % 4) * D:(j % 4 + 1) * D],
                                                  ct[:, s, j * KP:(j + 1) * KP], wk[:, :],
                                                  start=True, stop=True)
                        mm.then_inc(projected.sem, 1)

            @block.scalar
            def _(act):
                act.sem_inc(squared.sem, 2)
                act.sem_inc(summed.sem, 2)
                with act.Fori(0, B // 2) as i:
                    for s in range(2):
                        act.wait_ge(ct_in[s].sem, 16 * i + 16)
                        act.wait_ge(summed.sem, 2 * i + s + 2)
                        nc.scalar.activation(junk[:, :], ct[:, s, :], ACT.Copy,
                                             accum_out=csum[:, bass.ds(2 * i + s, 1)]).then_inc(summed.sem, 1)
                        act.wait_ge(projected.sem, 2 * i + s + 3)
                        act.wait_ge(reduced.sem, 2 * i + s + 1)
                        nc.scalar.activation(sq[:, s, :, :].rearrange("p j n -> p (j n)"),
                                             core.ps[0:KP, 3 * s:3 * s + 3, :].rearrange("p b n -> p (b n)"),
                                             ACT.Square).then_inc(squared.sem, 1)
                act.wait_ge(reduced.sem, B + 2)
                nc.scalar.activation(rk[:, :], n2[:, :], ACT.Sqrt).then_inc(normed.sem, 1)

            @block.vector
            def _(dve):
                link = core.linker(dve, "dve")
                dve.sem_inc(reduced.sem, 2)
                dve.sem_inc(maxed.sem, 2)
                with dve.Fori(0, B // 2) as i:
                    for s in range(2):
                        dve.wait_ge(ct_in[s].sem, 16 * i + 16)
                        nc.vector.tensor_reduce(am[:, bass.ds(2 * i + s, 1)], ct[0:DC, s, :], AX.X, ALU.max,
                                                apply_absolute_value=True).then_inc(maxed.sem, 1)
                        dve.wait_ge(squared.sem, 2 * i + s + 3)
                        nc.vector.tensor_reduce(n2[:, bass.ds((2 * i + s) * KT, KT)], sq[:, s, :, :],
                                                AX.X, ALU.add).then_inc(reduced.sem, 1)
                dve.wait_ge(maxed.sem, B + 2)
                link(nc.vector.tensor_reduce(amax[:, :], am[:, :], AX.X, ALU.max))
                dve.wait_ge(normed.sem, 1)
                link(nc.vector.tensor_scalar(n2[:, :], rk[:, :], 1e-12, None, ALU.max))
                link(nc.vector.reciprocal(rk[:, :], n2[:, :]))
                link(nc.vector.tensor_scalar(rk[:, :], rk[:, :], float(8) ** -0.5, None, ALU.mult))


def l2_norm_queries(core, qp, qn):
    nc, d = core.nc, core.d
    w_in = core.sig("l2q_w_in")
    mm1, qpd, sqd, mm2, nrm = (core.sig(f"l2q_{n}") for n in ("mm", "qp", "sq", "sum", "norm"))
    with ExitStack() as ctx:
        wq = core.sb("l2q_w", [D, D], F32, ctx)
        x2 = core.sb("l2q_x2", [D, T], F32, ctx)
        with nc.Block() as block:
            @block.sync
            def _(sp):
                sp.dma_start(wq[:, :], d["L0_Wq"]).then_inc(w_in.sem, 16)

            @block.tensor
            def _(pe):
                pe.wait_ge(w_in.sem, 16)
                for c in range(NCH):
                    nc.tensor.matmul(core.ps[:, c, 0:CH], wq[:, :], core.xn[:, c * CH:(c + 1) * CH],
                                     start=True, stop=True).then_inc(mm1.sem, 1)
                for c in range(NCH):
                    pe.wait_ge(sqd.sem, c + 1)
                    nc.tensor.matmul(core.ps[:, 4 + c, 0:CH], core.ones[:, :], x2[:, c * CH:(c + 1) * CH],
                                     start=True, stop=True).then_inc(mm2.sem, 1)

            @block.scalar
            def _(act):
                for c in range(NCH):
                    s = slice(c * CH, (c + 1) * CH)
                    act.wait_ge(qpd.sem, c + 1)
                    nc.scalar.activation(x2[:, s], qp[:, s], ACT.Square).then_inc(sqd.sem, 1)
                act.wait_ge(sqd.sem, NCH)
                for c in range(NCH):
                    act.wait_ge(mm2.sem, c + 1)
                    nc.scalar.activation(x2[:, c * CH:(c + 1) * CH], core.ps[:, 4 + c, 0:CH],
                                         ACT.Sqrt).then_inc(nrm.sem, 1)

            @block.vector
            def _(dve):
                link = core.linker(dve, "dve")
                for c in range(NCH):
                    dve.wait_ge(mm1.sem, c + 1)
                    nc.vector.tensor_scalar(qp[:, c * CH:(c + 1) * CH], core.ps[:, c, 0:CH],
                                            v(core, "L0_bq"), None, ALU.add).then_inc(qpd.sem, 1)
                dve.wait_ge(qpd.sem, NCH)
                for c in range(NCH):
                    s = slice(c * CH, (c + 1) * CH)
                    dve.wait_ge(nrm.sem, c + 1)
                    link(nc.vector.tensor_scalar(x2[:, s], x2[:, s], 1e-12, None, ALU.max))
                    link(nc.vector.reciprocal(x2[:, s], x2[:, s]))
                    link(nc.vector.tensor_tensor(qn[:, s], qp[:, s], x2[:, s], ALU.mult))


HB = B // 2
NP = HB // 2


def attention(core, L, src, bo, scale=1.0, keep_max=True, clip=None, rk=None, dh=8, csum=None):
    nc, d = core.nc, core.d
    outer = ExitStack()
    few = dh == DH
    N = core.sb(f"{L}_N", [KA, H, D], F32, outer) if not few or clip is not None else None
    M = core.sb(f"{L}_M", [D, H, KA], F32, outer)
    cq = core.sb(f"{L}_cq", [KA, H], F32, outer) if keep_max else None
    ok = core.sb(f"{L}_ok", [128, 2 * QV], F32, outer) if clip is not None else None
    values = None
    if few:
        values = (core.sb(f"{L}_wve", [KA, H // 2 * VW], F32, outer),
                  core.sb(f"{L}_woe", [128, 4, D], F32, outer),
                  [core.sb(f"{L}_values{s}", [KP, KT, H // 2, 32], F32, outer) for s in range(2)])
    with outer:
        fold_weights(core, L, M, N, cq, scale, keep_max, dh, values)
        if few:
            with nc.Block() as block:
                @block.gpsimd
                def _(pool):
                    link = core.linker(pool, "pool")
                    for t in values[2]:
                        link(nc.gpsimd.memset(t[:, :, :, :], 0.0))
                    if ok is not None:
                        link(nc.gpsimd.memset(ok[:, :], 1.0))
        for half in range(2):
            with ExitStack() as ctx:
                qp = core.sb(f"{L}_qp{half}", [KM if keep_max else KA, HB, HQ], F32, ctx)
                make_queries(core, qp, M, cq, src, scale, half)
                attend_half(core, f"{L}{half}", qp, N, bo, half, keep_max, clip, rk, ok, values, ctx)
        if clip is not None:
            uniform_if_nan(core, L, N, ok, csum, bo, outer)


QV = H // 4 * NQ


def fold_weights(core, L, M, N, cq, scale, keep_max, dh, values):
    nc, d, ps = core.nc, core.d, core.ps
    with ExitStack() as c2:
        w_in, m_mm, m_sb = (core.sig(f"{L}_{n}") for n in ("w_in", "fold_mm", "fold_sb"))
        loads = []
        if N is not None:
            wva = core.sb(f"{L}_wva", [dh, H, KA], F32, c2)
            wo = core.sb(f"{L}_wo", [dh, H, D], F32, c2)
            loads += [(wva[:, :, :], "WvA"), (wo[:, :, :], "Wo")]
        if keep_max:
            wqt = core.sb(f"{L}_wqt", [dh, H, D], F32, c2)
            wka = core.sb(f"{L}_wka", [dh, H, KA], F32, c2)
            bqh = core.sb(f"{L}_bqh", [dh, H], F32, c2)
            loads += [(wqt[:, :, :], "WqT"), (wka[:, :, :], "WkAT"), (bqh[:, :], "bqh")]
        else:
            loads += [(M[:, :, :], "WkBD")]
        if values:
            loads += [(values[0][:, :], "WvE"), (values[1][:, :, :], "WoE")]
        nw = 16 * len(loads)
        with nc.Block() as block:
            @block.sync
            def _(sp):
                for dst, name in loads:
                    sp.dma_start(dst, d[f"{L}_{name}"]).then_inc(w_in.sem, 16)
                sp.wait_ge(w_in.sem, nw)

            if N is None and not keep_max:
                return

            @block.tensor
            def _(pe):
                pe.wait_ge(w_in.sem, nw)
                for h in range(H):
                    g, k = h // 4, h % 4
                    mm = nc.tensor.matmul(ps[0:KA, 4 + g, k * D:(k + 1) * D], wva[:, h, :], wo[:, h, :],
                                          start=True, stop=True)
                    if keep_max:
                        mm = nc.tensor.matmul(ps[:, g, k * KA:(k + 1) * KA], wqt[:, h, :], wka[:, h, :],
                                              start=True, stop=True)
                mm.then_inc(m_mm.sem, 1)
                if keep_max:
                    pe.wait_ge(m_sb.sem, 4)
                    for h in range(H):
                        mm = nc.tensor.matmul(ps[0:KA, 0, h:h + 1], wka[:, h, :], bqh[:, h:h + 1],
                                              start=True, stop=True)
                    mm.then_inc(m_mm.sem, 1)

            @block.vector
            def _(dve):
                dve.wait_ge(m_mm.sem, 1)
                if keep_max:
                    for g in range(4):
                        nc.vector.tensor_copy(M[:, 4 * g:4 * g + 4, :].rearrange("p h n -> p (h n)"),
                                              ps[:, g, 0:4 * KA]).then_inc(m_sb.sem, 1)
                for g in range(4):
                    nc.vector.tensor_copy(N[:, 4 * g:4 * g + 4, :].rearrange("p h n -> p (h n)"),
                                          ps[0:KA, 4 + g, :]).then_inc(m_sb.sem, 1)
                if keep_max:
                    dve.wait_ge(m_mm.sem, 2)
                    nc.vector.tensor_scalar(cq[:, :], ps[0:KA, 0, 0:H], scale, None,
                                            ALU.mult).then_inc(m_sb.sem, 1)


def make_queries(core, qp, M, cq, src, scale, half):
    nc, ps = core.nc, core.ps
    qmm, qa, qd_ = core.queries_made, core.queries_act, core.queries_dve
    nch = NCH // 2
    with nc.Block() as block:
        @block.tensor
        def _(pe):
            with pe.Fori(0, nch) as c:
                for h in range(H):
                    w = qa if h % 2 == 0 else qd_
                    pe.wait_ge(w.sem, w.at(8 * c + h // 2 + 1))
                    nc.tensor.matmul(ps[0:KA, h % 8, 0:CH], M[:, h, :],
                                     src[:, bass.ds(c * CH + half * nch * CH, CH)],
                                     start=True, stop=True).then_inc(qmm.sem, 1)

        def bank(h):
            return ps[0:KA, h % 8, 0:CH].rearrange("p (b q) -> p b q", q=NQ)

        def place(h, c):
            return qp[0:KA, bass.ds(c * 8, 8), h * NQ:(h + 1) * NQ]

        @block.scalar
        def _(act):
            act.sem_inc(qa.sem, 4)
            with act.Fori(0, nch) as c:
                for h in range(0, H, 2):
                    act.wait_ge(qmm.sem, qmm.at(H * c + h + 1))
                    if cq is not None:
                        ins = nc.scalar.activation(place(h, c), bank(h), ACT.Identity,
                                                   bias=cq[:, h:h + 1], scale=scale)
                    else:
                        ins = nc.scalar.activation(place(h, c), bank(h), ACT.Copy)
                    ins.then_inc(qa.sem, 1)

        @block.vector
        def _(dve):
            dve.sem_inc(qd_.sem, 4)
            with dve.Fori(0, nch) as c:
                for h in range(1, H, 2):
                    dve.wait_ge(qmm.sem, qmm.at(H * c + h + 1))
                    if cq is not None:
                        ins = nc.vector.tensor_scalar(place(h, c), bank(h), scale, cq[:, h:h + 1],
                                                      ALU.mult, ALU.add)
                    else:
                        ins = nc.vector.tensor_copy(place(h, c), bank(h))
                    ins.then_inc(qd_.sem, 1)
    qmm.base += H * nch
    qa.base += H * nch // 2 + 4
    qd_.base += H * nch // 2 + 4


PRODUCTS = [(0, 0), (0, 1), (1, 0), (1, 1), (0, 2), (2, 0)]
PF = 2 * DH
PAIRS = H // 2


def in_parts(link, nc, parts, rest, src):
    for n, part in enumerate(parts):
        link(nc.vector.tensor_copy(part, src))
        if n < 2:
            link(nc.vector.tensor_tensor(rest, src, part, ALU.subtract))
            src = rest


def attention_normed(core, L, qn, bo, rk):
    nc, d, ps = core.nc, core.d, core.ps
    NPB = B // 2
    NAMES = ["w_in", "zeroed", "q_turned", "q_split", "q_in", "ctx_in0", "ctx_in1", "keys_in0",
             "keys_in1", "keys_made", "keys_first", "keys_rest", "keys_second", "keys_third",
             "scored", "exped", "weighed", "u_copied", "values_made", "values_copied", "sums_spread",
             "sums_inverted", "u_normed", "projected", "out_copied"]
    S = {n: core.sig(f"{L}_{n}").sem for n in NAMES}
    KEYS0, KEYS1 = (8, 9, 10), (18, 19, 20)
    VALUES1, VALUES0 = (7, 9, 11, 13), (16, 18, 20, 22)
    with ExitStack() as ctx:
        def sb(n, shape, dt=F32, c=ctx):
            return core.sb(f"{L}_{n}", shape, dt, c)
        QS = sb("qs", [128, 2, PAIRS, T], BF16)
        KS = [sb(f"ks{s}", [128, PAIRS, NK], BF16) for s in range(2)]
        VS = [sb(f"vs{s}", [KP, KT, PAIRS, 32]) for s in range(2)]
        WK, WVE, WOE = sb("wk", [KA, D]), sb("wve", [KA, PAIRS * VW]), sb("woe", [128, 4, D])

        with ExitStack() as c1:
            turn, rest = sb("turn", [D, D], c=c1), sb("q_rest", [D, T], c=c1)
            qparts = [sb(f"q_part{n}", [D, T], BF16, c1) for n in range(3)]
            with nc.Block() as block:
                @block.sync
                def _(sp):
                    for dst, n in ((turn[:, :], "turn"), (WK[:, :], "L0_WkP"), (WVE[:, :], "L0_WvE"),
                                   (WOE[:, :, :], "L0_WoE")):
                        sp.dma_start(dst, d[n]).then_inc(S["w_in"], 16)
                    sp.wait_ge(S["w_in"], 64)
                    sp.wait_ge(S["q_split"], 1)
                    sp.wait_ge(S["zeroed"], 3)
                    for u, (_, part) in enumerate(PRODUCTS):
                        for j in range(2):
                            r0 = PF * u + DH * j
                            sp.dma_start(QS[r0:r0 + DH, j, :, :].rearrange("p m n -> p (m n)"),
                                         qparts[part][64 * j:64 * j + 64, :]).then_inc(S["q_in"], 16)
                    sp.wait_ge(S["q_in"], 16 * 2 * len(PRODUCTS))

                @block.tensor
                def _(pe):
                    pe.wait_ge(S["w_in"], 64)
                    for c in range(NCH):
                        mm = nc.tensor.matmul(ps[:, c, 0:CH], turn[:, :], qn[:, c * CH:(c + 1) * CH],
                                              start=True, stop=True)
                    mm.then_inc(S["q_turned"], 1)

                @block.gpsimd
                def _(pool):
                    nc.gpsimd.memset(QS[:, 0, :, :].rearrange("p m n -> p (m n)").bitcast(F32), 0.0
                                     ).then_inc(S["zeroed"], 1)
                    link = core.linker(pool, "pool")
                    for s in range(2):
                        link(nc.gpsimd.memset(VS[s][:, :, :, :], 0.0))

                @block.scalar
                def _(act):
                    act.wait_ge(S["q_turned"], 1)

                @block.vector
                def _(dve):
                    link = core.linker(dve, "dve")
                    nc.vector.memset(QS[:, 1, :, :].rearrange("p m n -> p (m n)").bitcast(F32), 0.0
                                     ).then_inc(S["zeroed"], 1)
                    for s in range(2):
                        link(nc.vector.memset(KS[s][96:128, :, :].rearrange("p m n -> p (m n)")
                                              .bitcast(F32), 0.0))
                    dve.wait_ge(S["q_turned"], 1)

                    def chunks(t):
                        return t[:, :].rearrange("p (c n) -> p c n", c=NCH)
                    in_parts(link, nc, [chunks(t) for t in qparts], chunks(rest), ps[:, 0:NCH, 0:CH])
                    nc.vector.memset(rest[:, 0:1], 0.0).then_inc(S["q_split"], 1)
                    dve.sem_inc(S["zeroed"], 1)

        CT = [sb(f"ct{s}", [KA, NK]) for s in range(2)]
        kparts = [sb(f"k_part{n}", [D, NK], BF16) for n in range(3)]
        krest = sb("k_rest", [D, NK])
        P = sb("p", [KP, 2, HQ])
        UE, RD, UN = (sb(n, [128, 2, QV]) for n in ("ue", "rd", "un"))
        SB = [ps[0:KP, 0:2, 0:HALF], ps[0:KP, 2:4, 0:HALF]]

        def body_pairs(eng, body):
            body(0, False, True)
            with eng.Fori(1, NPB - 1) as i:
                body(i, True, True)
            body(NPB - 1, True, False)

        def key_steps(k, nxt, i, do):
            if k in KEYS0 and nxt:
                do(i + 1, 0, KEYS0.index(k))
            if k in KEYS1 and nxt:
                do(i + 1, 1, KEYS1.index(k))

        def value_steps(k, nxt, i, do):
            if k in VALUES1:
                do(i, 1, VALUES1.index(k))
            if k in VALUES0 and nxt:
                do(i + 1, 0, VALUES0.index(k))

        def columns(c):
            return slice(c * 500, (c + 1) * 500)

        with nc.Block() as block:
            @block.sync
            def _(sp):
                def load(i, s):
                    sp.dma_start(CT[s][:, :], d["ctxT"][bass.ds(2 * i + s, 1), 0:KA, :]
                                 .rearrange("o p n -> (o p) n")).then_inc(S[f"ctx_in{s}"], 16)

                def place_keys(i, s):
                    sp.wait_ge(S["keys_third"], 6 * i + 3 * s + 6)
                    for u, (part, _) in enumerate(PRODUCTS):
                        sp.dma_start(KS[s][PF * u:PF * (u + 1), :, :].rearrange("p m n -> p (m n)"),
                                     kparts[part][:, :]).then_inc(S[f"keys_in{s}"], 16)

                def body(i, prev, nxt):
                    if nxt:
                        sp.wait_ge(S["values_made"], 8 * i + 4)
                        load(i + 1, 0)
                    if prev:
                        sp.wait_ge(S["scored"], 24 * i)
                    place_keys(i, 1)
                    if nxt:
                        sp.wait_ge(S["scored"], 24 * i + 12)
                        place_keys(i + 1, 0)
                        sp.wait_ge(S["values_made"], 8 * i + 8)
                        load(i + 1, 1)

                for s in range(2):
                    load(0, s)
                place_keys(0, 0)
                body_pairs(sp, body)

            @block.gpsimd
            def _(pool):
                pool.sem_inc(S["keys_third"], 3)

                def third(i, s, c):
                    pool.wait_ge(S["keys_second"], 6 * i + 3 * s + c + 1)
                    nc.gpsimd.tensor_tensor(kparts[2][:, columns(c)], krest[:, columns(c)],
                                            kparts[1][:, columns(c)], ALU.subtract
                                            ).then_inc(S["keys_third"], 1)

                for s in range(2):
                    for c in range(3):
                        third(0, s, c)
                with pool.Fori(1, NPB) as i:
                    for s in range(2):
                        for c in range(3):
                            third(i, s, c)

            @block.tensor
            def _(pe):
                def make_keys(i, s, c):
                    n = 3 * s + c
                    if c == 0:
                        pe.wait_ge(S[f"ctx_in{s}"], 16 * i + 16)
                    pe.wait_ge(S["keys_rest"], 6 * i + n + 1)
                    nc.tensor.matmul(ps[:, 6 + n % 2, 0:500], WK[:, :], CT[s][:, columns(c)],
                                     start=True, stop=True).then_inc(S["keys_made"], 1)

                def make_values(i, s, g):
                    if g == 0:
                        pe.wait_ge(S[f"ctx_in{s}"], 16 * i + 16)
                    pe.wait_ge(S["values_copied"], 8 * i + 4 * s + g + 1)
                    for t in range(3):
                        mm = nc.tensor.matmul(ps[0:KP, 5, t * PAIRS * VW:(t + 1) * PAIRS * VW],
                                              CT[s][:, (3 * g + t) * KP:(3 * g + t + 1) * KP], WVE[:, :],
                                              start=True, stop=True)
                    mm.then_inc(S["values_made"], 1)

                def score(i, n):
                    s, j = n // KT, n % KT
                    if j == 0:
                        pe.wait_ge(S[f"keys_in{s}"], (i + 1) * 16 * len(PRODUCTS))
                    pe.wait_ge(S["exped"], 24 * i + n + 1)
                    for m in range(PAIRS):
                        mm = nc.tensor.matmul(
                            SB[n % 2][:, m // 4, m % 4 * 2 * NQ:(m % 4 + 1) * 2 * NQ]
                            .rearrange("p (j q) -> p j q", j=2), KS[s][:, m, j * KP:(j + 1) * KP],
                            QS[:, :, m, bass.ds((2 * i + s) * NQ, NQ)], start=True, stop=True)
                    mm.then_inc(S["scored"], 1)

                def weigh(i, n):
                    s, j = n // KT, n % KT
                    pe.wait_ge(S["exped"], 24 * i + n + 3)
                    if j == 0:
                        pe.wait_ge(S["u_copied"], 2 * i + s + 1)
                    if j % 3 == 0:
                        pe.wait_ge(S["values_copied"], 8 * i + 4 * s + j // 3 + 2)
                    for m in range(PAIRS):
                        g, c = m % 4, m // 4 * 2 * NQ
                        mm = nc.tensor.matmul(ps[32 * g:32 * g + 32, 4, c:c + 2 * NQ], VS[s][:, j, m, :],
                                              P[:, n % 2, m * 2 * NQ:(m + 1) * 2 * NQ],
                                              start=(j == 0 and m < 4), stop=(j == KT - 1 and m >= 4))
                    mm.then_inc(S["weighed"], 1)

                def of_head(t, j):
                    return t.rearrange("p (s r j q) -> p (s r) j q", s=2, j=2, q=NQ)[:, :, j, :]

                def spread_sums(i):
                    pe.wait_ge(S["u_copied"], 2 * i + 3)
                    for j in range(2):
                        mm = nc.tensor.matmul(of_head(ps[:, 5, 0:2 * QV], j), core.sum_row[:, j, :],
                                              of_head(UE[:, :, :].rearrange("p s n -> p (s n)"), j),
                                              start=True, stop=True)
                    mm.then_inc(S["sums_spread"], 1)

                def project(i):
                    pe.wait_ge(S["u_normed"], i + 2)
                    n = UN[:, :, :].rearrange("p s (r j q) -> p s r j q", j=2, q=NQ)
                    for c in range(4):
                        mm = nc.tensor.matmul(ps[:, 5, 0:2 * NQ].rearrange("p (s q) -> p s q", s=2),
                                              WOE[:, c, :], n[:, :, c // 2, c % 2, :],
                                              start=(c == 0), stop=(c == 3))
                    mm.then_inc(S["projected"], 1)

                def body(i, prev, nxt):
                    for k in range(24):
                        weigh(i, k)
                        if k + 2 < 24:
                            score(i, k + 2)
                        elif nxt:
                            score(i + 1, k - 22)
                        if k == 1 and prev:
                            pe.wait_ge(S["values_copied"], 8 * i + 5)
                            spread_sums(i - 1)
                        if k == 4 and prev:
                            project(i - 1)
                        if k == 7 and prev:
                            pe.wait_ge(S["out_copied"], i)
                        key_steps(k, nxt, i, make_keys)
                        value_steps(k, nxt, i, make_values)

                for c in range(3):
                    make_keys(0, 0, c)
                for g in range(4):
                    make_values(0, 0, g)
                for c in range(3):
                    make_keys(0, 1, c)
                score(0, 0)
                score(0, 1)
                body_pairs(pe, body)
                pe.wait_ge(S["values_copied"], 8 * NPB + 1)
                spread_sums(NPB - 1)
                project(NPB - 1)

            @block.scalar
            def _(act):
                act.sem_inc(S["exped"], 2)
                act.sem_inc(S["u_copied"], 1)

                def first(i, s, c, after=True):
                    act.wait_ge(S["keys_made"], 6 * i + 3 * s + c + 1)
                    if c == 0 and after:
                        act.wait_ge(S[f"keys_in{1 - s}"], (i + s) * 16 * len(PRODUCTS))
                    nc.scalar.activation(kparts[0][:, columns(c)], ps[:, 6 + (3 * s + c) % 2, 0:500],
                                         ACT.Copy).then_inc(S["keys_first"], 1)

                def second(i, s, c):
                    act.wait_ge(S["keys_rest"], 6 * i + 3 * s + c + 3)
                    nc.scalar.activation(kparts[1][:, columns(c)], krest[:, columns(c)],
                                         ACT.Copy).then_inc(S["keys_second"], 1)

                def out(i):
                    act.wait_ge(S["projected"], i + 1)
                    nc.scalar.activation(core.OT[:, bass.ds(2 * i * NQ, 2 * NQ)], ps[:, 5, 0:2 * NQ],
                                         ACT.Identity, bias=bo).then_inc(S["out_copied"], 1)

                def copy_sums(i, s):
                    act.wait_ge(S["weighed"], 24 * i + 12 * s + 12)
                    act.wait_ge(S["u_normed"], i + 1)
                    nc.scalar.activation(UE[:, s, :], ps[:, 4, 0:QV], ACT.Copy
                                         ).then_inc(S["u_copied"], 1)

                def body(i, prev, nxt):
                    for n in range(24):
                        if n == 7 and prev:
                            out(i - 1)
                        if n == 1 and prev:
                            copy_sums(i - 1, 1)
                        if n == 13:
                            copy_sums(i, 0)
                        key_steps(n - 2, nxt, i, first)
                        key_steps(n - 3, nxt, i, second)
                        act.wait_ge(S["scored"], 24 * i + n + 1)
                        if prev or n >= 2:
                            act.wait_ge(S["weighed"], 24 * i + n - 1)
                        nc.scalar.activation(P[:, n % 2, :].rearrange("p (a n) -> p a n", a=2), SB[n % 2],
                                             ACT.Exp, scale=rk[:, bass.ds(24 * i + n, 1)]
                                             ).then_inc(S["exped"], 1)

                for c in range(3):
                    first(0, 0, c, False)
                    second(0, 0, c)
                for c in range(3):
                    first(0, 1, c)
                    second(0, 1, c)
                body_pairs(act, body)
                copy_sums(NPB - 1, 1)
                out(NPB - 1)

            @block.vector
            def _(dve):
                dve.sem_inc(S["keys_rest"], 2)
                dve.sem_inc(S["u_normed"], 1)
                dve.sem_inc(S["values_copied"], 1)

                def rest_of_keys(i, s, c):
                    n = 6 * i + 3 * s + c
                    dve.wait_ge(S["keys_first"], n + 1)
                    dve.wait_ge(S["keys_third"], n + 1)
                    nc.vector.tensor_tensor(krest[:, columns(c)], ps[:, 6 + (3 * s + c) % 2, 0:500],
                                            kparts[0][:, columns(c)], ALU.subtract
                                            ).then_inc(S["keys_rest"], 1)

                def copy_values(i, s, g):
                    dve.wait_ge(S["values_made"], 8 * i + 4 * s + g + 1)
                    w = PAIRS * VW
                    nc.vector.tensor_copy(VS[s][:, 3 * g:3 * g + 3, :, 0:VW],
                                          ps[0:KP, 5, 0:3 * w].rearrange("p (t m c) -> p t m c", t=3, c=VW)
                                          ).then_inc(S["values_copied"], 1)

                def norm_sums(i):
                    dve.wait_ge(S["sums_spread"], i + 1)
                    nc.vector.reciprocal(RD[:, :, :].rearrange("p s n -> p (s n)"), ps[:, 5, 0:2 * QV]
                                         ).then_inc(S["sums_inverted"], 1)
                    dve.wait_ge(S["sums_inverted"], i + 1)
                    nc.vector.tensor_tensor(UN[:, :, :], UE[:, :, :], RD[:, :, :], ALU.mult
                                            ).then_inc(S["u_normed"], 1)

                def body(i, prev, nxt):
                    for k in range(24):
                        if k == 2 and prev:
                            norm_sums(i - 1)
                        key_steps(k, nxt, i, rest_of_keys)
                        value_steps(k, nxt, i, copy_values)

                for c in range(3):
                    rest_of_keys(0, 0, c)
                for g in range(4):
                    copy_values(0, 0, g)
                for c in range(3):
                    rest_of_keys(0, 1, c)
                body_pairs(dve, body)
                norm_sums(NPB - 1)


ATTEND = {"scored": 24 * NP, "exped": 24 * NP + 2, "weighed": 24 * NP + 2, "u_copied": 2 * NP + 1,
          "projected": NP, "out_copied": NP}
ATTEND_WIDE = {"ctx_in0": 32 * NP, "ctx_in1": 32 * NP, "den_out": 32 * NP, "den_in": 32 * NP,
               "den_inverted": 2 * NP, "den_spread": 2 * NP, "u_normed": 2 * NP + 1}
ATTEND_FEW = {"ctx_in0": 16 * NP, "ctx_in1": 16 * NP, "values_made": 8 * NP,
              "values_copied": 8 * NP + 1, "den_spread": NP, "den_inverted": NP, "u_normed": NP + 1}
ATTEND_MAX = {"qb_ready0": NP, "qb_ready1": NP, "ctr_in0": 16 * NP, "ctr_in1": 16 * NP,
              "chunk_scored": 24 * NP, "chunk_maxed": 24 * NP, "max_ready": 2 * NP,
              "max_turned": 2 * NP, "max_negated": 2 * NP, "max_in0": 16 * NP, "max_in1": 16 * NP}
ATTEND_CLIP = {"clip_max": 2 * NP, "low_spread": 2 * NP, "low_ready": 2 * NP, "clipped": 24 * NP + 2,
               "sel_ready": 2, "nan_seen": 2 * NP}
ATTEND_ALL = {**ATTEND, **ATTEND_WIDE, **ATTEND_FEW, **ATTEND_MAX, **ATTEND_CLIP}


def attend_half(core, tag, qp, N, bo, half, keep_max, clip, rk, ok, values, ctx):
    nc, d, ps = core.nc, core.d, core.ps
    S = core.attend

    def at(name, n):
        return S[name].sem, S[name].at(n)

    CT = [core.sb(f"{tag}_ct{s}", [KM, NK], F32, ctx) for s in range(2)]
    P = core.sb(f"{tag}_p", [KP, 2, HQ], F32, ctx)
    if values:
        WVE, WOE, VS = values
        UE, RD, UN = (core.sb(f"{tag}_{n}", [128, 2, QV], F32, ctx) for n in ("ue", "rd", "un"))
        eq = core.sb(f"{tag}_eq", [128, 2, QV], F32, ctx) if clip is not None else None
    else:
        CN = [core.sb(f"{tag}_cn{s}", [KP, KT, KA], F32, ctx) for s in range(2)]
        UE = core.sb(f"{tag}_ue", [KA, HQ], F32, ctx)
        UN = core.sb(f"{tag}_un", [KA, H, 2, NQ], F32, ctx)
        RC = core.sb(f"{tag}_rc", [KA, HQ], F32, ctx)
        dn, dr = (core.sb(f"{tag}_{n}", [8, TT], F32, ctx) for n in ("dn", "dr"))
    if keep_max:
        QB = [core.sb(f"{tag}_qb{s}", [KA, HQ], F32R, ctx) for s in range(2)]
        CR = [core.sb(f"{tag}_cr{s}", [KA, NK], F32R, ctx) for s in range(2)]
        mp = core.sb(f"{tag}_mp", [TT, 24], F32, ctx)
        mu = core.sb(f"{tag}_mu", [TT, 8], F32, ctx)
        mc = [core.sb(f"{tag}_mc{s}", [TT, 8], F32, ctx) for s in range(2)]
        mt = [core.sb(f"{tag}_mt{s}", [8, TT], F32, ctx) for s in range(2)]
    if clip is not None:
        LB = [core.sb(f"{tag}_lb{s}", [KP, HQ], F32, ctx) for s in range(2)]
        sel = core.sb(f"{tag}_sel", [KM, 128], F32, ctx)
    KS = KM if keep_max else KA
    SB = [ps[0:KP, 0:2, 0:HALF], ps[0:KP, 2:4, 0:HALF]]
    U = ps[:, 4, 0:QV] if values else ps[0:KA, 4:6, 0:HALF]
    b0 = half * HB
    NEXT_VALUES, FIRST_VALUES = (7, 9, 11, 13), (16, 18, 20, 22)

    def two(ap):
        return ap.rearrange("p (a n) -> p a n", a=2)

    def heads(ap):
        return ap.rearrange("p (h q) -> p h q", q=NQ)

    def query(i, s, a, rows):
        return qp[0:rows, bass.ds(2 * i + s, 1), a * HALF:(a + 1) * HALF].rearrange("p o n -> p (o n)")

    def pairs(eng, body, last=1):
        body(0, False, True, True)
        with eng.Fori(1, NP - last) as i:
            body(i, True, True, True)
        for i in range(NP - last, NP):
            body(i, True, i + 1 < NP, i + 2 < NP)

    with nc.Block() as block:
        @block.sync
        def _(sp):
            def load(i, s):
                bb = bass.ds(2 * i + s + b0, 1)
                sp.dma_start(CT[s][:, :], d["ctxT"][bb, :, :].rearrange("o p n -> (o p) n")
                             ).then_inc(S[f"ctx_in{s}"].sem, 16)
                if values:
                    return
                sp.dma_start(CN[s][:, :, :].rearrange("p j n -> p (j n)"),
                             d["ctxN"][bb, :, :].rearrange("o p n -> (o p) n")
                             ).then_inc(S[f"ctx_in{s}"].sem, 16)

            def invert(i, s):
                sp.wait_ge(*at("u_copied", 2 * i + s + 2))
                sp.dma_start(dn[:, :], UE[DC:KA, :]).then_inc(S["den_out"].sem, 16)
                sp.wait_ge(*at("den_inverted", 2 * i + s + 1))
                sp.dma_start(RC[DC:KA, :], dr[:, :]).then_inc(S["den_in"].sem, 16)

            def body(i, prev, nxt, after):
                if prev and not values:
                    invert(i - 1, 1)
                for s in range(2):
                    if nxt:
                        if values:
                            sp.wait_ge(*at("scored", 24 * i + 12 * s + 12))
                        else:
                            sp.wait_ge(*at("weighed", 24 * i + 12 * s + 14))
                        load(i + 1, s)
                    if s == 0 and not values:
                        invert(i, 0)

            for s in range(2):
                load(0, s)
            pairs(sp, body)
            if not values:
                invert(NP - 1, 1)

        @block.gpsimd
        def _(pool):
            def first_pass_inputs(i, s):
                nc.gpsimd.tensor_copy(QB[s][:, :], qp[0:KA, bass.ds(2 * i + s, 1), :]
                                      .rearrange("p o n -> p (o n)")).then_inc(S[f"qb_ready{s}"].sem, 1)
                pool.dma_start(CR[s][:, :], d["ctxT"][bass.ds(2 * i + s + b0, 1), 0:KA, :]
                               .rearrange("o p n -> (o p) n")).then_inc(S[f"ctr_in{s}"].sem, 16)

            def max_row(i, s):
                pool.wait_ge(*at("max_negated", 2 * i + s + 1))
                pool.dma_start(qp[KA:KM, bass.ds(2 * i + s, 1), :].rearrange("p o n -> p (o n)"),
                               mt[s][:, :]).then_inc(S[f"max_in{s}"].sem, 16)

            if clip is not None:
                nc.gpsimd.memset(sel[:, :], 1.0).then_inc(S["sel_ready"].sem, 1)
                pool.wait_ge(*at("sel_ready", 1))
                nc.gpsimd.affine_select(out=sel[:, :], in_=sel[:, :], compare_op=ALU.is_ge, fill=0.0,
                                        base=-(KM - 1), pattern=[[0, 128]],
                                        channel_multiplier=1).then_inc(S["sel_ready"].sem, 1)
            if keep_max:
                for s in range(2):
                    first_pass_inputs(0, s)
                for s in range(2):
                    pool.wait_ge(*at("chunk_scored", 12 * s + 12))
                    first_pass_inputs(1, s)
                max_row(0, 0)

            def body(i, prev, nxt, after):
                max_row(i, 1)
                if after:
                    pool.wait_ge(*at("chunk_scored", 24 * i + 36))
                    first_pass_inputs(i + 2, 0)
                if nxt:
                    max_row(i + 1, 0)
                if after:
                    pool.wait_ge(*at("chunk_scored", 24 * i + 48))
                    first_pass_inputs(i + 2, 1)

            if keep_max:
                pairs(pool, body, 2)

        @block.tensor
        def _(pe):
            def chunks(i, s, k, ahead=False):
                if k == 0:
                    pe.wait_ge(*at(f"ctr_in{s}", 16 * i + 16))
                    pe.wait_ge(*at(f"qb_ready{s}", i + 1))
                if not ahead:
                    pe.wait_ge(*at("chunk_maxed", 24 * i + 12 * s + k))
                elif 12 * s + k >= 2:
                    pe.wait_ge(*at("chunk_maxed", 12 * s + k - 1))
                bank = 0 if ahead and k % 2 == 1 else 6
                for a in range(2):
                    t, c = (2 * k + a) // 3, (2 * k + a) % 3
                    mm = nc.tensor.matmul(ps[0:TT, bank + a, 0:500], QB[s][:, t * TT:(t + 1) * TT],
                                          CR[s][:, c * 500:(c + 1) * 500], start=True, stop=True)
                mm.then_inc(S["chunk_scored"].sem, 1)

            def turn_max(i, s):
                pe.wait_ge(*at("max_ready", 2 * i + s + 1))
                nc.tensor.transpose(ps[0:8, 6, 0:TT], mc[s][:, :], core.ident[0:TT, 0:TT]
                                    ).then_inc(S["max_turned"].sem, 1)

            def spread_low(i, s):
                pe.wait_ge(*at(f"max_in{s}", 16 * i + 16))
                for a in range(2):
                    mm = nc.tensor.matmul(ps[0:KP, 6 + a, 0:HALF], sel[:, 0:KP], query(i, s, a, KM),
                                          start=True, stop=True)
                mm.then_inc(S["low_spread"].sem, 1)

            def spread_den(i, s):
                pe.wait_ge(*at("den_in", 32 * i + 16 * s + 16))
                for a in range(2):
                    mm = nc.tensor.matmul(ps[0:KA, 6 + a, 0:HALF], core.ones[DC:KA, 0:KA],
                                          RC[DC:KA, a * HALF:(a + 1) * HALF], start=True, stop=True)
                mm.then_inc(S["den_spread"].sem, 1)

            def project(i):
                pe.wait_ge(*at("u_normed", 2 * i + 3))
                for h in range(H):
                    mm = nc.tensor.matmul(ps[:, 6, 0:2 * NQ], N[:, h, :],
                                          UN[:, h, :, :].rearrange("p s q -> p (s q)"),
                                          start=(h == 0), stop=(h == H - 1))
                mm.then_inc(S["projected"].sem, 1)

            def columns(t, j):
                return t.rearrange("p (s r j q) -> p (s r) j q", s=2, j=2, q=NQ)[:, :, j, :]

            def spread_sums(i, is_last=False):
                pe.wait_ge(*at("values_copied", 8 * i + 8 + (1 if is_last else 5)))
                pe.wait_ge(*at("u_copied", 2 * i + 3))
                for j in range(2):
                    mm = nc.tensor.matmul(columns(ps[:, 5, 0:2 * QV], j), core.sum_row[:, j, :],
                                          columns(UE[:, :, :].rearrange("p s n -> p (s n)"), j),
                                          start=True, stop=True)
                mm.then_inc(S["den_spread"].sem, 1)

            def project_sums(i):
                pe.wait_ge(*at("u_normed", i + 2))
                n = UN[:, :, :].rearrange("p s (r j q) -> p s r j q", j=2, q=NQ)
                for c in range(4):
                    mm = nc.tensor.matmul(ps[:, 5, 0:2 * NQ].rearrange("p (s q) -> p s q", s=2),
                                          WOE[:, c, :], n[:, :, c // 2, c % 2, :],
                                          start=(c == 0), stop=(c == 3))
                mm.then_inc(S["projected"].sem, 1)

            def make_values(i, s, g):
                if g == 0:
                    pe.wait_ge(*at(f"ctx_in{s}", 16 * i + 16))
                pe.wait_ge(*at("values_copied", 8 * i + 4 * s + g + 1))
                for t in range(3):
                    j = 3 * g + t
                    mm = nc.tensor.matmul(ps[0:KP, 5, t * H // 2 * VW:(t + 1) * H // 2 * VW],
                                          CT[s][0:KA, j * KP:(j + 1) * KP], WVE[:, :],
                                          start=True, stop=True)
                mm.then_inc(S["values_made"].sem, 1)

            def bank5(i, k, prev, nxt):
                if k == 1 and prev:
                    spread_sums(i - 1)
                if k == 4 and prev:
                    project_sums(i - 1)
                if k == 7 and prev:
                    pe.wait_ge(*at("out_copied", i))
                if k in NEXT_VALUES:
                    make_values(i, 1, NEXT_VALUES.index(k))
                if k in FIRST_VALUES and nxt:
                    make_values(i + 1, 0, FIRST_VALUES.index(k))

            def score(i, n):
                s, j = n // KT, n % KT
                if j == 0:
                    n_in = 16 if values else 32
                    pe.wait_ge(*at(f"ctx_in{s}", n_in * i + n_in))
                    if keep_max:
                        pe.wait_ge(*at(f"max_in{s}", 16 * i + 16))
                pe.wait_ge(*at("exped" if clip is None else "clipped", 24 * i + n + 1))
                for a in range(2):
                    mm = nc.tensor.matmul(SB[n % 2][:, a, :], CT[s][0:KS, j * KP:(j + 1) * KP],
                                          query(i, s, a, KS), start=True, stop=True)
                mm.then_inc(S["scored"].sem, 1)

            def weigh(i, n):
                s, j = n // KT, n % KT
                pe.wait_ge(*at("exped", 24 * i + n + 3))
                if j == 0:
                    pe.wait_ge(*at("u_copied", 2 * i + s + 1))
                if values:
                    if j % 3 == 0:
                        pe.wait_ge(*at("values_copied", 8 * i + 4 * s + j // 3 + 2))
                    for m in range(H // 2):
                        g, c = m % 4, m // 4 * 2 * NQ
                        mm = nc.tensor.matmul(U[32 * g:32 * g + 32, c:c + 2 * NQ], VS[s][:, j, m, :],
                                              P[:, n % 2, m * 2 * NQ:(m + 1) * 2 * NQ],
                                              start=(j == 0 and m < 4), stop=(j == KT - 1 and m >= 4))
                    mm.then_inc(S["weighed"].sem, 1)
                    return
                for a in range(2):
                    mm = nc.tensor.matmul(U[:, a, :], CN[s][:, j, :], P[:, n % 2, a * HALF:(a + 1) * HALF],
                                          start=(j == 0), stop=(j == KT - 1))
                mm.then_inc(S["weighed"].sem, 1)

            def settled(i, k, prev, nxt):
                if k == 0 and keep_max:
                    pe.wait_ge(*at("max_negated", 2 * i + 2))
                if k == 4 and prev and not values:
                    pe.wait_ge(*at("u_normed", 2 * i + 1))
                if k == 6 and prev and not values:
                    pe.wait_ge(*at("out_copied", i))
                if k == 8 and clip is not None:
                    pe.wait_ge(*at("low_ready", 2 * i + 2))
                if k == 12 and nxt and keep_max:
                    pe.wait_ge(*at("max_negated", 2 * i + 3))
                if k == 17 and not values:
                    pe.wait_ge(*at("u_normed", 2 * i + 2))
                if k == 19 and nxt and clip is not None:
                    pe.wait_ge(*at("low_ready", 2 * i + 3))

            ASIDE = (0, 4, 6, 8, 12, 17, 19)

            def aside(i, k, prev, nxt):
                if k not in ASIDE:
                    return
                if keep_max and nxt:
                    pe.wait_ge(*at("chunk_maxed", 24 * i + 24 + k + 1))
                elif k != 0:
                    settled(i, ASIDE[ASIDE.index(k) - 1], prev, nxt)
                if k == 0 and keep_max:
                    turn_max(i, 1)
                if k == 4 and prev and not values:
                    spread_den(i - 1, 1)
                if k == 6 and prev and not values:
                    project(i - 1)
                if k == 8 and clip is not None:
                    spread_low(i, 1)
                if k == 12 and nxt and keep_max:
                    turn_max(i + 1, 0)
                if k == 17 and not values:
                    spread_den(i, 0)
                if k == 19 and nxt and clip is not None:
                    spread_low(i + 1, 0)

            def body(i, prev, nxt, after):
                for k in range(24):
                    weigh(i, k)
                    if keep_max and nxt:
                        if k:
                            settled(i, k - 1, prev, nxt)
                        chunks(i + 1, k // 12, k % 12)
                    if k + 2 < 24:
                        score(i, k + 2)
                    elif nxt:
                        score(i + 1, k - 22)
                    aside(i, k, prev, nxt)
                    if values:
                        bank5(i, k, prev, nxt)

            if keep_max:
                for k in range(24):
                    chunks(0, k // 12, k % 12, True)
                pe.wait_ge(*at("chunk_maxed", 24))
                turn_max(0, 0)
                if clip is not None:
                    pe.wait_ge(*at("sel_ready", 2))
                    pe.wait_ge(*at("max_negated", 1))
                    spread_low(0, 0)
                    pe.wait_ge(*at("low_ready", 1))
                pe.wait_ge(*at("max_negated", 1))
            if values:
                for g in range(4):
                    make_values(0, 0, g)
            score(0, 0)
            score(0, 1)
            pairs(pe, body)
            if values:
                spread_sums(NP - 1, True)
                project_sums(NP - 1)
            else:
                pe.wait_ge(*at("u_normed", 2 * NP))
                spread_den(NP - 1, 1)
                project(NP - 1)

        @block.scalar
        def _(act):
            act.sem_inc(S["exped"].sem, 2)
            act.sem_inc(S["u_copied"].sem, 1)

            def out(i):
                act.wait_ge(*at("projected", i + 1))
                nc.scalar.activation(core.OT[:, bass.ds((2 * i + b0) * NQ, 2 * NQ)],
                                     ps[:, 5 if values else 6, 0:2 * NQ],
                                     ACT.Identity, bias=bo).then_inc(S["out_copied"].sem, 1)

            def copy_sums(i, s):
                act.wait_ge(*at("weighed", 24 * i + 12 * s + 14))
                if values:
                    act.wait_ge(*at("u_normed", i + 1))
                    nc.scalar.activation(UE[:, s, :], U, ACT.Copy).then_inc(S["u_copied"].sem, 1)
                    return
                act.wait_ge(*at("u_normed", 2 * i + s + 1))
                nc.scalar.activation(two(UE[:, :]), U, ACT.Copy).then_inc(S["u_copied"].sem, 1)

            def body(i, prev, nxt, after):
                for n in range(24):
                    if n == 9 and prev:
                        out(i - 1)
                    if n == 1 and prev:
                        copy_sums(i - 1, 1)
                    if n == 13:
                        copy_sums(i, 0)
                    if clip is None:
                        act.wait_ge(*at("scored", 24 * i + n + 1))
                    else:
                        act.wait_ge(*at("clipped", 24 * i + n + 3))
                    act.wait_ge(*at("weighed", 24 * i + n + 1))
                    sc = 1.0 if rk is None else rk[:, bass.ds(24 * i + n + b0 * KT, 1)]
                    src = two(P[:, n % 2, :]) if clip is not None else SB[n % 2]
                    nc.scalar.activation(two(P[:, n % 2, :]), src, ACT.Exp,
                                         scale=sc).then_inc(S["exped"].sem, 1)

            pairs(act, body)
            copy_sums(NP - 1, 1)
            out(NP - 1)

        @block.vector
        def _(dve):
            dve.sem_inc(S["weighed"].sem, 2)
            dve.sem_inc(S["u_normed"].sem, 1)

            def chunk_max(i, s, k, ahead=False):
                bank = 0 if ahead and k % 2 == 1 else 6
                dve.wait_ge(*at("chunk_scored", 24 * i + 12 * s + k + 1))
                nc.vector.tensor_reduce(mp[:, 2 * k:2 * k + 2], ps[0:TT, bank:bank + 2, 0:500],
                                        AX.X, ALU.max).then_inc(S["chunk_maxed"].sem, 1)
                if k < 11:
                    return
                dve.wait_ge(*at("chunk_maxed", 24 * i + 12 * s + 12))
                m3 = mp[:, :].rearrange("p (t c) -> p t c", c=3)
                if clip is None:
                    nc.vector.tensor_reduce(mc[s][:, :], m3, AX.X, ALU.max).then_inc(S["max_ready"].sem, 1)
                else:
                    nc.vector.tensor_reduce(mu[:, :], m3, AX.X, ALU.max).then_inc(S["clip_max"].sem, 1)
                    dve.wait_ge(*at("clip_max", 2 * i + s + 1))
                    nc.vector.tensor_scalar(mc[s][:, :], mu[:, :], clip, -clip, ALU.min,
                                            ALU.max).then_inc(S["max_ready"].sem, 1)
                dve.wait_ge(*at("max_ready", 2 * i + s + 1))

            def turned(i, s):
                dve.wait_ge(*at("max_turned", 2 * i + s + 1))
                nc.vector.tensor_scalar(mt[s][:, :], ps[0:8, 6, 0:TT], -1.0, None,
                                        ALU.mult).then_inc(S["max_negated"].sem, 1)

            def low(i, s):
                dve.wait_ge(*at("low_spread", 2 * i + s + 1))
                nc.vector.tensor_scalar(two(LB[s][:, :]), ps[0:KP, 6:8, 0:HALF], -clip, None,
                                        ALU.add).then_inc(S["low_ready"].sem, 1)

            def clip_tile(i, n):
                dve.wait_ge(*at("scored", 24 * i + n + 1))
                dve.wait_ge(*at("weighed", 24 * i + n + 1))
                if n % KT == 0:
                    dve.wait_ge(*at("low_ready", 2 * i + n // KT + 1))
                nc.vector.scalar_tensor_tensor(out=two(P[:, n % 2, :]), in0=SB[n % 2], scalar=0.0,
                                               in1=two(LB[n // KT][:, :]), op0=ALU.min,
                                               op1=ALU.max).then_inc(S["clipped"].sem, 1)

            def invert(i, s):
                dve.wait_ge(*at("den_out", 32 * i + 16 * s + 16))
                nc.vector.reciprocal(dr[:, :], dn[:, :]).then_inc(S["den_inverted"].sem, 1)

            def norm(i, s):
                dve.wait_ge(*at("den_spread", 2 * i + s + 1))
                for a in range(2):
                    ins = nc.vector.tensor_tensor(UN[:, a * 8:(a + 1) * 8, s, :],
                                                  heads(UE[:, a * HALF:(a + 1) * HALF]),
                                                  heads(ps[0:KA, 6 + a, 0:HALF]), ALU.mult)
                ins.then_inc(S["u_normed"].sem, 1)

            def norm_sums(i):
                dve.wait_ge(*at("den_spread", i + 1))
                nc.vector.reciprocal(RD[:, :, :].rearrange("p s n -> p (s n)"), ps[:, 5, 0:2 * QV]
                                     ).then_inc(S["den_inverted"].sem, 1)
                dve.wait_ge(*at("den_inverted", i + 1))
                nc.vector.tensor_tensor(UN[:, :, :], UE[:, :, :], RD[:, :, :], ALU.mult
                                        ).then_inc(S["u_normed"].sem, 1)
                if clip is not None:
                    nc.vector.tensor_tensor(eq[:, :, :], RD[:, :, :], RD[:, :, :],
                                            ALU.is_equal).then_inc(S["nan_seen"].sem, 1)
                    dve.wait_ge(*at("nan_seen", 2 * i + 1))
                    nc.vector.tensor_tensor(ok[:, :], ok[:, :], eq[:, :, :].rearrange("p s n -> p (s n)"),
                                            ALU.mult).then_inc(S["nan_seen"].sem, 1)
                    dve.wait_ge(*at("nan_seen", 2 * i + 2))

            def copy_values(i, s, g):
                dve.wait_ge(*at("values_made", 8 * i + 4 * s + g + 1))
                w = H // 2 * VW
                nc.vector.tensor_copy(VS[s][:, 3 * g:3 * g + 3, :, 0:VW],
                                      ps[0:KP, 5, 0:3 * w].rearrange("p (t m c) -> p t m c", t=3, c=VW)
                                      ).then_inc(S["values_copied"].sem, 1)

            def body(i, prev, nxt, after):
                for k in range(24):
                    if keep_max and nxt:
                        chunk_max(i + 1, k // 12, k % 12)
                    if clip is not None and k + 2 < 24:
                        clip_tile(i, k + 2)
                    elif clip is not None and nxt:
                        clip_tile(i + 1, k - 22)
                    if k == 0 and keep_max:
                        turned(i, 1)
                    if k == 8 and clip is not None:
                        low(i, 1)
                    if k == 12 and nxt and keep_max:
                        turned(i + 1, 0)
                    if k == 19 and nxt and clip is not None:
                        low(i + 1, 0)
                    if values:
                        if k == 2 and prev:
                            norm_sums(i - 1)
                        if k in NEXT_VALUES:
                            copy_values(i, 1, NEXT_VALUES.index(k))
                        if k in FIRST_VALUES and nxt:
                            copy_values(i + 1, 0, FIRST_VALUES.index(k))
                        continue
                    if k == 2 and prev:
                        invert(i - 1, 1)
                    if k == 4 and prev:
                        norm(i - 1, 1)
                    if k == 14:
                        invert(i, 0)
                    if k == 17:
                        norm(i, 0)

            if clip is not None:
                dve.sem_inc(S["clipped"].sem, 2)
            if keep_max:
                for k in range(24):
                    chunk_max(0, k // 12, k % 12, True)
                turned(0, 0)
                if clip is not None:
                    low(0, 0)
            if values:
                dve.sem_inc(S["values_copied"].sem, 1)
                for g in range(4):
                    copy_values(0, 0, g)
            if clip is not None:
                clip_tile(0, 0)
                clip_tile(0, 1)
            pairs(dve, body)
            if values:
                norm_sums(NP - 1)
            else:
                invert(NP - 1, 1)
                norm(NP - 1, 1)

    for counts in (ATTEND, ATTEND_FEW if values else ATTEND_WIDE, ATTEND_MAX if keep_max else {}, ATTEND_CLIP if clip is not None else {}):
        for name, n in counts.items():
            S[name].base += n


def uniform_if_nan(core, L, N, okays, csum, bo, ctx):
    nc, ps = core.nc, core.ps
    ok = core.sb(f"{L}_row_ok", [128, 1], F32, ctx)
    row_bad = core.sb(f"{L}_row_bad", [128, 1], F32, ctx)
    bad = core.sb(f"{L}_bad", [128, 1], F32, ctx)
    badT = core.sb(f"{L}_badT", [D, T], I32, ctx)
    cm = core.sb(f"{L}_cm", [KA, B], F32, ctx)
    uo = core.sb(f"{L}_uo", [D, B], F32, ctx)
    uT = core.sb(f"{L}_uT", [D, T], F32, ctx)
    reduced, spread = core.sig(f"{L}_ok_reduced"), core.sig(f"{L}_ok_spread")
    with nc.Block() as block:
        @block.vector
        def _(dve):
            link = core.linker(dve, "dve")
            link(nc.vector.tensor_reduce(ok[:, :], okays[:, :], AX.X, ALU.min))
            nc.vector.tensor_scalar(row_bad[:, :], ok[:, :], -1.0, 1.0, ALU.mult, ALU.add).then_inc(reduced.sem, 1)
            nc.vector.tensor_scalar(cm[:, :], csum[:, :], 1.0 / NK, None, ALU.mult).then_inc(reduced.sem, 1)
            dve.wait_ge(spread.sem, 2)
            link(nc.vector.tensor_copy(bad[:, :], ps[:, 0, 0:1]))
            link(nc.vector.tensor_scalar(uo[:, :], ps[:, 1, 0:B], bo, None, ALU.add))
            link(nc.vector.tensor_copy(badT[:, :], bad[:, 0:1].to_broadcast([D, T])))
            link(nc.vector.tensor_copy(uT[:, :].rearrange("p (b q) -> p b q", q=NQ),
                                       uo[:, :].unsqueeze(2).to_broadcast([D, B, NQ])))
            link(nc.vector.copy_predicated(core.OT[:, :], badT[:, :], uT[:, :]))

        @block.tensor
        def _(pe):
            pe.wait_ge(reduced.sem, 2)
            nc.tensor.matmul(ps[:, 0, 0:1], core.ones[:, :], row_bad[:, :], start=True,
                             stop=True).then_inc(spread.sem, 1)
            for h in range(H):
                mm = nc.tensor.matmul(ps[:, 1, 0:B], N[:, h, :], cm[:, :], start=(h == 0), stop=(h == H - 1))
            mm.then_inc(spread.sem, 1)


def top_choice(link, nc, V, im, value, index, hot, tmp, shape, last):
    p, n, e = shape
    link(nc.vector.tensor_reduce(value, V, AX.X, ALU.max))
    link(nc.vector.tensor_tensor(tmp, V, value.unsqueeze(2).to_broadcast([p, n, e]), ALU.is_equal))
    link(nc.vector.tensor_tensor(tmp, tmp, im, ALU.mult))
    link(nc.vector.tensor_reduce(index, tmp, AX.X, ALU.min))
    link(nc.vector.tensor_tensor(hot, im, index.unsqueeze(2).to_broadcast([p, n, e]), ALU.is_equal))
    if not last:
        link(nc.vector.scalar_tensor_tensor(out=V, in0=hot, scalar=-1e30, in1=V, op0=ALU.mult, op1=ALU.add))


def experts0(core, gate):
    nc, d, ps = core.nc, core.d, core.ps
    R = E0 * CAP
    buf = nc.dram_tensor("moe_in", (R, D), F32).ap()
    ydr = nc.dram_tensor("moe_out", (R, D), F32).ap()
    C4 = HID0 // 128
    with ExitStack() as ctx:
        def sb(n, shape, dt=F32, c=ctx):
            return core.sb(f"moe_{n}", shape, dt, c)
        gat = [sb(f"gate{k}", [TT, NT]) for k in range(TOPK0)]
        row = [sb(f"row{k}", [TT, NT], I32) for k in range(TOPK0)]
        NS = 4
        w1 = sb("w1", [D, NS, 2, HID0])
        w2 = sb("w2", [D, NS, 2, HID0])
        b2 = sb("b2", [1, NS, 2, D])
        b1 = sb("b1", [D, E0, C4])
        wt_in = [core.sig(f"moe_wt_in{s}") for s in range(NS)]

        def load_weights(eng, e2, s):
            for src, dst in ((d["L0_w1"], w1), (d["L0_w2"], w2), (d["L0_b2"], b2)):
                eng.dma_start(dst[:, s, :, :], src[bass.ds(e2, 1)].rearrange("o p e n -> (o p) e n")
                              ).then_inc(wt_in[s].sem, 16)

        with ExitStack() as c1:
            gw, gb = sb("gw", [D, E0], c=c1), sb("gb", [TT, E0], c=c1)
            xnn = sb("xnn", [TT, NT, D], c=c1)
            V, im, tmp, mask, cum = (sb(n, [TT, NT, E0], c=c1) for n in ("V", "im", "tmp", "mask", "cum"))
            hot = [sb(f"hot{k}", [TT, NT, E0], c=c1) for k in range(TOPK0)]
            imi = sb("imi", [TT, E0], I32, c=c1)
            tri = sb("tri", [TT, TT], c=c1)
            zero = sb("zero", [128, R * D // 128 // 4], c=c1)
            val = [sb(f"val{k}", [TT, NT], c=c1) for k in range(TOPK0)]
            idx = [sb(f"idx{k}", [TT, NT], c=c1) for k in range(TOPK0)]
            slot, ok, rf, den = (sb(n, [TT, NT], c=c1) for n in ("slot", "ok", "rf", "den"))
            put = [sb(f"put{k}", [TT, NT], I32, c=c1) for k in range(TOPK0)]
            names = ["gw_in", "zeroed", "buf_zeroed", "turned", "logits", "iota", "tri_ready",
                     "rows_copied", "routed", "counted", "exp_in", "exp_out", "put_ready", "scattered"]
            S = {n: core.sig(f"moe_{n}").sem for n in names}
            shp = (TT, NT, E0)
            with nc.Block() as block:
                @block.sync
                def _(sp):
                    sp.dma_start(gw[:, :], d["L0_gw"]).then_inc(S["gw_in"], 16)
                    sp.dma_start(gb[:, :], d["L0_gb"]).then_inc(S["gw_in"], 16)
                    sp.dma_start(b1[:, :, :], d["L0_b1"]).then_inc(S["gw_in"], 16)
                    sp.wait_ge(S["zeroed"], 1)
                    for q in range(4):
                        sp.dma_start(buf[q * R // 4:(q + 1) * R // 4, :].rearrange("(p r) n -> p (r n)", p=128),
                                     zero[:, :]).then_inc(S["buf_zeroed"], 16)
                    for s in range(NS):
                        load_weights(sp, s, s)
                    sp.wait_ge(S["gw_in"], 48)

                @block.tensor
                def _(pe):
                    pe.wait_ge(S["gw_in"], 48)
                    for t in range(NT):
                        nc.tensor.matmul(ps[0:TT, t // 8, (t % 8) * E0:(t % 8 + 1) * E0],
                                         core.xn[:, t * TT:(t + 1) * TT], gw[:, :],
                                         start=True, stop=True).then_inc(S["logits"], 1)
                    for t in range(NT):
                        nc.tensor.transpose(ps[0:TT, 2 + t // 4, (t % 4) * D:(t % 4 + 1) * D],
                                            core.xn[:, t * TT:(t + 1) * TT],
                                            core.ident[:, :]).then_inc(S["turned"], 1)
                    pe.wait_ge(S["routed"], 1)
                    pe.wait_ge(S["tri_ready"], 2)
                    for a in range(2):
                        for lhs, rhs in ((tri[:, :], mask), (core.ones[0:TT, 0:TT], cum)):
                            mm = nc.tensor.matmul(ps[0:TT, a, :], lhs, rhs[:, 8 * a:8 * a + 8, :]
                                                  .rearrange("p t e -> p (t e)"),
                                                  start=(rhs is mask), stop=(rhs is cum))
                    mm.then_inc(S["counted"], 1)

                @block.scalar
                def _(act):
                    act.wait_ge(S["turned"], NT)
                    nc.scalar.activation(xnn[:, :, :].rearrange("p t n -> p (t n)"),
                                         ps[0:TT, 2:6, :].rearrange("p b n -> p (b n)"),
                                         ACT.Copy).then_inc(S["rows_copied"], 1)
                    act.wait_ge(S["exp_in"], 1)
                    for k in range(TOPK0):
                        nc.scalar.activation(gat[k][:, :], gat[k][:, :], ACT.Exp).then_inc(S["exp_out"], 1)

                @block.gpsimd
                def _(pool):
                    nc.gpsimd.memset(zero[:, :], 0.0).then_inc(S["zeroed"], 1)
                    nc.gpsimd.iota(imi[:, :], pattern=[[1, E0]], base=-E0,
                                   channel_multiplier=0).then_inc(S["iota"], 1)
                    nc.gpsimd.memset(tri[:, :], 1.0).then_inc(S["tri_ready"], 1)
                    pool.wait_ge(S["tri_ready"], 1)
                    nc.gpsimd.affine_select(out=tri[:, :], in_=tri[:, :], compare_op=ALU.is_gt, fill=0.0,
                                            base=0, pattern=[[1, TT]],
                                            channel_multiplier=-1).then_inc(S["tri_ready"], 1)
                    pool.wait_ge(S["rows_copied"], 1)
                    pool.wait_ge(S["put_ready"], 1)
                    pool.wait_ge(S["buf_zeroed"], 64)
                    for k in range(TOPK0):
                        for t in range(NT):
                            pool.indirect_dma_start(
                                out=buf, out_offset=bass.IndirectOffsetOnAxis(ap=put[k][:, t:t + 1], axis=0),
                                in_=xnn[:, t, :], in_offset=None, bounds_check=R - 1,
                                oob_is_err=False).then_inc(S["scattered"], 16)
                    pool.wait_ge(S["scattered"], 16 * TOPK0 * NT)

                @block.vector
                def _(dve):
                    link = core.linker(dve, "dve")
                    dve.wait_ge(S["iota"], 1)
                    link(nc.vector.tensor_copy(im[:, :, :], imi[:, :].unsqueeze(1).to_broadcast([TT, NT, E0])))
                    dve.wait_ge(S["logits"], NT)
                    link(nc.vector.tensor_tensor(V[:, :, :], ps[0:TT, 0:2, :].rearrange(
                        "p b (t e) -> p (b t) e", e=E0), gb[:, :].unsqueeze(1).to_broadcast([TT, NT, E0]),
                        ALU.add))
                    for k in range(TOPK0):
                        top_choice(link, nc, V[:, :, :], im[:, :, :], val[k][:, :], idx[k][:, :],
                                   hot[k][:, :, :], tmp[:, :, :], shp, k == TOPK0 - 1)
                    link(nc.vector.tensor_tensor(mask[:, :, :], hot[0][:, :, :], hot[1][:, :, :], ALU.add))
                    link(nc.vector.tensor_tensor(mask[:, :, :], mask[:, :, :], hot[2][:, :, :], ALU.add))
                    link(nc.vector.memset(cum[:, 0, :], 0.0))
                    for t in range(1, NT):
                        link(nc.vector.tensor_tensor(cum[:, t, :], cum[:, t - 1, :], mask[:, t - 1, :], ALU.add))
                    nc.vector.tensor_copy(tmp[:, 0, 0:1], cum[:, 0, 0:1]).then_inc(S["routed"], 1)
                    for k in range(TOPK0):
                        link(nc.vector.tensor_tensor(gat[k][:, :], val[k][:, :], val[0][:, :], ALU.subtract))
                    nc.vector.tensor_copy(tmp[:, 0, 1:2], cum[:, 0, 0:1]).then_inc(S["exp_in"], 1)
                    dve.wait_ge(S["exp_out"], TOPK0)
                    link(nc.vector.tensor_tensor(den[:, :], gat[0][:, :], gat[1][:, :], ALU.add))
                    link(nc.vector.tensor_tensor(den[:, :], den[:, :], gat[2][:, :], ALU.add))
                    link(nc.vector.reciprocal(den[:, :], den[:, :]))
                    dve.wait_ge(S["counted"], 1)
                    for k in range(TOPK0):
                        link(nc.vector.tensor_tensor(tmp[:, :, :], hot[k][:, :, :], ps[0:TT, 0:2, :].rearrange(
                            "p b (t e) -> p (b t) e", e=E0), ALU.mult))
                        link(nc.vector.tensor_reduce(slot[:, :], tmp[:, :, :], AX.X, ALU.add))
                        link(nc.vector.tensor_scalar(ok[:, :], slot[:, :], float(CAP), None, ALU.is_lt))
                        link(nc.vector.tensor_tensor(gat[k][:, :], gat[k][:, :], den[:, :], ALU.mult))
                        link(nc.vector.tensor_tensor(gat[k][:, :], gat[k][:, :], ok[:, :], ALU.mult))
                        link(nc.vector.tensor_scalar(rf[:, :], idx[k][:, :], float(E0), float(CAP), ALU.add,
                                                     ALU.mult))
                        link(nc.vector.tensor_tensor(rf[:, :], rf[:, :], slot[:, :], ALU.add))
                        link(nc.vector.tensor_tensor(rf[:, :], rf[:, :], ok[:, :], ALU.mult))
                        link(nc.vector.tensor_copy(row[k][:, :], rf[:, :]))
                        link(nc.vector.tensor_scalar(ok[:, :], ok[:, :], -float(R), float(R), ALU.mult, ALU.add))
                        link(nc.vector.tensor_tensor(rf[:, :], rf[:, :], ok[:, :], ALU.add))
                        link(nc.vector.tensor_copy(put[k][:, :], rf[:, :]))
                    nc.vector.tensor_copy(tmp[:, 0, 2:3], cum[:, 0, 0:1]).then_inc(S["put_ready"], 1)

        with ExitStack() as c2:
            xr = sb("xr", [2 * CAP, NS, D], c=c2)
            xb = sb("xb", [D, 2, 2 * CAP], c=c2)
            hb = sb("hb", [D, 2, 2 * C4, CAP], c=c2)
            hg = sb("hg", [D, 2, 2 * C4, CAP], c=c2)
            ys = sb("ys", [2 * CAP, 2, D], c=c2)
            names = [f"x_in{s}" for s in range(NS)] + ["y_out0", "y_out1",
                     "x_turned", "x_ready", "h_ready", "biased", "gelued", "y_ready", "y_copied"]
            S = {n: core.sig(f"moe_{n}").sem for n in names}
            NP = E0 // 2

            def load_rows(sp, e2, s):
                sp.dma_start(xr[:, s, :], buf[bass.ds(e2 * 2 * CAP, 2 * CAP), :]).then_inc(S[f"x_in{s}"], 16)

            with nc.Block() as block:
                @block.sync
                def _(sp):
                    for s in range(NS):
                        load_rows(sp, s, s)
                    with sp.Fori(0, NP // NS - 1) as i:
                        for s in range(NS):
                            sp.wait_ge(S["y_ready"], NS * i + s + 1)
                            load_rows(sp, NS * (i + 1) + s, s)
                            load_weights(sp, NS * (i + 1) + s, s)

                @block.tensor
                def _(pe):
                    with pe.Fori(0, NP // NS) as i:
                        def turn_and_lift(k):
                            pe.wait_ge(S[f"x_in{k}"], 16 * i + 16)
                            pe.wait_ge(S["x_ready"], NS * i + k + 1)
                            nc.tensor.transpose(ps[:, k % 2, 0:2 * CAP], xr[:, k, :],
                                                core.ident[:, :]).then_inc(S["x_turned"], 1)
                            pe.wait_ge(wt_in[k].sem, 48 * i + 48)
                            pe.wait_ge(S["x_ready"], NS * i + k + 3)
                            pe.wait_ge(S["biased"], NS * i + k + 1)
                            for e in range(2):
                                for c in range(C4):
                                    n = e * C4 + c
                                    mm = nc.tensor.matmul(ps[:, 2 + k % 2, n * CAP:(n + 1) * CAP],
                                                          w1[:, k, e, c:HID0:C4],
                                                          xb[:, k % 2, e * CAP:(e + 1) * CAP],
                                                          start=True, stop=True)
                            mm.then_inc(S["h_ready"], 1)

                        def lower(k):
                            pe.wait_ge(S["gelued"], NS * i + k + 1)
                            pe.wait_ge(S["y_copied"], NS * i + k + 1)
                            for e in range(2):
                                o = ps[e * CAP:(e + 1) * CAP, 4 + k % 2, 0:D]
                                nc.tensor.matmul(o, core.ones[0:1, 0:CAP], b2[:, k, e, :], start=True, stop=False)
                                for c in range(C4):
                                    mm = nc.tensor.matmul(o, hg[:, k % 2, e * C4 + c, :],
                                                          w2[:, k, e, c * D:(c + 1) * D],
                                                          start=False, stop=(c == C4 - 1))
                            mm.then_inc(S["y_ready"], 1)

                        turn_and_lift(0)
                        for k in range(NS):
                            if k + 1 < NS:
                                turn_and_lift(k + 1)
                            lower(k)

                @block.vector
                def _(dve):
                    dve.sem_inc(S["x_ready"], 2)
                    dve.sem_inc(S["biased"], 2)
                    with dve.Fori(0, NP // NS) as i:
                        for k in range(NS):
                            n = NS * i + k
                            dve.wait_ge(S["x_turned"], n + 1)
                            nc.vector.tensor_copy(xb[:, k % 2, :], ps[:, k % 2, 0:2 * CAP]
                                                  ).then_inc(S["x_ready"], 1)
                            dve.wait_ge(S["h_ready"], n + 1)
                            dve.wait_ge(S["y_copied"], n + 1)
                            nc.vector.tensor_tensor(
                                hb[:, k % 2, :, :], ps[:, 2 + k % 2, :].rearrange("p (n c) -> p n c", c=CAP),
                                b1[:, bass.ds(2 * n, 2), :].rearrange("p e c -> p (e c)").unsqueeze(2)
                                .to_broadcast([D, 2 * C4, CAP]), ALU.add).then_inc(S["biased"], 1)

                @block.scalar
                def _(act):
                    act.sem_inc(S["y_copied"], 2)
                    act.sem_inc(S["y_out0"], 16)
                    act.sem_inc(S["y_out1"], 16)
                    with act.Fori(0, NP // NS) as i:
                        for k in range(NS):
                            n = NS * i + k
                            act.wait_ge(S["biased"], n + 3)
                            nc.scalar.activation(hg[:, k % 2, :, :], hb[:, k % 2, :, :],
                                                 ACT.Gelu).then_inc(S["gelued"], 1)
                            act.wait_ge(S["y_ready"], n + 1)
                            act.wait_ge(S[f"y_out{k % 2}"], 32 * i + 16 * (k // 2) + 16)
                            nc.scalar.activation(ys[:, k % 2, :], ps[:, 4 + k % 2, 0:D],
                                                 ACT.Copy).then_inc(S["y_copied"], 1)
                            act.wait_ge(S["y_copied"], n + 3)
                            act.dma_start(ydr[bass.ds(n * 2 * CAP, 2 * CAP), :], ys[:, k % 2, :]
                                          ).then_inc(S[f"y_out{k % 2}"], 16)
                    act.wait_ge(S["y_out0"], 16 * NP // 2 + 16)
                    act.wait_ge(S["y_out1"], 16 * NP // 2 + 16)

        with ExitStack() as c3:
            yr = [sb(f"yr{k}", [TT, NT, D], c=c3) for k in range(TOPK0)]
            S = {n: core.sig(f"moe_{n}").sem for n in ("gathered0", "gathered1", "gathered2", "mixed",
                                                        "mix_turned")}
            with nc.Block() as block:
                @block.gpsimd
                def _(pool):
                    for k in range(TOPK0):
                        for t in range(NT):
                            pool.indirect_dma_start(
                                out=yr[k][:, t, :], out_offset=None, in_=ydr,
                                in_offset=bass.IndirectOffsetOnAxis(ap=row[k][:, t:t + 1], axis=0),
                                bounds_check=R - 1, oob_is_err=False).then_inc(S[f"gathered{k}"], 16)

                @block.vector
                def _(dve):
                    link = core.linker(dve, "dve")
                    for k in range(TOPK0):
                        dve.wait_ge(S[f"gathered{k}"], 16 * NT)
                        link(nc.vector.tensor_tensor(yr[k][:, :, :], yr[k][:, :, :], gat[k][:, :].unsqueeze(2)
                                                     .to_broadcast([TT, NT, D]), ALU.mult))
                        if k:
                            link(nc.vector.tensor_tensor(yr[0][:, :, :], yr[0][:, :, :], yr[k][:, :, :], ALU.add))
                    nc.vector.tensor_copy(yr[1][:, 0, 0:1], yr[0][:, 0, 0:1]).then_inc(S["mixed"], 1)
                    for g in range(4):
                        dve.wait_ge(S["mix_turned"], g + 1)
                        s = slice(g * CH, (g + 1) * CH)
                        link(nc.vector.scalar_tensor_tensor(
                            out=core.xT[:, s], in0=ps[:, g, 0:CH], scalar=core.tg[:, gate:gate + 1],
                            in1=core.xT[:, s], op0=ALU.mult, op1=ALU.add))

                @block.tensor
                def _(pe):
                    pe.wait_ge(S["mixed"], 1)
                    for t in range(NT):
                        mm = nc.tensor.transpose(ps[:, t // 4, (t % 4) * TT:(t % 4 + 1) * TT], yr[0][:, t, :],
                                                 core.ident[0:TT, 0:TT])
                        if t % 4 == 3:
                            mm.then_inc(S["mix_turned"], 1)


def gated_experts(core, L, n_exp, n_chunk, eps, gate):
    nc, d, ps = core.nc, core.d, core.ps
    EA = n_exp + 1
    with ExitStack() as ctx:
        def sb(n, shape, dt=F32):
            return core.sb(f"{L}f_{n}", shape, dt, ctx)
        wr = sb("wr", [D, n_exp])
        wg, wu, wd = (sb(n, [128, n_chunk, 128]) for n in ("wg", "wu", "wd"))
        ex = sb("ex", [EA, n_chunk, 128])
        V, im, tmp, hot0, hot1 = (sb(n, [TT, NT, n_exp]) for n in ("V", "im", "tmp", "hot0", "hot1"))
        imi = sb("imi", [TT, n_exp], I32)
        comb = sb("comb", [TT, NT, EA])
        combT = sb("combT", [EA, T])
        mx, ix, p0, p1, den = (sb(n, [TT, NT]) for n in ("mx", "ix", "p0", "p1", "den"))
        sg, t1, hh = (sb(n, [128, 2, CH]) for n in ("sg", "t1", "hh"))
        names = ["w_in", "iota", "logits", "shifted", "exped", "combined", "comb_turned", "combT_ready",
                 "lifted", "silued", "gated", "hidden", "lowered", "added"]
        S = {n: core.sig(f"{L}f_{n}").sem for n in names}
        shp = (TT, NT, n_exp)

        def bc(ap):
            return ap.unsqueeze(2).to_broadcast([TT, NT, n_exp])

        with nc.Block() as block:
            @block.sync
            def _(sp):
                for dst, n in ((wr[:, :], "wr"), (ex[:, :, :], "ex"), (wg[:, :, :], "wg"),
                               (wu[:, :, :], "wu"), (wd[:, :, :], "wd")):
                    sp.dma_start(dst, d[f"{L}_{n}"]).then_inc(S["w_in"], 16)
                sp.wait_ge(S["w_in"], 80)

            @block.gpsimd
            def _(pool):
                nc.gpsimd.iota(imi[:, :], pattern=[[1, n_exp]], base=-n_exp,
                               channel_multiplier=0).then_inc(S["iota"], 1)

            @block.tensor
            def _(pe):
                pe.wait_ge(S["w_in"], 80)
                for t in range(NT):
                    mm = nc.tensor.matmul(ps[0:TT, 0, t * n_exp:(t + 1) * n_exp],
                                          core.xn[:, t * TT:(t + 1) * TT], wr[:, :], start=True, stop=True)
                mm.then_inc(S["logits"], 1)
                pe.wait_ge(S["combined"], 1)
                for t in range(NT):
                    mm = nc.tensor.transpose(ps[0:EA, 1 + t // 4, (t % 4) * TT:(t % 4 + 1) * TT],
                                             comb[:, t, :], core.ident[0:TT, 0:TT])
                mm.then_inc(S["comb_turned"], 1)

            @block.scalar
            def _(act):
                act.wait_ge(S["shifted"], 1)
                nc.scalar.activation(V[:, :, :], V[:, :, :], ACT.Exp).then_inc(S["exped"], 1)

            @block.vector
            def _(dve):
                link = core.linker(dve, "dve")
                dve.wait_ge(S["iota"], 1)
                link(nc.vector.tensor_copy(im[:, :, :], imi[:, :].unsqueeze(1).to_broadcast([TT, NT, n_exp])))
                dve.wait_ge(S["logits"], 1)
                lg = ps[0:TT, 0, 0:NT * n_exp].rearrange("p (t e) -> p t e", e=n_exp)
                link(nc.vector.tensor_reduce(mx[:, :], lg, AX.X, ALU.max))
                nc.vector.tensor_tensor(V[:, :, :], lg, bc(mx[:, :]), ALU.subtract).then_inc(S["shifted"], 1)
                dve.wait_ge(S["exped"], 1)
                link(nc.vector.tensor_reduce(den[:, :], V[:, :, :], AX.X, ALU.add))
                link(nc.vector.reciprocal(den[:, :], den[:, :]))
                link(nc.vector.tensor_tensor(V[:, :, :], V[:, :, :], bc(den[:, :]), ALU.mult))
                top_choice(link, nc, V[:, :, :], im[:, :, :], p0[:, :], ix[:, :], hot0[:, :, :],
                           tmp[:, :, :], shp, False)
                top_choice(link, nc, V[:, :, :], im[:, :, :], p1[:, :], ix[:, :], hot1[:, :, :],
                           tmp[:, :, :], shp, True)
                link(nc.vector.tensor_tensor(den[:, :], p0[:, :], p1[:, :], ALU.add))
                link(nc.vector.tensor_scalar(den[:, :], den[:, :], eps, None, ALU.add))
                link(nc.vector.reciprocal(den[:, :], den[:, :]))
                for p, hot in ((p0, hot0), (p1, hot1)):
                    link(nc.vector.tensor_tensor(p[:, :], p[:, :], den[:, :], ALU.mult))
                    link(nc.vector.tensor_tensor(hot[:, :, :], hot[:, :, :], bc(p[:, :]), ALU.mult))
                link(nc.vector.memset(comb[:, :, :], 1.0))
                nc.vector.tensor_tensor(comb[:, :, 0:n_exp], hot0[:, :, :], hot1[:, :, :],
                                        ALU.add).then_inc(S["combined"], 1)
                dve.wait_ge(S["comb_turned"], 1)
                nc.vector.tensor_copy(combT[:, :].rearrange("p (b n) -> p b n", b=4),
                                      ps[0:EA, 1:5, 0:CH]).then_inc(S["combT_ready"], 1)

        feed_forward(core, S, n_chunk, (wg, wu, wd), (sg, t1, hh), gate, ex=ex, combT=combT)


def feed_forward(core, S, n_chunk, weights, bufs, gate, ex=None, combT=None, b1=None, b2=None):
    nc, ps = core.nc, core.ps
    wg, wu, wd = weights
    sg, t1, hh = bufs
    with nc.Block() as block:
        def n_of(i, c):
            return n_chunk * i + c

        def free(i, c):
            odd = n_chunk % 2 == 1 and c == 0
            return n_of(i, c) + (2 if odd else 1)

        @block.tensor
        def _(pe):
            def lift(i, c):
                s = c % 2
                x = core.xn[:, bass.ds(i * CH, CH)]
                pe.wait_ge(S["hidden"], free(i, c))
                mm = nc.tensor.matmul(ps[:, 3 * s, 0:CH], wg[:, c, :], x, start=True, stop=True)
                if wu is not None:
                    nc.tensor.matmul(ps[:, 3 * s + 1, 0:CH], wu[:, c, :], x, start=True, stop=True)
                    mm = nc.tensor.matmul(ps[:, 3 * s + 2, 0:CH], ex[:, c, :], combT[:, bass.ds(i * CH, CH)],
                                          start=True, stop=True)
                mm.then_inc(S["lifted"], 1)

            with pe.Fori(0, NCH) as i:
                lift(i, 0)
                pe.wait_ge(S["added"], i + 1)
                for c in range(n_chunk):
                    if c + 1 < n_chunk:
                        lift(i, c + 1)
                    pe.wait_ge(S["hidden"], n_of(i, c) + 3)
                    mm = nc.tensor.matmul(ps[:, 6, 0:CH], wd[:, c, :], hh[:, c % 2, :], start=(c == 0),
                                          stop=(c == n_chunk - 1))
                    mm.then_inc(S["lowered"], 1)

        @block.scalar
        def _(act):
            if wu is None:
                act.sem_inc(S["hidden"], 2)
            with act.Fori(0, NCH) as i:
                for c in range(n_chunk):
                    s = c % 2
                    act.wait_ge(S["lifted"], n_of(i, c) + 1)
                    if wu is None:
                        act.wait_ge(S["lowered"], free(i, c))
                        nc.scalar.activation(hh[:, s, :], ps[:, 3 * s, 0:CH], ACT.Gelu,
                                             bias=b1[c]).then_inc(S["hidden"], 1)
                    else:
                        act.wait_ge(S["hidden"], free(i, c))
                        nc.scalar.activation(sg[:, s, :], ps[:, 3 * s, 0:CH], ACT.Silu).then_inc(S["silued"], 1)

        @block.vector
        def _(dve):
            dve.sem_inc(S["lowered"], 2)
            dve.sem_inc(S["added"], 1)
            if wu is not None:
                dve.sem_inc(S["hidden"], 2)
            with dve.Fori(0, NCH) as i:
                for c in range(n_chunk):
                    s = c % 2
                    if wu is None:
                        continue
                    dve.wait_ge(S["silued"], n_of(i, c) + 1)
                    nc.vector.tensor_tensor(t1[:, s, :], ps[:, 3 * s + 1, 0:CH], sg[:, s, :],
                                            ALU.mult).then_inc(S["gated"], 1)
                    dve.wait_ge(S["gated"], n_of(i, c) + 1)
                    dve.wait_ge(S["lowered"], free(i, c))
                    nc.vector.tensor_tensor(hh[:, s, :], ps[:, 3 * s + 2, 0:CH], t1[:, s, :],
                                            ALU.mult).then_inc(S["hidden"], 1)
                dve.wait_ge(S["lowered"], n_chunk * i + n_chunk + 2)
                x = core.xT[:, bass.ds(i * CH, CH)]
                o = core.OT[:, bass.ds(i * CH, CH)]
                if b2 is not None:
                    nc.vector.tensor_scalar(o, ps[:, 6, 0:CH], b2, None, ALU.add).then_inc(S["biased2"], 1)
                    dve.wait_ge(S["biased2"], i + 1)
                nc.vector.scalar_tensor_tensor(out=x, in0=ps[:, 6, 0:CH] if b2 is None else o,
                                               scalar=core.tg[:, gate:gate + 1], in1=x,
                                               op0=ALU.mult, op1=ALU.add).then_inc(S["added"], 1)


def binarized_mlp(core, gate):
    nc, d, ps = core.nc, core.d, core.ps
    with ExitStack() as ctx:
        def sb(n, shape):
            return core.sb(f"bin_{n}", shape, F32, ctx)
        w = sb("w", [128, 8, 128])
        sgn = sb("sgn", [128, 8, 128])
        al, al2 = sb("al", [128, 8]), sb("al2", [128, 1])
        wT = sb("wT", [128, 8, 128])
        hh = sb("hh", [128, 2, CH])
        S = {n: core.sig(f"bin_{n}").sem for n in ("w_in", "signed", "binarized", "turned", "lifted",
                                                    "hidden", "lowered", "added", "biased2")}
        with nc.Block() as block:
            @block.sync
            def _(sp):
                sp.dma_start(w[:, 0:4, :], d["L3_w1"]).then_inc(S["w_in"], 16)
                sp.dma_start(w[:, 4:8, :], d["L3_w2"]).then_inc(S["w_in"], 16)

            @block.scalar
            def _(act):
                act.wait_ge(S["w_in"], 32)
                nc.scalar.activation(sgn[:, :, :], w[:, :, :], ACT.Sign).then_inc(S["signed"], 1)

            @block.vector
            def _(dve):
                link = core.linker(dve, "dve")
                dve.wait_ge(S["w_in"], 32)
                link(nc.vector.tensor_reduce(al[:, :], w[:, :, :], AX.X, ALU.add, apply_absolute_value=True))
                link(nc.vector.tensor_reduce(al2[:, :], al[:, 4:8], AX.X, ALU.add))
                link(nc.vector.tensor_scalar(al[:, 0:4], al[:, 0:4], 1.0 / D, None, ALU.mult))
                link(nc.vector.tensor_scalar(al2[:, :], al2[:, :], 1.0 / 512, None, ALU.mult))
                dve.wait_ge(S["signed"], 1)
                link(nc.vector.tensor_tensor(sgn[:, 0:4, :], sgn[:, 0:4, :],
                                             al[:, 0:4].unsqueeze(2).to_broadcast([128, 4, 128]), ALU.mult))
                link(nc.vector.tensor_scalar(sgn[:, 4:8, :], sgn[:, 4:8, :], al2[:, 0:1], None, ALU.mult))
                link(nc.vector.tensor_tensor(sgn[:, :, :], sgn[:, :, :], w[:, :, :], ALU.subtract))
                nc.vector.tensor_tensor(w[:, :, :], w[:, :, :], sgn[:, :, :], ALU.add
                                        ).then_inc(S["binarized"], 1)
                dve.wait_ge(S["turned"], 1)
                link(nc.vector.tensor_copy(wT[:, :, :].rearrange("p (a c) n -> p a (c n)", a=2), ps[:, 0:2, :]))

            @block.tensor
            def _(pe):
                pe.wait_ge(S["binarized"], 1)
                for n in range(8):
                    mm = nc.tensor.transpose(ps[:, n // 4, (n % 4) * 128:(n % 4 + 1) * 128], w[:, n, :],
                                             core.ident[:, :])
                mm.then_inc(S["turned"], 1)
        feed_forward(core, S, 4, (wT[:, 0:4, :], None, wT[:, 4:8, :]), (None, None, hh), gate,
                     b1=[v(core, f"ffb1_{c}") for c in range(4)], b2=v(core, "L3_b2"))


BITS = {"d2v": (DC, 1, 128), "img": (128, 1, 128), "txt": (128, 1, 128), "att0": (128, 1, 128),
        "att1": (128, 1, 128), "f1": (128, 2, 512), "f2": (128, 4, 128)}
BIT_COUNT = {"d2v": DC * 128, "img": 128 * 128, "txt": 128 * 128, "att0": 128 * 64, "att1": 128 * 64,
             "f1": 256 * 512, "f2": 512 * 128}
QMAX = 127.0


class Bit:

    def __init__(self, core, ctx):
        self.core, self.ctx = core, ctx
        self.q = {n: core.sb(f"bit_{n}", [p, k, o], BF16, ctx) for n, (p, k, o) in BITS.items()}
        self.ws = core.sb("bit_ws", [128, len(BITS)], F32, ctx)
        self.isc = core.sb("bit_isc", [128, 6], F32, ctx)
        self.inv = core.sb("bit_inv", [128, 6], F32, ctx)
        self.out = core.sb("bit_out", [128, len(BITS)], F32, ctx)
        self.magic = core.sb("bit_magic", [128, 1], F32, ctx)
        self.small = core.sb("bit_small", [128, 2], F32, ctx)
        self.turned, self.one, self.spread = (core.sig(f"bit_{n}") for n in ("turned", "one", "spread"))

    def weight(self, n):
        return list(BITS).index(n)


def quantize_weights(core, bit):
    nc, d, ps = core.nc, core.d, core.ps
    with ExitStack() as ctx:
        w = {n: core.sb(f"bitw_{n}", [p, k, o], F32, ctx) for n, (p, k, o) in BITS.items()}
        tot = core.sb("bitw_tot", [128, len(BITS)], F32, ctx)
        thr = core.sb("bitw_thr", [128, 2 * len(BITS)], F32, ctx)
        hi = core.sb("bitw_hi", [128, 1024], F32, ctx)
        lo = core.sb("bitw_lo", [128, 1024], F32, ctx)
        w_in, summed, spread = (core.sig(f"bitw_{n}") for n in ("in", "summed", "spread"))
        with nc.Block() as block:
            @block.sync
            def _(sp):
                for n in BITS:
                    sp.dma_start(w[n][:, :, :], d[f"bit_{n}"]).then_inc(w_in.sem, 16)

            @block.tensor
            def _(pe):
                pe.wait_ge(summed.sem, 1)
                nc.tensor.matmul(ps[:, 0, 0:len(BITS)], core.ones[:, :], tot[:, :], start=True,
                                 stop=True).then_inc(spread.sem, 1)

            @block.vector
            def _(dve):
                link = core.linker(dve, "dve")
                dve.wait_ge(w_in.sem, 16 * len(BITS))
                link(nc.vector.memset(tot[:, :], 0.0))
                link(nc.vector.memset(bit.magic[:, :], -MAGIC))
                for i, (n, (p, k, o)) in enumerate(BITS.items()):
                    o = 64 if n.startswith("att") else o
                    link(nc.vector.tensor_reduce(tot[0:p, i:i + 1], w[n][:, :, 0:o], AX.XY, ALU.add,
                                                 apply_absolute_value=True))
                nc.vector.tensor_copy(hi[:, 0:1], tot[:, 0:1]).then_inc(summed.sem, 1)
                dve.wait_ge(spread.sem, 1)
                for i, (n, (p, k, o)) in enumerate(BITS.items()):
                    link(nc.vector.tensor_scalar(bit.ws[:, i:i + 1], ps[:, 0, i:i + 1], 1.0 / BIT_COUNT[n],
                                                 1e-5, ALU.mult, ALU.max))
                    link(nc.vector.tensor_scalar(thr[:, i:i + 1], bit.ws[:, i:i + 1], 0.5, None, ALU.mult))
                    j = len(BITS) + i
                    link(nc.vector.tensor_scalar(thr[:, j:j + 1], bit.ws[:, i:i + 1], -0.5, None, ALU.mult))
                    h, l_ = hi[0:p, 0:k * o], lo[0:p, 0:k * o]
                    flat = w[n][:, :, :].rearrange("p k o -> p (k o)")
                    link(nc.vector.tensor_scalar(h, flat, thr[0:p, i:i + 1], None, ALU.is_gt))
                    link(nc.vector.tensor_scalar(l_, flat, thr[0:p, j:j + 1], None, ALU.is_lt))
                    link(nc.vector.tensor_tensor(bit.q[n][:, :, :].rearrange("p k o -> p (k o)"), h, l_,
                                                 ALU.subtract))


def input_scale(core, bit, col, p, k, weights):
    nc, ps = core.nc, core.ps
    with nc.Block() as block:
        @block.tensor
        def _(pe):
            nc.tensor.transpose(ps[0:1, 0, 0:p], col, core.ident[0:p, 0:p]).then_inc(bit.turned.sem, 1)
            pe.wait_ge(bit.one.sem, bit.one.at(1))
            nc.tensor.matmul(ps[:, 1, 0:1], core.ones[0:1, :], bit.small[0:1, 0:1], start=True,
                             stop=True).then_inc(bit.spread.sem, 1)

        @block.vector
        def _(dve):
            link = core.linker(dve, "dve")
            dve.wait_ge(bit.turned.sem, bit.turned.at(1))
            nc.vector.tensor_reduce(bit.small[0:1, 0:1], ps[0:1, 0, 0:p], AX.X,
                                    ALU.max).then_inc(bit.one.sem, 1)
            dve.wait_ge(bit.spread.sem, bit.spread.at(1))
            link(nc.vector.tensor_scalar(bit.isc[:, k:k + 1], ps[:, 1, 0:1], 1e-8, 1.0 / QMAX, ALU.max,
                                         ALU.mult))
            link(nc.vector.reciprocal(bit.inv[:, k:k + 1], bit.isc[:, k:k + 1]))
            for n in weights:
                i = bit.weight(n)
                link(nc.vector.tensor_tensor(bit.out[:, i:i + 1], bit.ws[:, i:i + 1], bit.isc[:, k:k + 1],
                                             ALU.mult))
    for s in (bit.turned, bit.one, bit.spread):
        s.base += 1


def image_pass(core, bit, V, n_in, k, w_in, w_out, amax, isum, last=False):
    nc, d, ps = core.nc, core.d, core.ps
    tag = f"img{k}"
    first = n_in == DC
    with ExitStack() as ctx:
        Y = [core.sb(f"{tag}_y{s}", [n_in, NK], F32, ctx) for s in range(2)]
        R = core.sb(f"{tag}_r", [n_in, NK], F32, ctx)
        Q = [core.sb(f"{tag}_q{s}", [n_in, NK], BF16, ctx) for s in range(2)]
        A = [core.sb(f"{tag}_a{s}", [128, NK], F32, ctx) for s in range(2)]
        mx = core.sb(f"{tag}_mx", [128, B], F32, ctx)
        S = {n: core.sig(f"{tag}_{n}").sem for n in ("y_in0", "y_in1", "valued", "scaled", "rounded",
                                                      "lifted", "kept", "absed", "maxed")}
        inv = bit.inv[0:n_in, k:k + 1]

        with nc.Block() as block:
            if first:
                @block.sync
                def _(sp):
                    def load(b, s):
                        sp.dma_start(Y[s][:, :], d["ctxT"][bass.ds(b, 1), 0:DC, :]
                                     .rearrange("o p n -> (o p) n")).then_inc(S[f"y_in{s}"], 16)
                    for s in range(2):
                        load(s, s)
                    with sp.Fori(0, B // 2 - 1) as i:
                        for s in range(2):
                            sp.wait_ge(S["scaled"], 2 * i + s + 3)
                            load(2 * (i + 1) + s, s)

            @block.scalar
            def _(act):
                if not last:
                    act.sem_inc(S["kept"], 2)
                with act.Fori(0, B // 2) as i:
                    for s in range(2):
                        n = 2 * i + s
                        if not first:
                            act.wait_ge(S["scaled"], n + 1)
                            j = bit.weight(w_in)
                            nc.scalar.activation(Y[s][:, :], V[:, bass.ds(n * NK, NK)], ACT.Identity,
                                                 scale=bit.out[:, j:j + 1],
                                                 bias=v(core, w_in)).then_inc(S["valued"], 1)
                    for s in range(2):
                        n = 2 * i + s
                        if not last:
                            act.wait_ge(S["lifted"], n + 3)
                            o = ps[:, 4 * s:4 * s + 3, 0:500]
                            act.wait_ge(S["maxed"], n + 1)
                            j = bit.weight(w_out)
                            nc.scalar.activation(A[s][:, :].rearrange("p (a m) -> p a m", a=3), o, ACT.Abs,
                                                 scale=bit.out[:, j:j + 1], bias=v(core, w_out)
                                                 ).then_inc(S["absed"], 1)
                            sums = {} if isum is None else {"accum_out": isum[:, bass.ds(n, 1)]}
                            nc.scalar.activation(V[:, bass.ds(n * NK, NK)].rearrange("p (a m) -> p a m", a=3),
                                                 o, ACT.Copy, **sums).then_inc(S["kept"], 1)

            @block.vector
            def _(dve):
                link = core.linker(dve, "dve")
                dve.sem_inc(S["scaled"], 2)
                dve.sem_inc(S["rounded"], 2)
                dve.sem_inc(S["maxed"], 2)
                with dve.Fori(0, B // 2) as i:
                    for s in range(2):
                        n = 2 * i + s
                        if first:
                            dve.wait_ge(S[f"y_in{s}"], 16 * i + 16)
                        else:
                            dve.wait_ge(S["valued"], n + 1)
                        dve.wait_ge(S["rounded"], n + 2)
                        nc.vector.tensor_scalar(R[:, :], Y[s][:, :], inv, MAGIC, ALU.mult,
                                                ALU.add).then_inc(S["scaled"], 1)
                        dve.wait_ge(S["scaled"], n + 3)
                        if last:
                            q = V[:, bass.ds(n * NK, NK)].bitcast(BF16)
                        else:
                            dve.wait_ge(S["lifted"], n + 1)
                            q = Q[s][:, :]
                        nc.vector.tensor_scalar(q, R[:, :], -MAGIC, None, ALU.add
                                                ).then_inc(S["rounded"], 1)
                    if not last:
                        for s in range(2):
                            n = 2 * i + s
                            dve.wait_ge(S["absed"], n + 1)
                            nc.vector.tensor_reduce(mx[:, bass.ds(n, 1)], A[s][:, :], AX.X,
                                                    ALU.max).then_inc(S["maxed"], 1)
                if not last:
                    dve.wait_ge(S["maxed"], B + 2)
                    link(nc.vector.tensor_reduce(amax[:, :], mx[:, :], AX.X, ALU.max))

            if not last:
                @block.tensor
                def _(pe):
                    pe.sem_inc(S["lifted"], 2)
                    with pe.Fori(0, B // 2) as i:
                        for s in range(2):
                            n = 2 * i + s
                            pe.wait_ge(S["rounded"], n + 3)
                            pe.wait_ge(S["kept"], n + 1)
                            for a in range(3):
                                mm = nc.tensor.matmul(ps[:, 4 * s + a, 0:500], bit.q[w_out][:, 0, :],
                                                      Q[s][:, a * 500:(a + 1) * 500], start=True, stop=True)
                            mm.then_inc(S["lifted"], 1)


def bit_attend(core, bit, V, FU, which):
    nc, d, ps = core.nc, core.d, core.ps
    tag = f"bat{which}"
    w = bit.weight(which)
    W = bit.q[which][:, 0, :]
    sc = bit.out[:, w:w + 1]
    NPB = B // 2
    with ExitStack() as ctx:
        FB = core.sb(f"{tag}_fb", [D, 128], F32, ctx)
        KTs = core.sb(f"{tag}_kt", [D, 2, NK], F32, ctx)
        KV = [core.sb(f"{tag}_kv{p}", [KP, 2, KT, D], F32, ctx) for p in range(2)]
        brow = core.sb(f"{tag}_brow", [KP, D], F32, ctx)
        P = core.sb(f"{tag}_p", [128, NK], F32, ctx)
        PT = core.sb(f"{tag}_pt", [KP, KT, 128], F32, ctx)
        OS = core.sb(f"{tag}_os", [128, D], F32, ctx)
        sm = core.sb(f"{tag}_sm", [128, 4], F32, ctx)
        S = {n: core.sig(f"{tag}_{n}").sem for n in
             ("row_in", "fb_ready", "k_made", "kv_made", "kt_copied", "kv_copied", "scored", "max_taken",
              "maxed", "exped", "inverted", "turned", "pt_copied", "weighed", "o_scaled", "o_turned",
              "fused")}

        def all_pairs(eng, body):
            with eng.Fori(0, NPB // 2 - 1) as i2:
                for p in range(2):
                    body(2 * i2 + p, p, True)
            for p in range(2):
                body(NPB - 2 + p, p, p == 0)

        with nc.Block() as block:
            @block.sync
            def _(sp):
                sp.dma_start(brow[:, :], d[f"bit_row_{which}"]).then_inc(S["row_in"], 16)
                sp.wait_ge(S["row_in"], 16)

            @block.gpsimd
            def _(pool):
                nc.gpsimd.memset(FB[:, :], 0.0).then_inc(S["fb_ready"], 1)
                pool.wait_ge(S["fb_ready"], 1)
                with pool.Fori(0, NPB) as i:
                    pool.wait_ge(S["scored"], i + 1)
                    for s in range(2):
                        nc.gpsimd.tensor_copy(FB[:, 64 * s:64 * s + NQ], FU[:, bass.ds((2 * i + s) * NQ, NQ)]
                                              ).then_inc(S["fb_ready"], 1)

            @block.tensor
            def _(pe):
                def keys(i, s):
                    pe.wait_ge(S["kv_copied"], 2 * i + s + 1)
                    for a in range(3):
                        mm = nc.tensor.matmul(ps[:, 3 + a, 0:500], W,
                                              V[:, bass.ds((2 * i + s) * NK + a * 500, 500)],
                                              start=True, stop=True)
                    mm.then_inc(S["k_made"], 1)

                def keys_by_row(i, s):
                    pe.wait_ge(S["kt_copied"], 2 * i + s + 1)
                    for t in range(KT):
                        mm = nc.tensor.matmul(ps[0:KP, 3 + t // 4, (t % 4) * D:(t % 4 + 1) * D],
                                              V[:, bass.ds((2 * i + s) * NK + t * KP, KP)], W,
                                              start=True, stop=True)
                    mm.then_inc(S["kv_made"], 1)

                def turn(i, g):
                    for t in range(4 * g, 4 * g + 4):
                        mm = nc.tensor.transpose(ps[0:KP, 6 + g % 2, (t % 4) * 128:(t % 4 + 1) * 128],
                                                 P[:, t * KP:(t + 1) * KP], core.ident[:, :])
                    mm.then_inc(S["turned"], 1)

                def body(i, p, nxt):
                    pe.wait_ge(S["kt_copied"], 2 * i + 2)
                    pe.wait_ge(S["fb_ready"], 2 * i + 3)
                    pe.wait_ge(S["exped"], i + 1)
                    for a in range(3):
                        for s in range(2):
                            mm = nc.tensor.matmul(ps[64 * s:64 * s + 64, a, 0:500], FB[:, 64 * s:64 * s + 64],
                                                  KTs[:, s, a * 500:(a + 1) * 500], start=True, stop=True)
                    mm.then_inc(S["scored"], 1)
                    if nxt:
                        keys(i + 1, 0)
                        keys_by_row(i + 1, 0)
                    pe.wait_ge(S["exped"], i + 2)
                    pe.wait_ge(S["fused"], i + 1)
                    turn(i, 0)
                    turn(i, 1)
                    if nxt:
                        keys(i + 1, 1)
                    pe.wait_ge(S["pt_copied"], 3 * i + 1)
                    turn(i, 2)
                    pe.wait_ge(S["pt_copied"], 3 * i + 3)
                    pe.wait_ge(S["kv_copied"], 2 * i + 3)
                    for t in range(KT):
                        for s in range(2):
                            mm = nc.tensor.matmul(ps[64 * s:64 * s + 64, 7, 0:D],
                                                  PT[:, t, 64 * s:64 * s + 64], KV[p][:, s, t, :],
                                                  start=(t == 0), stop=(t == KT - 1))
                    mm.then_inc(S["weighed"], 1)
                    if nxt:
                        keys_by_row(i + 1, 1)
                    pe.wait_ge(S["o_scaled"], i + 1)
                    nc.tensor.transpose(ps[:, 6, 0:128], OS[:, :], core.ident[:, :]).then_inc(S["o_turned"], 1)

                for s in range(2):
                    keys(0, s)
                    keys_by_row(0, s)
                all_pairs(pe, body)

            @block.scalar
            def _(act):
                act.sem_inc(S["exped"], 1)

                def copy_keys(i, s):
                    act.wait_ge(S["k_made"], 2 * i + s + 1)
                    nc.scalar.activation(KTs[:, s, :].rearrange("p (a m) -> p a m", a=3),
                                         ps[:, 3:6, 0:500], ACT.Identity, scale=sc,
                                         bias=v(core, which)).then_inc(S["kt_copied"], 1)

                def body(i, p, nxt):
                    if nxt:
                        copy_keys(i + 1, 0)
                    act.wait_ge(S["maxed"], i + 1)
                    nc.scalar.activation(P[:, :].rearrange("p (a m) -> p a m", a=3), ps[:, 0:3, 0:500],
                                         ACT.Exp, bias=sm[:, 0:1], scale=float(D) ** -0.5,
                                         accum_out=sm[:, 1:2]).then_inc(S["exped"], 1)
                    if nxt:
                        copy_keys(i + 1, 1)

                for s in range(2):
                    copy_keys(0, s)
                all_pairs(act, body)

            @block.vector
            def _(dve):
                dve.sem_inc(S["kv_copied"], 1)
                dve.sem_inc(S["scored"], 1)
                dve.sem_inc(S["fused"], 1)
                dve.wait_ge(S["row_in"], 16)

                def copy_keys_by_row(i, p, s):
                    dve.wait_ge(S["kv_made"], 2 * i + s + 1)
                    nc.vector.scalar_tensor_tensor(
                        out=KV[p][:, s, :, :], in0=ps[0:KP, 3:6, :].rearrange("p b (t n) -> p (b t) n", n=D),
                        scalar=sc[0:KP, :], in1=brow[:, :].unsqueeze(1).to_broadcast([KP, KT, D]),
                        op0=ALU.mult, op1=ALU.add).then_inc(S["kv_copied"], 1)

                def body(i, p, nxt):
                    dve.wait_ge(S["scored"], i + 2)
                    nc.vector.tensor_reduce(sm[:, 2:3], ps[:, 0:3, 0:500], AX.XY, ALU.max
                                            ).then_inc(S["max_taken"], 1)
                    dve.wait_ge(S["max_taken"], i + 1)
                    nc.vector.tensor_scalar(sm[:, 0:1], sm[:, 2:3], -float(D) ** -0.5, None,
                                            ALU.mult).then_inc(S["maxed"], 1)
                    if nxt:
                        copy_keys_by_row(i + 1, 1 - p, 0)
                    dve.wait_ge(S["exped"], i + 2)
                    nc.vector.reciprocal(sm[:, 3:4], sm[:, 1:2]).then_inc(S["inverted"], 1)
                    for g in range(3):
                        dve.wait_ge(S["turned"], 3 * i + g + 1)
                        nc.vector.tensor_copy(PT[:, 4 * g:4 * g + 4, :].rearrange("p t n -> p (t n)"),
                                              ps[0:KP, 6 + g % 2, :]).then_inc(S["pt_copied"], 1)
                    dve.wait_ge(S["inverted"], i + 1)
                    dve.wait_ge(S["weighed"], i + 1)
                    nc.vector.tensor_scalar(OS[:, :], ps[:, 7, 0:D], sm[:, 3:4], None, ALU.mult
                                            ).then_inc(S["o_scaled"], 1)
                    if nxt:
                        copy_keys_by_row(i + 1, 1 - p, 1)
                    dve.wait_ge(S["o_turned"], i + 1)
                    f = FU[:, bass.ds(2 * i * NQ, 2 * NQ)].rearrange("p (s q) -> p s q", s=2)
                    nc.vector.scalar_tensor_tensor(
                        out=f, in0=ps[:, 6, 0:128].rearrange("p (s q) -> p s q", s=2)[:, :, 0:NQ],
                        scalar=0.1, in1=f, op0=ALU.mult, op1=ALU.add).then_inc(S["fused"], 1)

                for s in range(2):
                    copy_keys_by_row(0, 0, s)
                all_pairs(dve, body)


def quantized(core, bit, link, dst, src, k, tmp, p=128):
    nc = core.nc
    link(nc.vector.tensor_scalar(tmp, src, bit.inv[0:p, k:k + 1], MAGIC, ALU.mult, ALU.add))
    link(nc.vector.tensor_scalar(dst, tmp, -MAGIC, None, ALU.add))


def bit_linear(core, bit, name, q, dst, relu, tag):
    nc, ps = core.nc, core.ps
    p, kt, outs = BITS[name]
    j = bit.weight(name)
    S = {n: core.sig(f"{tag}_{n}").sem for n in ("made", "copied")}
    no = outs // 128
    with nc.Block() as block:
        @block.tensor
        def _(pe):
            for o in range(no):
                for c in range(NCH):
                    n = o * NCH + c
                    if n >= 8:
                        pe.wait_ge(S["copied"], n - 7)
                    for t in range(kt):
                        mm = nc.tensor.matmul(ps[:, n % 8, 0:CH], bit.q[name][:, t, o * 128:(o + 1) * 128],
                                              q[t][:, c * CH:(c + 1) * CH], start=(t == 0), stop=(t == kt - 1))
                    mm.then_inc(S["made"], 1)

        @block.scalar
        def _(act):
            for o in range(no):
                bias = v(core, name if no == 1 else f"{name}_{o}")
                for c in range(NCH):
                    n = o * NCH + c
                    act.wait_ge(S["made"], n + 1)
                    nc.scalar.activation(dst[:, o, c * CH:(c + 1) * CH], ps[:, n % 8, 0:CH],
                                         ACT.Relu if relu else ACT.Identity, scale=bit.out[:, j:j + 1],
                                         bias=bias).then_inc(S["copied"], 1)


def bit_attention(core, amax):
    nc, ps = core.nc, core.ps
    with ExitStack() as ctx:
        bit = Bit(core, ctx)
        FU = core.sb("bit_fused", [D, 1, T], F32, ctx)
        isum = core.sb("bit_isum", [128, B], F32, ctx)
        avg = core.sb("bit_avg", [128, B], F32, ctx)
        vmax = core.sb("bit_vmax", [128, 3], F32, ctx)
        quantize_weights(core, bit)
        with ExitStack() as c1:
            V = core.sb("bit_V", [128, B * NK], I16, c1)
            input_scale(core, bit, amax[:, :], DC, 0, ["d2v"])
            image_pass(core, bit, V, DC, 0, None, "d2v", vmax[:, 0:1], None)
            input_scale(core, bit, vmax[:, 0:1], 128, 1, ["img"])
            image_pass(core, bit, V, 128, 1, "d2v", "img", vmax[:, 1:2], isum)
            input_scale(core, bit, vmax[:, 1:2], 128, 2, ["att0", "att1"])
            image_pass(core, bit, V, 128, 2, "img", None, None, None, last=True)

            def with_block(f):
                with nc.Block() as block:
                    @block.vector
                    def _(dve):
                        f(core.linker(dve, "dve"))

            with ExitStack() as c2:
                tmp = core.sb("bit_tmp", [D, T], F32, c2)
                q = core.sb("bit_qx", [D, T], BF16, c2)
                tm = core.sb("bit_tm", [128, 1], F32, c2)
                with_block(lambda link: link(nc.vector.tensor_reduce(
                    tm[:, :], core.xn[:, :], AX.X, ALU.max, apply_absolute_value=True)))
                input_scale(core, bit, tm[:, :], 128, 3, ["txt"])
                with_block(lambda link: quantized(core, bit, link, q[:, :], core.xn[:, :], 3, tmp[:, :]))
                bit_linear(core, bit, "txt", [q], FU, False, "btxt")
            Vb = V[:, :].bitcast(BF16)
            for which in ("att0", "att1"):
                bit_attend(core, bit, Vb, FU[:, 0, :], which)

        with ExitStack() as c2:
            tmp = core.sb("bit_tmp2", [D, 4, T], F32, c2)
            qf = core.sb("bit_qf", [D, 4, T], BF16, c2)
            hh = core.sb("bit_hh", [D, 4, T], F32, c2)
            tm = core.sb("bit_tm2", [128, 4], F32, c2)
            j = bit.weight("img")

            def inputs(link):
                link(nc.vector.tensor_scalar(avg[:, :], isum[:, :], bit.out[:, j:j + 1], None, ALU.mult))
                link(nc.vector.tensor_scalar(avg[:, :], avg[:, :], 1.0 / NK, v(core, "img"), ALU.mult, ALU.add))
                link(nc.vector.tensor_reduce(tm[:, 0:1], FU[:, 0, :], AX.X, ALU.max, apply_absolute_value=True))
                link(nc.vector.tensor_reduce(tm[:, 1:2], avg[:, :], AX.X, ALU.max, apply_absolute_value=True))
                link(nc.vector.tensor_tensor(tm[:, 2:3], tm[:, 0:1], tm[:, 1:2], ALU.max))

            def rounded(link):
                quantized(core, bit, link, qf[:, 0, :], FU[:, 0, :], 4, tmp[:, 0, :])
                quantized(core, bit, link, avg[:, :], avg[:, :], 4, tmp[:, 1, 0:B])
                link(nc.vector.tensor_copy(qf[:, 1, :].rearrange("p (b q) -> p b q", q=NQ),
                                           avg[:, :].unsqueeze(2).to_broadcast([128, B, NQ])))

            with_block(inputs)
            input_scale(core, bit, tm[:, 2:3], 128, 4, ["f1"])
            with_block(rounded)
            bit_linear(core, bit, "f1", [qf[:, 0, :], qf[:, 1, :]], hh, True, "bf1")
            with_block(lambda link: link(nc.vector.tensor_reduce(
                tm[:, 3:4], hh[:, :, :], AX.XY, ALU.max)))
            input_scale(core, bit, tm[:, 3:4], 128, 5, ["f2"])
            with_block(lambda link: quantized(core, bit, link, qf[:, :, :], hh[:, :, :], 5, tmp[:, :, :]))
            bit_linear(core, bit, "f2", [qf[:, t, :] for t in range(4)],
                       core.OT[:, :].rearrange("p (o t) -> p o t", o=1), False, "bf2")


def build(nc, d, out):
    with ExitStack() as ctx:
        core = Core(nc, ctx, d, out)
        rk = core.sb("rk", [KP, B * KT])
        amax = core.sb("amax", [DC, 1])
        csum = core.sb("csum", [KA, B])
        start_up(core)
        context_statistics(core, rk, amax, csum)
        layer_norm(core, core.xT, core.xn, "a0")
        with ExitStack() as c0:
            qp = core.sb("L0_Qp", [D, T], F32, c0)
            l2_norm_queries(core, qp, core.xn)
            attention_normed(core, "L0", core.xn, v(core, "L0_bo"), rk)
            with nc.Block() as block:
                @block.vector
                def _(dve):
                    link = core.linker(dve, "dve")
                    link(nc.vector.tensor_tensor(core.OT[:, :], core.OT[:, :], qp[:, :], ALU.add))

            def gamma_beta(link):
                link(nc.vector.tensor_scalar(core.xn[:, :], core.xn[:, :], v(core, "L0_g"), v(core, "L0_b"),
                                             ALU.mult, ALU.add))
            layer_norm(core, core.OT, core.xn, "o0", gamma_beta)
            add_gated(core, core.xn, 0)
        core.new_signals()
        layer_norm(core, core.xT, core.xn, "f0")
        experts0(core, 1)
        core.new_signals()
        layer_norm(core, core.xT, core.xn, "a1")
        attention(core, "L1", core.xn, v(core, "L1_bo"), scale=0.125, dh=64)
        add_gated(core, core.OT, 2)
        core.new_signals()
        layer_norm(core, core.xT, core.xn, "f1")
        gated_experts(core, "L1", 16, 5, 1e-9, 3)
        core.new_signals()
        layer_norm(core, core.xT, core.xn, "a2")
        bit_attention(core, amax)
        add_gated(core, core.OT, 4)
        core.new_signals()
        layer_norm(core, core.xT, core.xn, "f2")
        gated_experts(core, "L2", 8, 9, 1e-20, 5)
        core.new_signals()
        layer_norm(core, core.xT, core.xn, "a3")
        attention(core, "L3", core.xn, v(core, "L3_bo"), scale=float(8) ** -0.5, dh=8, clip=10000.0,
                  csum=csum)
        add_gated(core, core.OT, 6)
        core.new_signals()
        layer_norm(core, core.xT, core.xn, "f3")
        binarized_mlp(core, 7)
        store(core)


def store(core):
    nc = core.nc
    stored = core.sig("stored")
    with nc.Block() as block:
        @block.sync
        def _(sp):
            sp.dma_start(core.out, core.xT[:, :]).then_inc(stored.sem, 16)
            sp.wait_ge(stored.sem, 16)


def arrange(a):
    z = np.float32
    r = {}
    f = {k: np.asarray(w) for k, w in a.items()}
    r["xT"] = f["x"].reshape(T, D).T
    ctx = f["ctx_768"]
    keys = ctx.reshape(B, KP, KT, DC)
    r["ctxT"] = np.concatenate([keys.transpose(0, 3, 2, 1).reshape(B, DC, NK), np.ones((B, 2, NK), z)], 1)
    r["ctxN"] = np.concatenate([keys, np.ones((B, KP, KT, 1), z)], 3).reshape(B, KP, KT * KA)
    r["gates"] = np.broadcast_to(np.stack([f["g_xattn"], f["g_ffn"]], 1).reshape(1, 8), (128, 8))
    cols = {"L0_bq": f["L0_xattn_bq"], "L0_bo": f["L0_xattn_bo"], "L0_g": f["L0_xattn_ln_gamma"],
            "L0_b": f["L0_xattn_ln_beta"], "L1_bo": f["L1_xattn_bo"], "L3_bo": f["L3_xattn_bo"],
            "L3_b2": f["L3_ffn_b2"], "d2v": f["L2_xattn_b_d2v"], "img": f["L2_xattn_b_img"],
            "txt": f["L2_xattn_b_txt"], "f2": f["L2_xattn_b_f2"]}
    for n in ("att0", "att1"):
        cols[n] = np.concatenate([f[f"L2_xattn_b_{n}"]] * 2)
    for c in range(4):
        cols[f"f1_{c}"] = f["L2_xattn_b_f1"][c * 128:(c + 1) * 128]
        cols[f"ffb1_{c}"] = f["L3_ffn_b1"][c * 128:(c + 1) * 128]
    r["vec"] = np.stack([cols[n] for n in VECS], 1)

    def heads(w, dh):
        return w.reshape(w.shape[0], H, dh).transpose(2, 1, 0)

    for L, dh in (("L0", 8), ("L1", 64), ("L3", 8)):
        p = L + "_xattn_"
        zero = np.zeros(H * dh, z)
        bk, bv, bq = (f.get(p + n, zero) for n in ("bk", "bv", "bq"))
        wk = np.concatenate([f[p + "Wk"], bk[None]], 0)
        wv = np.concatenate([f[p + "Wv"], bv[None]], 0)
        r[f"{L}_WvA"] = heads(wv, dh)
        r[f"{L}_Wo"] = f[p + "Wo"].reshape(H, dh, D).transpose(1, 0, 2)
        if dh == DH:
            e = np.zeros((KA, H, DH + 1), z)
            e[:, :, 0:DH] = wv.reshape(KA, H, DH)
            e[DC, :, DH] = 1
            r[f"{L}_WvE"] = e.reshape(KA, H // 2 * VW)
            e = np.zeros((4, 32, 2, 2, D), z)
            for h in range(H):
                rr, g, j = h // 8, h // 2 % 4, h % 2
                e[g, (DH + 1) * j:(DH + 1) * j + DH, rr, j] = f[p + "Wo"][h * DH:(h + 1) * DH]
            r[f"{L}_WoE"] = e.reshape(128, 4, D)
        if L == "L0":
            r["L0_Wq"] = f[p + "Wq"]
            r["L0_WkA"] = wk
            r["L0_WkP"] = wk.reshape(KA, PAIRS, PF).transpose(0, 2, 1).reshape(KA, D)
            r["turn"] = np.eye(D, dtype=z).reshape(D, PAIRS, PF).transpose(0, 2, 1).reshape(D, D)
        else:
            r[f"{L}_WqT"] = heads(f[p + "Wq"], dh)
            r[f"{L}_WkAT"] = heads(wk, dh)
            r[f"{L}_bqh"] = bq.reshape(H, dh).T

    p = "L0_ffn_"
    r["L0_gw"] = f[p + "gate_w"]
    r["L0_gb"] = np.broadcast_to(f[p + "gate_b"], (TT, E0))
    r["L0_w1"] = f[p + "w1"].reshape(E0 // 2, 2, D, HID0).transpose(0, 2, 1, 3)
    r["L0_w2"] = f[p + "w2"].reshape(E0 // 2, 2, 128, HID0).transpose(0, 2, 1, 3)
    r["L0_b1"] = f[p + "b1"].reshape(E0, 128, HID0 // 128).transpose(1, 0, 2)
    r["L0_b2"] = f[p + "b2"].reshape(E0 // 2, 1, 2, D)

    def spread(n_exp, n_chunk, mid):
        ex = np.zeros((n_exp + 1, n_chunk * 128), z)
        for e in range(n_exp):
            ex[e, e * mid:(e + 1) * mid] = 1
        ex[n_exp, n_exp * mid:] = 1
        return ex.reshape(n_exp + 1, n_chunk, 128)

    def up(w):
        return w.transpose(1, 0, 2).reshape(D, -1)

    def rows(w):
        return w.reshape(-1, 128, D).transpose(1, 0, 2)

    p = "L1_ffn_"
    r["L1_wr"] = f[p + "router_w"]
    r["L1_ex"] = spread(16, 5, 32)
    r["L1_wg"] = np.concatenate([up(f[p + "wg_r"]), up(f[p + "wg_s"])], 1).reshape(D, 5, 128)
    r["L1_wu"] = np.concatenate([up(f[p + "wu_r"]), up(f[p + "wu_s"])], 1).reshape(D, 5, 128)
    r["L1_wd"] = rows(np.concatenate([f[p + "wd_r"].reshape(-1, D), f[p + "wd_s"].reshape(-1, D)], 0))
    p = "L2_ffn_"
    r["L2_wr"] = f[p + "gate_w"]
    r["L2_ex"] = spread(8, 9, 128)
    r["L2_wg"] = np.concatenate([up(f[p + "ew_gate"]), f[p + "sw_gate"]], 1).reshape(D, 9, 128)
    r["L2_wu"] = np.concatenate([up(f[p + "ew_up"]), f[p + "sw_up"]], 1).reshape(D, 9, 128)
    r["L2_wd"] = rows(np.concatenate([f[p + "ew_down"].reshape(-1, D), f[p + "sw_down"]], 0))
    p = "L2_xattn_"
    for n, (rows_, kt, o) in BITS.items():
        w = f[f"{p}W_{n}"].T
        if n.startswith("att"):
            w = np.concatenate([w, w], 1)
            r[f"bit_row_{n}"] = np.broadcast_to(cols[n], (KP, D))
        r[f"bit_{n}"] = w.reshape(kt, rows_, o).transpose(1, 0, 2)
    r["L3_w1"] = f["L3_ffn_w1"].reshape(4, 128, D).transpose(1, 0, 2)
    r["L3_w2"] = f["L3_ffn_w2"].reshape(D, 4, 128)
    return r


def kernel(**inputs):
    import concourse.bacc as _bacc
    from concourse.bass_utils import run_bass_kernel_spmd as _run

    nc = _bacc.Bacc("TRN2", target_bir_lowering=False, num_devices=1)
    arrays, d = {}, {}
    for name, a in arrange(inputs).items():
        a = np.ascontiguousarray(a)
        arrays[f"in_{name}"] = a
        d[name] = nc.dram_tensor(f"in_{name}", a.shape, mybir.dt.from_np(a.dtype), kind="ExternalInput").ap()
    out = nc.dram_tensor("out_x", (D, T), F32, kind="ExternalOutput").ap()
    build(nc, d, out)
    got = _run(nc, [arrays], core_ids=[0]).results[0]["out_x"]
    return np.ascontiguousarray(got.T).reshape(B, NQ, D)
```
